# Optimizing a Trainium2 kernel written in Bass

```python
import numpy as np
import jax
import jax.numpy as jnp

def _softmax(x, axis=-1):
    return jax.nn.softmax(x, axis=axis)

def _gelu(x):
    return jax.nn.gelu(x, approximate=True)

def _silu(x):
    return jax.nn.silu(x)

def _sigmoid(x):
    return jax.nn.sigmoid(x)

def _layernorm(x, axis=-1, eps=1e-05):
    m = jnp.mean(x, axis=axis, keepdims=True)
    v = jnp.var(x, axis=axis, keepdims=True)
    return (x - m) / jnp.sqrt(v + eps)

def _scatter_add(tgt, idx, src, axis=0):
    return tgt.at[idx].add(src)

def _segment_sum(src, seg, n):
    return jax.ops.segment_sum(src, seg, n)
kernel_name = 'mk_xattn_ffn_d2_seqx_r4_067863'

def setup_inputs(seed: int=0):
    np.random.seed(seed)
    _w = jnp.asarray

    def _rec_inputs():
        import jax
        import jax.numpy as jnp
        _rk = jax.random.key(seed)
        x = -0.0003929 + 0.9999 * jax.random.normal(jax.random.fold_in(_rk, 1), (8, 256, 256), jnp.float32)
        _lenS = 256 - jax.random.randint(jax.random.fold_in(_rk, 7), (8,), 0, max(1, 256 // 4) + 1, jnp.int32)
        _lenS2 = 120 - jax.random.randint(jax.random.fold_in(_rk, 8), (8,), 0, max(1, 120 // 4) + 1, jnp.int32)
        _ctx_512P = jax.random.normal(jax.random.fold_in(_rk, 11), (8, 16, 128), jnp.float32)
        _ctx_512c = jax.random.dirichlet(jax.random.fold_in(_rk, 511), 0.3 * jnp.ones((16,), jnp.float32), (8, 120))
        _ctx_512t = jnp.einsum('bsk,bkd->bsd', _ctx_512c, _ctx_512P)
        _ctx_512t = _ctx_512t * jax.lax.rsqrt(jnp.mean(jnp.square(_ctx_512t)) + 1e-12) * 0.953939
        ctx_512 = -1.39393e-06 + 0.999914 * (_ctx_512t + 0.3 * jax.random.normal(jax.random.fold_in(_rk, 611), (8, 120, 128), jnp.float32))
        return (x, ctx_512)
    x, ctx_512 = _rec_inputs()

    def _L0_xattn_setup():
        import jax, jax.numpy as jnp
        import numpy as np
        HEADS = 16
        D_MODEL = 256
        IMG_MODEL = 128
        D_K = D_MODEL // HEADS
        key = jax.random.key(seed)
        ks = jax.random.split(key, 12)
        B, LQ, LKV = (8, 512, 256)
        s_dm = 1.0 / np.sqrt(D_MODEL)
        s_im = 1.0 / np.sqrt(IMG_MODEL)
        return {'q': jax.random.normal(ks[0], (B, LQ, D_MODEL), jnp.float32), 'k': jax.random.normal(ks[1], (B, LKV, IMG_MODEL), jnp.float32), 'v': jax.random.normal(ks[2], (B, LKV, IMG_MODEL), jnp.float32), 'Wq': jax.random.normal(ks[3], (D_MODEL, D_MODEL), jnp.float32) * s_dm, 'bq': jnp.zeros((D_MODEL,), jnp.float32), 'Wk': jax.random.normal(ks[4], (IMG_MODEL, D_MODEL), jnp.float32) * s_im, 'bk': jnp.zeros((D_MODEL,), jnp.float32), 'Wv': jax.random.normal(ks[5], (IMG_MODEL, D_MODEL), jnp.float32) * s_im, 'bv': jnp.zeros((D_MODEL,), jnp.float32), 'Wo': jax.random.normal(ks[6], (D_MODEL, D_MODEL), jnp.float32) * s_dm, 'bo': jnp.zeros((D_MODEL,), jnp.float32)}
    _L0_xattn_all = _L0_xattn_setup()
    _L0_xattn_in = {k: v for k, v in _L0_xattn_all.items() if k in ('Wq', 'bq', 'Wk', 'bk', 'Wv', 'bv', 'Wo', 'bo')}
    del _L0_xattn_all

    def _L0_ffn_setup():
        import jax, jax.numpy as jnp
        import numpy as np
        HIDDEN = 256
        INNER = 1024

        def _weight_quant(w):
            scale = 1.0 / jnp.clip(jnp.mean(jnp.abs(w)), 1e-05)
            wq = jnp.clip(jnp.round(w * scale), -1.0, 1.0) / scale
            return w + jax.lax.stop_gradient(wq - w)

        def _act_quant(x):
            scale = 127.0 / jnp.clip(jnp.max(jnp.abs(x), axis=-1, keepdims=True), 1e-05)
            xq = jnp.clip(jnp.round(x * scale), -128.0, 127.0) / scale
            return x + jax.lax.stop_gradient(xq - x)

        def _bitlinear(x, w):
            return jnp.einsum('bsi,oi->bso', _act_quant(x), _weight_quant(w))
        key = jax.random.key(seed)
        k0, k1, k2, k3 = jax.random.split(key, 4)
        x = jax.random.normal(k0, (4, 512, HIDDEN), dtype=jnp.float32)
        w_gate = jax.random.normal(k1, (INNER, HIDDEN), dtype=jnp.float32) / np.sqrt(HIDDEN)
        w_up = jax.random.normal(k2, (INNER, HIDDEN), dtype=jnp.float32) / np.sqrt(HIDDEN)
        w_down = jax.random.normal(k3, (HIDDEN, INNER), dtype=jnp.float32) / np.sqrt(INNER)
        return {'x': x, 'w_gate': w_gate, 'w_up': w_up, 'w_down': w_down}
    _L0_ffn_all = _L0_ffn_setup()
    _L0_ffn_in = {k: v for k, v in _L0_ffn_all.items() if k in ('w_gate', 'w_up', 'w_down')}
    del _L0_ffn_all

    def _L1_xattn_setup():
        import jax, jax.numpy as jnp
        import numpy as np
        H, D, C1, C2, S, M, B, W = (16, 32, 256, 128, 512, 128, 2, 4)

        def _ln(x, g, b):
            m = jnp.mean(x, -1, keepdims=True)
            v = jnp.var(x, -1, keepdims=True)
            return (x - m) * jax.lax.rsqrt(v + 1e-05) * g + b

        def _mha(x, y, wq, wk, wv, li1_w, li1_b, lnx_g, lnx_b, lny_g, lny_b, ln3_g, ln3_b, li2_w, li2_b, li3_w, li3_b, causal):
            xn = _ln(x, lnx_g, lnx_b)
            yn = _ln(y, lny_g, lny_b)
            q = jnp.einsum('bsc,hcd->bhsd', xn, wq)
            k = jnp.einsum('btc,hcd->bhtd', yn, wk)
            v = jnp.einsum('btc,hcd->bhtd', yn, wv)
            a = jax.nn.softmax(jnp.einsum('bhsd,bhtd->bhst', q, k) * D ** (-0.5), axis=-1)
            if causal:
                s, t = (a.shape[-2], a.shape[-1])
                mask = (jnp.arange(t)[None, :] > jnp.arange(s)[:, None]).astype(a.dtype)
                a = a * mask
            o = jnp.einsum('bhst,bhtd->bhsd', a, v)
            o = o.transpose(0, 2, 1, 3).reshape(x.shape[0], x.shape[1], H * D)
            x_out = x + o @ li1_w + li1_b
            h = jax.nn.gelu(_ln(x_out, ln3_g, ln3_b) @ li2_w + li2_b, approximate=False)
            return x_out + h @ li3_w + li3_b
        key = jax.random.key(seed)
        ks = iter(jax.random.split(key, 64))

        def w(shape, scale=0.02):
            return jax.random.normal(next(ks), shape, jnp.float32) * scale
        inp = {'xx': jax.random.normal(next(ks), (B, S, C1), jnp.float32), 'ee': jax.random.normal(next(ks), (B, M, C2), jnp.float32), 'ln1_g': jnp.ones(C1, jnp.float32), 'ln1_b': jnp.zeros(C1, jnp.float32), 'ln2_g': jnp.ones(C1, jnp.float32), 'ln2_b': jnp.zeros(C1, jnp.float32)}
        for pfx, cy in (('a1', C1), ('a2', C2)):
            inp[pfx + '_wq'] = w((H, C1, D))
            inp[pfx + '_wk'] = w((H, cy, D))
            inp[pfx + '_wv'] = w((H, cy, D))
            inp[pfx + '_li1_w'] = w((H * D, C1))
            inp[pfx + '_li1_b'] = jnp.zeros(C1, jnp.float32)
            inp[pfx + '_lnx_g'] = jnp.ones(C1, jnp.float32)
            inp[pfx + '_lnx_b'] = jnp.zeros(C1, jnp.float32)
            inp[pfx + '_lny_g'] = jnp.ones(cy, jnp.float32)
            inp[pfx + '_lny_b'] = jnp.zeros(cy, jnp.float32)
            inp[pfx + '_ln3_g'] = jnp.ones(C1, jnp.float32)
            inp[pfx + '_ln3_b'] = jnp.zeros(C1, jnp.float32)
            inp[pfx + '_li2_w'] = w((C1, C1 * W))
            inp[pfx + '_li2_b'] = jnp.zeros(C1 * W, jnp.float32)
            inp[pfx + '_li3_w'] = w((C1 * W, C1))
            inp[pfx + '_li3_b'] = jnp.zeros(C1, jnp.float32)
        inp['training'] = 0
        return inp
    _L1_xattn_all = _L1_xattn_setup()
    _L1_xattn_in = {k: v for k, v in _L1_xattn_all.items() if k in ('ln1_g', 'ln1_b', 'ln2_g', 'ln2_b', 'a1_wq', 'a1_wk', 'a1_wv', 'a1_li1_w', 'a1_li1_b', 'a1_lnx_g', 'a1_lnx_b', 'a1_lny_g', 'a1_lny_b', 'a1_ln3_g', 'a1_ln3_b', 'a1_li2_w', 'a1_li2_b', 'a1_li3_w', 'a1_li3_b', 'a2_wq', 'a2_wk', 'a2_wv', 'a2_li1_w', 'a2_li1_b', 'a2_lnx_g', 'a2_lnx_b', 'a2_lny_g', 'a2_lny_b', 'a2_ln3_g', 'a2_ln3_b', 'a2_li2_w', 'a2_li2_b', 'a2_li3_w', 'a2_li3_b')}
    del _L1_xattn_all

    def _L1_ffn_setup():
        import jax, jax.numpy as jnp
        import numpy as np
        D = 256
        H = 1024
        E = 8
        B, N = (2, 512)
        key = jax.random.key(seed)
        ks = jax.random.split(key, 5)
        x = jax.random.normal(ks[0], (B, N, D), dtype=jnp.float32)
        W1 = jax.random.normal(ks[1], (E, D, H), dtype=jnp.float32) / np.sqrt(D)
        W2 = jax.random.normal(ks[2], (E, H, D), dtype=jnp.float32) / np.sqrt(H)
        Wg = jax.random.normal(ks[3], (D, E), dtype=jnp.float32) / np.sqrt(D)
        bg = jax.random.normal(ks[4], (E,), dtype=jnp.float32) * 0.01
        return {'x': x, 'W1': W1, 'W2': W2, 'Wg': Wg, 'bg': bg}
    _L1_ffn_all = _L1_ffn_setup()
    _L1_ffn_in = {k: v for k, v in _L1_ffn_all.items() if k in ('W1', 'W2', 'Wg', 'bg')}
    del _L1_ffn_all
    return {'x': x, 'ctx_512': ctx_512, 'L0_xattn_Wq': _L0_xattn_in['Wq'], 'L0_xattn_bq': _L0_xattn_in['bq'], 'L0_xattn_Wk': _L0_xattn_in['Wk'], 'L0_xattn_bk': _L0_xattn_in['bk'], 'L0_xattn_Wv': _L0_xattn_in['Wv'], 'L0_xattn_bv': _L0_xattn_in['bv'], 'L0_xattn_Wo': _L0_xattn_in['Wo'], 'L0_xattn_bo': _L0_xattn_in['bo'], 'L0_ffn_w_gate': _L0_ffn_in['w_gate'], 'L0_ffn_w_up': _L0_ffn_in['w_up'], 'L0_ffn_w_down': _L0_ffn_in['w_down'], 'L1_xattn_ln1_g': _L1_xattn_in['ln1_g'], 'L1_xattn_ln1_b': _L1_xattn_in['ln1_b'], 'L1_xattn_ln2_g': _L1_xattn_in['ln2_g'], 'L1_xattn_ln2_b': _L1_xattn_in['ln2_b'], 'L1_xattn_a1_wq': _L1_xattn_in['a1_wq'], 'L1_xattn_a1_wk': _L1_xattn_in['a1_wk'], 'L1_xattn_a1_wv': _L1_xattn_in['a1_wv'], 'L1_xattn_a1_li1_w': _L1_xattn_in['a1_li1_w'], 'L1_xattn_a1_li1_b': _L1_xattn_in['a1_li1_b'], 'L1_xattn_a1_lnx_g': _L1_xattn_in['a1_lnx_g'], 'L1_xattn_a1_lnx_b': _L1_xattn_in['a1_lnx_b'], 'L1_xattn_a1_lny_g': _L1_xattn_in['a1_lny_g'], 'L1_xattn_a1_lny_b': _L1_xattn_in['a1_lny_b'], 'L1_xattn_a1_ln3_g': _L1_xattn_in['a1_ln3_g'], 'L1_xattn_a1_ln3_b': _L1_xattn_in['a1_ln3_b'], 'L1_xattn_a1_li2_w': _L1_xattn_in['a1_li2_w'], 'L1_xattn_a1_li2_b': _L1_xattn_in['a1_li2_b'], 'L1_xattn_a1_li3_w': _L1_xattn_in['a1_li3_w'], 'L1_xattn_a1_li3_b': _L1_xattn_in['a1_li3_b'], 'L1_xattn_a2_wq': _L1_xattn_in['a2_wq'], 'L1_xattn_a2_wk': _L1_xattn_in['a2_wk'], 'L1_xattn_a2_wv': _L1_xattn_in['a2_wv'], 'L1_xattn_a2_li1_w': _L1_xattn_in['a2_li1_w'], 'L1_xattn_a2_li1_b': _L1_xattn_in['a2_li1_b'], 'L1_xattn_a2_lnx_g': _L1_xattn_in['a2_lnx_g'], 'L1_xattn_a2_lnx_b': _L1_xattn_in['a2_lnx_b'], 'L1_xattn_a2_lny_g': _L1_xattn_in['a2_lny_g'], 'L1_xattn_a2_lny_b': _L1_xattn_in['a2_lny_b'], 'L1_xattn_a2_ln3_g': _L1_xattn_in['a2_ln3_g'], 'L1_xattn_a2_ln3_b': _L1_xattn_in['a2_ln3_b'], 'L1_xattn_a2_li2_w': _L1_xattn_in['a2_li2_w'], 'L1_xattn_a2_li2_b': _L1_xattn_in['a2_li2_b'], 'L1_xattn_a2_li3_w': _L1_xattn_in['a2_li3_w'], 'L1_xattn_a2_li3_b': _L1_xattn_in['a2_li3_b'], 'L1_ffn_W1': _L1_ffn_in['W1'], 'L1_ffn_W2': _L1_ffn_in['W2'], 'L1_ffn_Wg': _L1_ffn_in['Wg'], 'L1_ffn_bg': _L1_ffn_in['bg']}

def reference(x, ctx_512, L0_xattn_Wq, L0_xattn_bq, L0_xattn_Wk, L0_xattn_bk, L0_xattn_Wv, L0_xattn_bv, L0_xattn_Wo, L0_xattn_bo, L0_ffn_w_gate, L0_ffn_w_up, L0_ffn_w_down, L1_xattn_ln1_g, L1_xattn_ln1_b, L1_xattn_ln2_g, L1_xattn_ln2_b, L1_xattn_a1_wq, L1_xattn_a1_wk, L1_xattn_a1_wv, L1_xattn_a1_li1_w, L1_xattn_a1_li1_b, L1_xattn_a1_lnx_g, L1_xattn_a1_lnx_b, L1_xattn_a1_lny_g, L1_xattn_a1_lny_b, L1_xattn_a1_ln3_g, L1_xattn_a1_ln3_b, L1_xattn_a1_li2_w, L1_xattn_a1_li2_b, L1_xattn_a1_li3_w, L1_xattn_a1_li3_b, L1_xattn_a2_wq, L1_xattn_a2_wk, L1_xattn_a2_wv, L1_xattn_a2_li1_w, L1_xattn_a2_li1_b, L1_xattn_a2_lnx_g, L1_xattn_a2_lnx_b, L1_xattn_a2_lny_g, L1_xattn_a2_lny_b, L1_xattn_a2_ln3_g, L1_xattn_a2_ln3_b, L1_xattn_a2_li2_w, L1_xattn_a2_li2_b, L1_xattn_a2_li3_w, L1_xattn_a2_li3_b, L1_ffn_W1, L1_ffn_W2, L1_ffn_Wg, L1_ffn_bg):
    import jax
    import jax.numpy as jnp

    def _L0_xattn_ref(q, k, v, Wq, bq, Wk, bk, Wv, bv, Wo, bo):
        import jax, jax.numpy as jnp
        import numpy as np
        HEADS = 16
        D_MODEL = 256
        IMG_MODEL = 128
        D_K = D_MODEL // HEADS
        B, LQ, _ = q.shape
        LKV = k.shape[1]
        qh = (q @ Wq + bq).reshape(B, LQ, HEADS, D_K).transpose(0, 2, 1, 3)
        kh = (k @ Wk + bk).reshape(B, LKV, HEADS, D_K).transpose(0, 2, 1, 3)
        vh = (v @ Wv + bv).reshape(B, LKV, HEADS, D_K).transpose(0, 2, 1, 3)
        scale = 1.0 / np.sqrt(D_K)
        scores = jnp.einsum('bhqd,bhkd->bhqk', qh, kh) * scale
        attn = jax.nn.softmax(scores, axis=-1)
        out = jnp.einsum('bhqk,bhkd->bhqd', attn, vh)
        concat = out.transpose(0, 2, 1, 3).reshape(B, LQ, D_MODEL)
        return concat @ Wo + bo

    def _L0_ffn_ref(x, w_gate, w_up, w_down):
        import jax, jax.numpy as jnp
        import numpy as np
        HIDDEN = 256
        INNER = 1024

        def _weight_quant(w):
            scale = 1.0 / jnp.clip(jnp.mean(jnp.abs(w)), 1e-05)
            wq = jnp.clip(jnp.round(w * scale), -1.0, 1.0) / scale
            return w + jax.lax.stop_gradient(wq - w)

        def _act_quant(x):
            scale = 127.0 / jnp.clip(jnp.max(jnp.abs(x), axis=-1, keepdims=True), 1e-05)
            xq = jnp.clip(jnp.round(x * scale), -128.0, 127.0) / scale
            return x + jax.lax.stop_gradient(xq - x)

        def _bitlinear(x, w):
            return jnp.einsum('bsi,oi->bso', _act_quant(x), _weight_quant(w))
        gate = jax.nn.silu(_bitlinear(x, w_gate))
        up = _bitlinear(x, w_up)
        return _bitlinear(gate * up, w_down)

    def _L1_xattn_ref(xx, ee, ln1_g, ln1_b, ln2_g, ln2_b, a1_wq, a1_wk, a1_wv, a1_li1_w, a1_li1_b, a1_lnx_g, a1_lnx_b, a1_lny_g, a1_lny_b, a1_ln3_g, a1_ln3_b, a1_li2_w, a1_li2_b, a1_li3_w, a1_li3_b, a2_wq, a2_wk, a2_wv, a2_li1_w, a2_li1_b, a2_lnx_g, a2_lnx_b, a2_lny_g, a2_lny_b, a2_ln3_g, a2_ln3_b, a2_li2_w, a2_li2_b, a2_li3_w, a2_li3_b, training):
        import jax, jax.numpy as jnp
        import numpy as np
        H, D, C1, C2, S, M, B, W = (16, 32, 256, 128, 512, 128, 2, 4)

        def _ln(x, g, b):
            m = jnp.mean(x, -1, keepdims=True)
            v = jnp.var(x, -1, keepdims=True)
            return (x - m) * jax.lax.rsqrt(v + 1e-05) * g + b

        def _mha(x, y, wq, wk, wv, li1_w, li1_b, lnx_g, lnx_b, lny_g, lny_b, ln3_g, ln3_b, li2_w, li2_b, li3_w, li3_b, causal):
            xn = _ln(x, lnx_g, lnx_b)
            yn = _ln(y, lny_g, lny_b)
            q = jnp.einsum('bsc,hcd->bhsd', xn, wq)
            k = jnp.einsum('btc,hcd->bhtd', yn, wk)
            v = jnp.einsum('btc,hcd->bhtd', yn, wv)
            a = jax.nn.softmax(jnp.einsum('bhsd,bhtd->bhst', q, k) * D ** (-0.5), axis=-1)
            if causal:
                s, t = (a.shape[-2], a.shape[-1])
                mask = (jnp.arange(t)[None, :] > jnp.arange(s)[:, None]).astype(a.dtype)
                a = a * mask
            o = jnp.einsum('bhst,bhtd->bhsd', a, v)
            o = o.transpose(0, 2, 1, 3).reshape(x.shape[0], x.shape[1], H * D)
            x_out = x + o @ li1_w + li1_b
            h = jax.nn.gelu(_ln(x_out, ln3_g, ln3_b) @ li2_w + li2_b, approximate=False)
            return x_out + h @ li3_w + li3_b
        x = _ln(xx, ln1_g, ln1_b)
        x = x + _mha(x, x, a1_wq, a1_wk, a1_wv, a1_li1_w, a1_li1_b, a1_lnx_g, a1_lnx_b, a1_lny_g, a1_lny_b, a1_ln3_g, a1_ln3_b, a1_li2_w, a1_li2_b, a1_li3_w, a1_li3_b, causal=True)
        x = _ln(x, ln2_g, ln2_b)
        return x + _mha(x, ee, a2_wq, a2_wk, a2_wv, a2_li1_w, a2_li1_b, a2_lnx_g, a2_lnx_b, a2_lny_g, a2_lny_b, a2_ln3_g, a2_ln3_b, a2_li2_w, a2_li2_b, a2_li3_w, a2_li3_b, causal=False)

    def _L1_ffn_ref(x, W1, W2, Wg, bg):
        import jax, jax.numpy as jnp
        import numpy as np
        D = 256
        H = 1024
        E = 8
        B, N = (2, 512)
        b, n, d = x.shape
        e = Wg.shape[1]
        xf = x.reshape(b * n, d)
        logits = xf @ Wg + bg
        one_hot = jax.nn.one_hot(jnp.argmax(logits, axis=-1), e, dtype=x.dtype)
        h = jax.nn.gelu(jnp.einsum('td,edh->eth', xf, W1), approximate=True)
        y = jnp.einsum('eth,ehd->etd', h, W2)
        out = jnp.einsum('etd,te->td', y, one_hot)
        return out.reshape(b, n, d)
    x = x + _L0_xattn_ref(_layernorm(x, axis=-1), ctx_512, ctx_512, L0_xattn_Wq, L0_xattn_bq, L0_xattn_Wk, L0_xattn_bk, L0_xattn_Wv, L0_xattn_bv, L0_xattn_Wo, L0_xattn_bo)
    x = x + _L0_ffn_ref(_layernorm(x, axis=-1), L0_ffn_w_gate, L0_ffn_w_up, L0_ffn_w_down)
    x = x + _L1_xattn_ref(_layernorm(x, axis=-1), ctx_512, L1_xattn_ln1_g, L1_xattn_ln1_b, L1_xattn_ln2_g, L1_xattn_ln2_b, L1_xattn_a1_wq, L1_xattn_a1_wk, L1_xattn_a1_wv, L1_xattn_a1_li1_w, L1_xattn_a1_li1_b, L1_xattn_a1_lnx_g, L1_xattn_a1_lnx_b, L1_xattn_a1_lny_g, L1_xattn_a1_lny_b, L1_xattn_a1_ln3_g, L1_xattn_a1_ln3_b, L1_xattn_a1_li2_w, L1_xattn_a1_li2_b, L1_xattn_a1_li3_w, L1_xattn_a1_li3_b, L1_xattn_a2_wq, L1_xattn_a2_wk, L1_xattn_a2_wv, L1_xattn_a2_li1_w, L1_xattn_a2_li1_b, L1_xattn_a2_lnx_g, L1_xattn_a2_lnx_b, L1_xattn_a2_lny_g, L1_xattn_a2_lny_b, L1_xattn_a2_ln3_g, L1_xattn_a2_ln3_b, L1_xattn_a2_li2_w, L1_xattn_a2_li2_b, L1_xattn_a2_li3_w, L1_xattn_a2_li3_b, 0)
    x = x + _L1_ffn_ref(_layernorm(x, axis=-1), L1_ffn_W1, L1_ffn_W2, L1_ffn_Wg, L1_ffn_bg)
    return x

_drawn_inputs = setup_inputs


def setup_inputs(seed=0):
    import zlib

    import numpy as np

    out = dict(_drawn_inputs(seed))
    spreads = {'L0_xattn_bq': (0.0, 0.1),
     'L0_xattn_bk': (0.0, 0.8),
     'L0_xattn_bv': (0.0, 0.1),
     'L0_xattn_bo': (0.0, 0.1),
     'L1_xattn_ln1_g': (1.0, 0.2),
     'L1_xattn_ln1_b': (0.0, 0.1),
     'L1_xattn_ln2_g': (1.0, 0.2),
     'L1_xattn_ln2_b': (0.0, 0.1),
     'L1_xattn_a1_li1_b': (0.0, 0.1),
     'L1_xattn_a1_lnx_g': (1.0, 0.6),
     'L1_xattn_a1_lnx_b': (0.0, 0.8),
     'L1_xattn_a1_lny_g': (1.0, 0.6),
     'L1_xattn_a1_lny_b': (0.0, 0.48),
     'L1_xattn_a1_ln3_g': (1.0, 0.6),
     'L1_xattn_a1_ln3_b': (0.0, 0.481),
     'L1_xattn_a1_li2_b': (0.0, 0.319),
     'L1_xattn_a1_li3_b': (0.0, 0.1),
     'L1_xattn_a2_li1_b': (0.0, 0.1),
     'L1_xattn_a2_lnx_g': (1.0, 0.6),
     'L1_xattn_a2_lnx_b': (0.0, 0.8),
     'L1_xattn_a2_lny_g': (1.0, 0.6),
     'L1_xattn_a2_lny_b': (0.0, 0.472),
     'L1_xattn_a2_ln3_g': (1.0, 0.6),
     'L1_xattn_a2_ln3_b': (0.0, 0.8),
     'L1_xattn_a2_li2_b': (0.0, 0.1),
     'L1_xattn_a2_li3_b': (0.0, 0.1)}
    factors = {'L1_xattn_a1_wq': 8.0, 'L1_xattn_a1_wk': 8.0, 'L1_xattn_a2_wq': 8.0, 'L1_xattn_a2_wk': 8.0}
    for name, (base, spread) in spreads.items():
        noise = np.random.default_rng([zlib.crc32(name.encode()), seed]).standard_normal(out[name].shape)
        drawn = base * np.exp(spread * noise) if base else spread * noise
        out[name] = jnp.asarray(drawn.astype(out[name].dtype))
    for name, factor in factors.items():
        out[name] = (out[name] * factor).astype(out[name].dtype)
    return out
```

```python
from collections import Counter
from contextlib import ExitStack

import concourse.bass as bass
from concourse import mybir

F32 = mybir.dt.float32
BF16 = mybir.dt.bfloat16
I32 = mybir.dt.int32
ALU = mybir.AluOpType
ACT = mybir.ActivationFunctionType
AX = mybir.AxisListType

P = 128
B, S, D = 8, 256, 256
C2, KV = 128, 120
HEADS = 16
D0, D1 = D // HEADS, 32
HD = HEADS * D1
INNER = 1024
E = 8
T = S // P
KC = D // P
HC = INNER // P
TILES = B * T
TOKENS = B * S
EPS = 1e-5
UNIT = 2 * P
UNITS = TOKENS // UNIT + E - 1
ROW = D + 1
MAGIC = 1.5 * 2.0 ** 23
PAD_ID = 1 << 20


class Tally:

    def __init__(self, sems):
        self.sems, self.n = sems, Counter()

    def wait(self, eng, name, h=0, more=1):
        self.n[name, h] += more
        eng.wait_ge(self.sems[name, h], self.n[name, h])


def build(nc, ins, out):
    ctx = ExitStack()
    with ctx:
        def sb(name, shape, dt=F32):
            return ctx.enter_context(nc.sbuf_tensor(name, shape, dt))

        x5_dram = nc.dram_tensor("x5_rows", [TOKENS, D], F32).ap()
        slots_dram = nc.dram_tensor("slot_rows", [UNITS * UNIT, ROW], F32).ap()

        wq0 = sb("wq0", [P, KC, D]); wk0 = sb("wk0", [P, D]); wv0 = sb("wv0", [P, D]); wo0 = sb("wo0", [P, KC, D])
        wgT = sb("wgT", [P, KC, INNER], BF16); wuT = sb("wuT", [P, KC, INNER], BF16)
        wdT = sb("wdT", [P, HC, D], BF16)
        w1 = {}
        for a, kc in (("a1", KC), ("a2", 1)):
            w1[a] = dict(wq=sb(a + "_wq", [P, KC, HD]), wk=sb(a + "_wk", [P, kc, HD]), wv=sb(a + "_wv", [P, kc, HD]),
                         li1=sb(a + "_li1", [P, HD // P, D]), li2=sb(a + "_li2", [P, KC, INNER]),
                         li3=sb(a + "_li3", [P, HC, D]))
        wg_moe = sb("wg_moe", [P, KC, E])
        PP = ["L0_xattn_bq", "L0_xattn_bk"]
        for a in ("a1", "a2"):
            PP += [f"L1_xattn_{a}_{n}" for n in ("lnx_g", "lnx_b", "lny_g", "lny_b", "ln3_g", "ln3_b", "li2_b")]
        col, ncol = {}, 0
        for n in PP:
            col[n] = (ncol, ins[n].shape[0] // P)
            ncol += ins[n].shape[0] // P
        pvec = sb("pvec", [P, ncol])
        BC = ["L0_xattn_bv", "L0_xattn_bo", "L1_xattn_ln1_g", "L1_xattn_ln1_b", "L1_xattn_ln2_g", "L1_xattn_ln2_b",
              "L1_xattn_a1_li1_b", "L1_xattn_a1_li3_b", "L1_xattn_a2_li1_b", "L1_xattn_a2_li3_b"]
        bvec = sb("bvec", [P, len(BC), D])
        bgt = sb("bgt", [P, E])

        def pv(n, m):
            return pvec[:, col[n][0] + m:col[n][0] + m + 1]

        def bv(n, tiles=T):
            return bvec[:, BC.index(n):BC.index(n) + 1, :].to_broadcast([P, tiles, D])

        ident = sb("ident", [P, P]); identb = sb("identb", [P, P], BF16)
        later = sb("later", [P, P])
        strict = sb("strict", [P, P], BF16)
        onesb = sb("onesb", [P, P], BF16)
        onesf = sb("onesf", [P, P])
        own16 = sb("own16", [P, 8]); own32 = sb("own32", [P, 4])
        epst = sb("epst", [P, 2]); neghalf = sb("neghalf", [P, 2])
        eidx = sb("eidx", [P, E])
        mean_w = sb("mean_w", [P, 3]); scale_w = sb("scale_w", [P, 3]); asum = sb("asum", [P, 3]); wtot = sb("wtot", [P, 3])

        ARENA = 13400
        arena = [sb(f"arena{h}", [P, ARENA]) for h in range(2)]
        small = [sb(f"small{h}", [P, 256]) for h in range(2)]
        onehot = sb("onehot", [P, TILES, E], BF16)

        def view(h, at, shape, dt=F32):
            n = 1
            for s in shape:
                n *= s
            words = n if dt != BF16 else n // 2
            v = arena[h][:, at:at + words]
            if dt != F32:
                v = v.bitcast(dt)
            if len(shape) == 2:
                v = v.rearrange("p (a b) -> p a b", a=shape[0])
            elif len(shape) == 3:
                v = v.rearrange("p (a b c) -> p a b c", a=shape[0], b=shape[1])
            return v

        X = [view(h, 0, [T, D]) for h in range(2)]
        XH = [view(h, 512, [T, D]) for h in range(2)]
        Y = [view(h, 1024, [T, D]) for h in range(2)]
        XB = [view(h, 1536, [T, D]) for h in range(2)]
        FT = [view(h, 2048, [KC, S]) for h in range(2)]
        QT = [view(h, 2560, [4, S]) for h in range(2)]
        KT = [view(h, 3584, [4, S]) for h in range(2)]
        V1 = [view(h, 4608, [T, HD]) for h in range(2)]
        OT = [view(h, 5632, [4, S]) for h in range(2)]
        PR = [view(h, 6656, [2, 512]) for h in range(2)]
        PT = [view(h, 7680, [2, 1024]) for h in range(2)]
        KM = [view(h, 9728, [2, 512]) for h in range(2)]
        RTS = [view(h, 10752, [S]) for h in range(2)]
        RBC = [view(h, 11008, [T, P]) for h in range(2)]
        KT0 = [view(h, 11264, [2, KV]) for h in range(2)]
        KT2 = [view(h, 11520, [4, KV]) for h in range(2)]
        VM = [view(h, 12032, [8, 2, 32]) for h in range(2)]
        V2 = [view(h, 12544, [HD]) for h in range(2)]
        FT2 = [view(h, 6656, [KC, S]) for h in range(2)]
        CT = [view(h, 2560, [P]) for h in range(2)]
        CH = [view(h, 2688, [P]) for h in range(2)]
        CTT = [view(h, 2816, [KV]) for h in range(2)]
        CYT = [view(h, 2944, [KV]) for h in range(2)]
        HH = [view(h, 7680, [T, INNER]) for h in range(2)]
        HT = [view(h, 7680, [HC, S]) for h in range(2)]
        N2 = [view(h, 2560, [T, INNER], BF16) for h in range(2)]
        N2T = [view(h, 3584, [HC, S], BF16) for h in range(2)]
        N1 = [view(h, 1024, [T, D], BF16) for h in range(2)]
        N1T = [view(h, 2048, [KC, S], BF16) for h in range(2)]
        SG = [view(h, 4608, [2, 512]) for h in range(2)]

        def sm(h, at, n):
            return small[h][:, at:at + n]

        ps = ctx.enter_context(nc.psum_tensor("ps", [P, 8, 512], F32))

        def bank(h, b, n=1):
            return ps[:, 4 * h + b, :] if n == 1 else ps[:, 4 * h + b:4 * h + b + n, :]

        NAMES = ["x_loaded", "ctx_loaded", "x5_stored", "var_ready", "rstd_ready", "xhat_ready", "xhatT_done",
                 "featT_ready", "ctx_proj_done", "kT_ready", "v_ready", "q_done", "qT_ready", "kv_done",
                 "res_ready", "km_ready", "s_done", "max_done", "exp_done", "t_done", "pt_ready", "pv_done",
                 "rec_ready", "rbc_ready", "rt_done", "rts_ready", "oT_ready", "out_done", "gu_done",
                 "silu_done", "hh_done", "n2_ready", "n2T_done", "n2T_ready", "h_done", "gelu_done",
                 "x5_ready", "logits_done", "dve_chain", "pool_chain"]
        sems = {}
        for n in NAMES:
            for h in range(2):
                sems[n, h] = ctx.enter_context(nc.semaphore(f"{n}{h}"))
        numbers = [s.num for s in sems.values()]
        sem_range = range(min(numbers), max(numbers) + 1)
        assert len(sem_range) == len(numbers)

        def sem(name, h=0):
            return sems[name, h]

        raw = [arena[0][:, 0:2048], arena[0][:, 2048:4096], arena[0][:, 4096:6144]]
        tern = [arena[1][:, 1024 * k:1024 * (k + 1)].bitcast(BF16) for k in range(3)]
        w_load = ctx.enter_context(nc.semaphore("w_load"))
        q_load = ctx.enter_context(nc.semaphore("q_load"))
        const_ready = ctx.enter_context(nc.semaphore("const_ready"))
        wsum_ready = ctx.enter_context(nc.semaphore("wsum_ready"))
        wtot_done = ctx.enter_context(nc.semaphore("wtot_done"))
        tern_ready = ctx.enter_context(nc.semaphore("tern_ready"))
        ternT_done = ctx.enter_context(nc.semaphore("ternT_done"))
        pro_chain = ctx.enter_context(nc.semaphore("pro_chain"))
        pads_written = ctx.enter_context(nc.semaphore("pads_written"))

        with nc.Block() as block:
            @block.sync
            def _(sp):
                for k, n in enumerate(("L0_ffn_w_gate", "L0_ffn_w_up")):
                    sp.dma_start(raw[k].rearrange("p (c i) -> p c i", i=D),
                                 ins[n].rearrange("(c p) i -> p c i", p=P)).then_inc(q_load, 16)
                sp.dma_start(raw[2].rearrange("p (c i) -> p c i", i=INNER),
                             ins["L0_ffn_w_down"].rearrange("(c p) i -> p c i", p=P)).then_inc(q_load, 16)
                n_w = 0

                def load(dst, src):
                    sp.dma_start(dst, src).then_inc(w_load, 16)
                    return 16
                n_w += load(wq0[:], ins["L0_xattn_Wq"].rearrange("(c p) n -> p c n", p=P))
                n_w += load(wk0[:], ins["L0_xattn_Wk"])
                n_w += load(wv0[:], ins["L0_xattn_Wv"])
                n_w += load(wo0[:], ins["L0_xattn_Wo"].rearrange("(c p) n -> p c n", p=P))
                n_w += load(wg_moe[:], ins["L1_ffn_Wg"].rearrange("(c p) n -> p c n", p=P))
                n_w += load(bgt[:], ins["L1_ffn_bg"].rearrange("(a n) -> a n", a=1).to_broadcast([P, E]))
                for k, n in enumerate(BC):
                    n_w += load(bvec[:, k, :], ins[n].rearrange("(a n) -> a n", a=1).to_broadcast([P, D]))
                with nc.allow_non_contiguous_dma(reason="per-feature vectors onto partitions, small"):
                    for n in PP:
                        c0, m = col[n]
                        n_w += load(pvec[:, c0:c0 + m], ins[n].rearrange("(c p) -> p c", p=P))
                for a in ("a1", "a2"):
                    w = w1[a]
                    for n in ("wq", "wk", "wv"):
                        src = ins[f"L1_xattn_{a}_{n}"]
                        for c in range(src.shape[1] // P):
                            n_w += load(w[n][:, c, :].rearrange("p (h d) -> p h d", h=HEADS),
                                        src[:, c * P:(c + 1) * P, :].rearrange("h p d -> p h d"))
                    for n in ("li1", "li2", "li3"):
                        n_w += load(w[n][:], ins[f"L1_xattn_{a}_{n}_w"].rearrange("(c p) n -> p c n", p=P))
                sp.wait_ge(w_load, n_w)

            @block.gpsimd
            def _(pool):
                pool.memset(ident[:], 0.0)
                pool.memset(identb[:], 0.0)
                pool.memset(later[:], 1.0)
                pool.memset(strict[:], 1.0)
                pool.memset(onesb[:], 1.0)
                pool.memset(onesf[:], 1.0)
                pool.memset(own16[:], 1.0)
                pool.memset(own32[:], 1.0)
                pool.memset(epst[:], EPS)
                pool.memset(neghalf[:], -0.5)
                pool.iota(eidx[:], pattern=[[1, E]], base=0, channel_multiplier=0,
                          allow_small_or_imprecise_dtypes=True).then_inc(const_ready, 1)
                pool.wait_ge(const_ready, 1)
                for m in (ident, identb):
                    pool.affine_select(out=m[:], in_=m[:], compare_op=ALU.not_equal, fill=1.0, base=0,
                                       pattern=[[-1, P]], channel_multiplier=1)
                pool.affine_select(out=later[:], in_=later[:], compare_op=ALU.is_gt, fill=0.0, base=0,
                                   pattern=[[-1, P]], channel_multiplier=1)
                pool.affine_select(out=strict[:], in_=strict[:], compare_op=ALU.is_gt, fill=0.0, base=0,
                                   pattern=[[1, P]], channel_multiplier=-1).then_inc(const_ready, 1)
                for m, width, n in ((own16, 16, 8), (own32, 32, 4)):
                    pool.affine_select(out=m[:], in_=m[:], compare_op=ALU.is_ge, fill=0.0, base=0,
                                       pattern=[[-width, n]], channel_multiplier=1).then_inc(const_ready, 1)
                pool.wait_ge(const_ready, 4)
                for m, width, n in ((own16, 16, 8), (own32, 32, 4)):
                    pool.affine_select(out=m[:], in_=m[:], compare_op=ALU.is_gt, fill=0.0, base=width,
                                       pattern=[[width, n]], channel_multiplier=-1).then_inc(const_ready, 1)
                for h in range(2):
                    pool.memset(VM[h], 0.0).then_inc(const_ready, 1)
                    pool.memset(small[h][:], 0.0)
                pad = arena[0][:, 6144:6144 + ROW]
                pool.memset(pad, float(PAD_ID)).then_inc(const_ready, 1)
                pool.wait_ge(const_ready, 9)
                n_rows = UNITS * UNIT // P
                pool.dma_start(slots_dram.rearrange("(p c) n -> p c n", c=n_rows),
                               pad.rearrange("p (a n) -> p a n", a=1).to_broadcast([P, n_rows, ROW])
                               ).then_inc(pads_written, 16)
                pool.wait_ge(pads_written, 16)

            @block.vector
            def _(dve):
                for k in range(3):
                    dve.wait_ge(q_load, 16 * 3)
                    dve.tensor_reduce(asum[:, k:k + 1], raw[k], AX.X, ALU.add,
                                      apply_absolute_value=True).then_inc(wsum_ready, 1)
                dve.wait_ge(wtot_done, 1)
                dve.tensor_scalar(mean_w[:], ps[:, 0, 0:3], 1.0 / (INNER * D), EPS, ALU.mult, ALU.max).then_inc(pro_chain, 1)
                dve.wait_ge(pro_chain, 1)
                dve.reciprocal(scale_w[:], mean_w[:]).then_inc(pro_chain, 1)
                dve.wait_ge(pro_chain, 2)
                n = 2
                for k in range(3):
                    dve.tensor_scalar(raw[k], raw[k], scale_w[:, k:k + 1], MAGIC, ALU.mult, ALU.add).then_inc(pro_chain, 1)
                    dve.wait_ge(pro_chain, n + 1)
                    dve.tensor_scalar(raw[k], raw[k], -MAGIC, 1.0, ALU.add, ALU.min).then_inc(pro_chain, 1)
                    dve.wait_ge(pro_chain, n + 2)
                    dve.tensor_scalar(tern[k], raw[k], -1.0, None, ALU.max).then_inc(tern_ready, 1)
                    n += 2
                dve.wait_ge(ternT_done, 1)
                for k, dst in ((0, wgT), (1, wuT)):
                    for i in range(KC):
                        dve.tensor_copy(dst[:, i, :], ps[:, 2 * k + i, :].bitcast(BF16))
                for c in range(KC):
                    dve.tensor_copy(wdT[:, :, c * P:(c + 1) * P],
                                    ps[:, 4 + c, :].bitcast(BF16).rearrange("p (i o) -> p i o", i=HC))

            @block.tensor
            def _(pe):
                pe.wait_ge(const_ready, 1)
                pe.wait_ge(wsum_ready, 3)
                pe.matmul(ps[:, 0, 0:3], onesf[:], asum[:], start=True, stop=True).then_inc(wtot_done, 1)
                pe.wait_ge(const_ready, 2)
                pe.wait_ge(tern_ready, 3)
                for k in range(2):
                    t_k = tern[k].rearrange("p (c i) -> p c i", i=D)
                    for i in range(KC):
                        for c in range(HC):
                            pe.transpose(ps[:, 2 * k + i, c * 64:(c + 1) * 64].bitcast(BF16),
                                         t_k[:, c, i * P:(i + 1) * P], identb[:])
                t_d = tern[2].rearrange("p (c i) -> p c i", i=INNER)
                for c in range(KC):
                    for i in range(HC):
                        last = pe.transpose(ps[:, 4 + c, i * 64:(i + 1) * 64].bitcast(BF16),
                                            t_d[:, c, i * P:(i + 1) * P], identb[:])
                last.then_inc(ternT_done, 1)
        nc.all_engine_barrier(sem_only=True)

        ATT = {"L0": dict(nh=4, nk=KV, d=D0, hc=8, gpc=2, groups=4), "a1": dict(nh=2, nk=S, d=D1, hc=4, gpc=2, groups=8),
               "a2": dict(nh=4, nk=KV, d=D1, hc=4, gpc=1, groups=4)}
        NMX, SUMS, REC, ST, MV, VE, RSTD = 0, 64, 96, 128, 144, 150, 154
        AM, RS, SC, SU, SGT, SUT = 160, 164, 168, 172, 176, 180
        LG, EQ, MX, IDX = 190, 206, 222, 226

        def layers(block, it):
            @block.sync
            def _(sp):
                tally = Tally(sems)
                for h in range(2):
                    sp.dma_start(CT[h][0:KV, :], ins["ctx_512"][bass.ds(it * 2 + h, 1)].rearrange("o p n -> p (o n)")
                                 ).then_inc(sem("ctx_loaded", h), 16)
                    sp.dma_start(X[h], ins["x"][bass.ds(it * 2 + h, 1)].rearrange("o (t p) n -> p (o t) n", p=P)
                                 ).then_inc(sem("x_loaded", h), 16)
                for h in range(2):
                    tally.wait(sp, "x5_ready", h)
                    sp.dma_start(x5_dram[bass.ds(it * 2 * S + h * S, S), :].rearrange("(t p) n -> p t n", p=P), X[h]
                                 ).then_inc(sem("x5_stored", h), 16)
                for h in range(2):
                    sp.wait_ge(sem("x5_stored", h), 16)

            @block.gpsimd
            def _(pool):
                tally = Tally(sems)
                chain = [0, 0]

                def rstd(h):
                    tally.wait(pool, "var_ready", h)
                    pool.tensor_tensor(sm(h, VE, 2), sm(h, MV, 4).rearrange("p (t k) -> p t k", k=2)[:, :, 1],
                                       epst[:], ALU.add).then_inc(sem("pool_chain", h), 1)
                    chain[h] += 1
                    pool.wait_ge(sem("pool_chain", h), chain[h])
                    pool.tensor_tensor(sm(h, RSTD, 2), sm(h, VE, 2), neghalf[:], ALU.pow).then_inc(sem("rstd_ready", h), 1)

                def attention(a):
                    q = ATT[a]
                    nh, nk, d, hc, gpc = q["nh"], q["nk"], q["d"], q["hc"], q["gpc"]
                    own = own16 if d == D0 else own32
                    for g in range(q["groups"]):
                        for h in range(2):
                            if g == 0 and a != "a2":
                                tally.wait(pool, "kT_ready", h)
                            if g >= 2:
                                tally.wait(pool, "s_done", h, 2)
                            kt = {"L0": KT0, "a1": KT, "a2": KT2}[a][h][:, g // gpc, :]
                            j0 = (g % gpc) * nh
                            pool.tensor_tensor(
                                KM[h][:, g % 2, 0:nh * nk].rearrange("p (j k) -> p j k", j=nh),
                                kt.rearrange("p (o k) -> p o k", o=1).to_broadcast([P, nh, nk]),
                                own[:, j0:j0 + nh].rearrange("p (j o) -> p j o", o=1).to_broadcast([P, nh, nk]),
                                ALU.mult).then_inc(sem("km_ready", h), 1)
                        if g >= 1 and (g - 1) % gpc == gpc - 1:
                            recs((g - 1) // gpc, a)
                    for h in range(2):
                        tally.n["s_done", h] += 4
                    recs((q["groups"] - 1) // gpc, a)

                def recs(c, a):
                    q = ATT[a]
                    hc, d = q["hc"], q["d"]
                    for h in range(2):
                        tally.wait(pool, "rec_ready", h)
                        if c >= 1:
                            tally.wait(pool, "rt_done", h)
                        for t in range(T):
                            last = pool.tensor_tensor(
                                RBC[h][:, t, :].rearrange("p (j k) -> p j k", k=d),
                                sm(h, REC + t * HEADS + c * hc, hc).rearrange("p (j o) -> p j o", o=1).to_broadcast([P, hc, d]),
                                onesf[:, 0:P].rearrange("p (j k) -> p j k", k=d), ALU.mult)
                        last.then_inc(sem("rbc_ready", h), 1)
                    if c == q["groups"] // q["gpc"] - 1:
                        for h in range(2):
                            tally.n["rt_done", h] += 1

                def add(h, o, x, y, name="res_ready"):
                    pool.tensor_tensor(o, x, y, ALU.add).then_inc(sem(name, h), 1)

                def mlp_residual(h, a):
                    pool.tensor_tensor(Y[h], Y[h], XB[h], ALU.add).then_inc(sem("pool_chain", h), 1)
                    chain[h] += 1
                    pool.wait_ge(sem("pool_chain", h), chain[h])
                    add(h, Y[h], Y[h], bv(f"L1_xattn_{a}_li3_b"))

                for h in range(2):
                    rstd(h)
                for h in range(2):
                    rstd(h)
                    add(h, XB[h], X[h], bv("L0_xattn_bo"))
                attention("L0")
                for h in range(2):
                    rstd(h)
                for _ in range(3):
                    for h in range(2):
                        rstd(h)
                for h in range(2):
                    add(h, XB[h], Y[h], bv("L1_xattn_a1_li1_b"))
                attention("a1")
                for h in range(2):
                    rstd(h)
                    mlp_residual(h, "a1")
                for _ in range(2):
                    for h in range(2):
                        rstd(h)
                for h in range(2):
                    add(h, XB[h], Y[h], bv("L1_xattn_a2_li1_b"))
                attention("a2")
                for h in range(2):
                    rstd(h)
                    mlp_residual(h, "a2")
                for h in range(2):
                    rstd(h)

            @block.vector
            def _(dve):
                tally = Tally(sems)
                chain = [0, 0]

                def step(h, ins_):
                    ins_.then_inc(sem("dve_chain", h), 1)
                    chain[h] += 1
                    dve.wait_ge(sem("dve_chain", h), chain[h])

                def stats(h, src, rows=P, tiles=T):
                    for t in range(tiles):
                        ins_ = dve.bn_stats(small[h][0:rows, ST + 6 * t:ST + 6 * t + 6], src[0:rows, t, :])
                    step(h, ins_)
                    for t in range(tiles):
                        ins_ = dve.bn_aggr(small[h][0:rows, MV + 2 * t:MV + 2 * t + 2],
                                           small[h][0:rows, ST + 6 * t:ST + 6 * t + 6])
                    ins_.then_inc(sem("var_ready", h), 1)

                def apply(h, dst, src, rows=P, tiles=T):
                    tally.wait(dve, "rstd_ready", h)
                    for t in range(tiles):
                        ins_ = dve.tensor_scalar(dst[0:rows, t, :], src[0:rows, t, :],
                                                 small[h][0:rows, MV + 2 * t:MV + 2 * t + 1],
                                                 small[h][0:rows, RSTD + t:RSTD + t + 1], ALU.subtract, ALU.mult)
                    return ins_

                def gain(h, g, b):
                    step(h, dve.tensor_tensor(Y[h], XH[h], bv(g), ALU.mult))
                    step(h, dve.tensor_tensor(Y[h], Y[h], bv(b), ALU.add))

                def quant_scales(h, src, t0, n):
                    step(h, dve.tensor_reduce(sm(h, AM + t0, n), src, AX.X, ALU.max, apply_absolute_value=True))
                    step(h, dve.tensor_scalar(sm(h, AM + t0, n), sm(h, AM + t0, n), EPS, None, ALU.max))
                    step(h, dve.reciprocal(sm(h, RS + t0, n), sm(h, AM + t0, n)))
                    dve.tensor_scalar(sm(h, SU + t0, n), sm(h, AM + t0, n), 1.0 / 127.0, None, ALU.mult)
                    step(h, dve.tensor_scalar(sm(h, SC + t0, n), sm(h, RS + t0, n), 127.0, None, ALU.mult))

                def attention(a):
                    q = ATT[a]
                    nh, nk, d, hc, gpc, ng = q["nh"], q["nk"], q["d"], q["hc"], q["gpc"], q["groups"]
                    units = 2 * ng

                    def row_max(h, u):
                        tally.wait(dve, "s_done", h)
                        dve.tensor_reduce(sm(h, NMX + u * nh, nh),
                                          bank(h, u % 2)[:, 0:nh * nk].rearrange("p (j k) -> p j k", j=nh),
                                          AX.X, ALU.max, negate=True).then_inc(sem("max_done", h), 1)

                    def evacuate(h, u):
                        g, t = divmod(u, 2)
                        tally.wait(dve, "t_done", h)
                        if t == 0 and g >= 2:
                            tally.wait(dve, "pv_done", h)
                        if a == "a1":
                            pt = PT[h][:, g % 2, :].rearrange("p (c j s) -> p c j s", c=2, j=nh)
                            msk = later[:].rearrange("p (o s) -> p o s", o=1).to_broadcast([P, nh, P])
                            if t == 0:
                                src = bank(h, 2).rearrange("p (c j s) -> p c j s", c=2, j=nh)
                                dve.tensor_tensor(pt[:, 0, :, 0:P], src[:, 0], msk, ALU.mult)
                                ins_ = dve.tensor_copy(pt[:, 1, :, 0:P], src[:, 1])
                            else:
                                src = bank(h, 2)[:, 0:nh * P].rearrange("p (j s) -> p j s", j=nh)
                                ins_ = dve.tensor_tensor(pt[:, 1, :, P:S], src, msk, ALU.mult)
                        else:
                            pt = PT[h][0:KV, g % 2, :].rearrange("p (j s) -> p j s", j=nh)
                            ins_ = dve.tensor_copy(pt[:, :, t * P:(t + 1) * P],
                                                   bank(h, 2)[0:KV].rearrange("p (j s) -> p j s", j=nh))
                        ins_.then_inc(sem("pt_ready", h), 1)

                    def recip(h, c):
                        tally.wait(dve, "exp_done", h, 2 * gpc)
                        sums = sm(h, SUMS, 2 * HEADS).rearrange("p (t j) -> p t j", t=T)[:, :, c * hc:(c + 1) * hc]
                        rec = sm(h, REC, 2 * HEADS).rearrange("p (t j) -> p t j", t=T)[:, :, c * hc:(c + 1) * hc]
                        dve.reciprocal(rec, sums).then_inc(sem("rec_ready", h), 1)

                    def normalise(h, c):
                        tally.wait(dve, "rts_ready", h)
                        dve.tensor_tensor(OT[h][:, c, :], bank(h, 3)[:, (c % 2) * S:(c % 2) * S + S], RTS[h], ALU.mult
                                          ).then_inc(sem("oT_ready", h), 1)

                    for u in range(units + 3):
                        for h in range(2):
                            v = u - 3
                            if v >= 0 and v % (2 * gpc) == 2 * gpc - 1:
                                normalise(h, v // (2 * gpc))
                            if u < units:
                                row_max(h, u)
                            if 1 <= u <= units:
                                evacuate(h, u - 1)
                            v = u - 1
                            if 0 <= v < units and v % (2 * gpc) == 2 * gpc - 1:
                                recip(h, v // (2 * gpc))
                    for h in range(2):
                        tally.n["pv_done", h] += 2

                def mlp(a, dst_residual):
                    for h in range(2):
                        tally.wait(dve, "out_done", h)
                        tally.wait(dve, "res_ready", h)
                        step(h, dve.tensor_tensor(XB[h], bank(h, 0).rearrange("p (t n) -> p t n", t=T), XB[h], ALU.add))
                        stats(h, XB[h])
                    for h in range(2):
                        apply(h, XH[h], XB[h]).then_inc(sem("xhat_ready", h), 1)
                    for h in range(2):
                        tally.wait(dve, "out_done", h)
                        tally.wait(dve, "res_ready", h)
                        step(h, dve.tensor_tensor(Y[h], bank(h, 0, 2)[:, :, 0:D], Y[h], ALU.add))
                        dst_residual(h)

                for h in range(2):
                    dve.wait_ge(sem("ctx_loaded", h), 16)
                    stats(h, CT[h].rearrange("p (t n) -> p t n", t=1), KV, 1)
                for h in range(2):
                    apply(h, CH[h].rearrange("p (t n) -> p t n", t=1), CT[h].rearrange("p (t n) -> p t n", t=1), KV, 1
                          ).then_inc(sem("xhat_ready", h), 1)
                for h in range(2):
                    dve.wait_ge(sem("x_loaded", h), 16)
                    stats(h, X[h])
                for h in range(2):
                    apply(h, XH[h], X[h]).then_inc(sem("xhat_ready", h), 1)
                for h in range(2):
                    tally.wait(dve, "ctx_proj_done", h)
                    for par in range(2):
                        dve.tensor_tensor(VM[h][0:KV, :, par, par * D0:(par + 1) * D0],
                                          bank(h, 3)[0:KV, 256:512].rearrange("p (a b d) -> p a b d", b=2, d=D0)[:, :, par, :],
                                          bvec[0:KV, BC.index("L0_xattn_bv"), :].rearrange("p (a b d) -> p a b d", b=2, d=D0)[:, :, par, :],
                                          ALU.add)
                    dve.tensor_copy(V2[h][0:KV, :], bank(h, 2)[0:KV]).then_inc(sem("v_ready", h), 1)
                for h in range(2):
                    tally.wait(dve, "q_done", h)
                    for m in range(KC):
                        ins_ = dve.tensor_scalar(QT[h][:, m, :], bank(h, 2)[:, m * S:(m + 1) * S], pv("L0_xattn_bq", m),
                                                 D0 ** -0.5, ALU.add, ALU.mult)
                    ins_.then_inc(sem("qT_ready", h), 1)
                attention("L0")

                for h in range(2):
                    tally.wait(dve, "out_done", h)
                    tally.wait(dve, "res_ready", h)
                    step(h, dve.tensor_tensor(X[h], bank(h, 0).rearrange("p (t n) -> p t n", t=T), XB[h], ALU.add))
                    stats(h, X[h])
                for h in range(2):
                    step(h, apply(h, XH[h], X[h]))
                    quant_scales(h, XH[h], 0, T)
                    dve.tensor_scalar(sm(h, SGT, T), sm(h, SU, T), mean_w[:, 0:1], None, ALU.mult)
                    dve.tensor_scalar(sm(h, SUT, T), sm(h, SU, T), mean_w[:, 1:2], None, ALU.mult)
                    for t in range(T):
                        ins_ = dve.tensor_scalar(XH[h][:, t, :], XH[h][:, t, :], sm(h, SC + t, 1), MAGIC, ALU.mult, ALU.add)
                    step(h, ins_)
                    dve.tensor_scalar(N1[h], XH[h], -MAGIC, 127.0, ALU.add, ALU.min).then_inc(sem("xhat_ready", h), 1)
                for k in range(4):
                    for h in range(2):
                        t, j = divmod(k, 2)
                        tally.wait(dve, "silu_done", h)
                        dve.scalar_tensor_tensor(HH[h][:, t, j * 512:(j + 1) * 512], bank(h, 2 * (k % 2) + 1),
                                                 sm(h, SUT + t, 1), SG[h][:, k % 2, :], ALU.mult, ALU.mult
                                                 ).then_inc(sem("hh_done", h), 1)
                        tally.n["hh_done", h] += 1
                for h in range(2):
                    dve.wait_ge(sem("hh_done", h), tally.n["hh_done", h])
                    quant_scales(h, HH[h], 0, T)
                    step(h, dve.tensor_scalar(sm(h, SUT, T), sm(h, SU, T), mean_w[:, 2:3], None, ALU.mult))
                    for t in range(T):
                        step(h, dve.tensor_scalar(HH[h][:, t, :], HH[h][:, t, :], sm(h, SC + t, 1), MAGIC, ALU.mult, ALU.add))
                        dve.tensor_scalar(N2[h][:, t, :], HH[h][:, t, :], -MAGIC, 127.0, ALU.add, ALU.min
                                          ).then_inc(sem("n2_ready", h), 1)
                for h in range(2):
                    tally.wait(dve, "out_done", h)
                    for t in range(T):
                        ins_ = dve.scalar_tensor_tensor(X[h][:, t, :], bank(h, 2)[:, t * D:(t + 1) * D], sm(h, SUT + t, 1),
                                                        X[h][:, t, :], ALU.mult, ALU.add)
                    step(h, ins_)
                    stats(h, X[h])

                for h in range(2):
                    step(h, apply(h, XH[h], X[h]))
                    stats(h, XH[h])
                for h in range(2):
                    step(h, apply(h, XH[h], XH[h]))
                    gain(h, "L1_xattn_ln1_g", "L1_xattn_ln1_b")
                    stats(h, Y[h])
                for h in range(2):
                    apply(h, XH[h], Y[h]).then_inc(sem("xhat_ready", h), 1)
                for h in range(2):
                    tally.wait(dve, "q_done", h)
                    dve.tensor_scalar(QT[h].rearrange("p a s -> p (a s)").rearrange("p (a s) -> p a s", a=2), bank(h, 0, 2),
                                      D1 ** -0.5, None, ALU.mult).then_inc(sem("qT_ready", h), 1)
                attention("a1")

                def after_a1(h):
                    stats(h, Y[h])
                mlp("a1", after_a1)
                for h in range(2):
                    step(h, apply(h, XH[h], Y[h]))
                    gain(h, "L1_xattn_ln2_g", "L1_xattn_ln2_b")
                    stats(h, Y[h])
                for h in range(2):
                    apply(h, XH[h], Y[h]).then_inc(sem("xhat_ready", h), 1)
                for h in range(2):
                    tally.wait(dve, "q_done", h)
                    dve.tensor_scalar(QT[h].rearrange("p a s -> p (a s)").rearrange("p (a s) -> p a s", a=2), bank(h, 0, 2),
                                      D1 ** -0.5, None, ALU.mult).then_inc(sem("qT_ready", h), 1)
                attention("a2")

                def after_a2(h):
                    dve.tensor_tensor(X[h], X[h], Y[h], ALU.add).then_inc(sem("x5_ready", h), 1)
                    dve.wait_ge(sem("x5_ready", h), 1)
                    stats(h, X[h])
                mlp("a2", after_a2)
                for h in range(2):
                    apply(h, XH[h], X[h]).then_inc(sem("xhat_ready", h), 1)
                for h in range(2):
                    tally.wait(dve, "logits_done", h)
                    lg = sm(h, LG, 2 * E).rearrange("p (t e) -> p t e", t=T)
                    eq = sm(h, EQ, 2 * E).rearrange("p (t e) -> p t e", t=T)
                    step(h, dve.tensor_tensor(lg, bank(h, 1)[:, 0:2 * E].rearrange("p (t e) -> p t e", t=T),
                                              bgt[:].rearrange("p (o e) -> p o e", o=1).to_broadcast([P, T, E]), ALU.add))
                    step(h, dve.tensor_reduce(sm(h, MX, T), lg, AX.X, ALU.max))
                    step(h, dve.tensor_tensor(eq, lg, sm(h, MX, T).rearrange("p (t o) -> p t o", o=1).to_broadcast([P, T, E]),
                                              ALU.is_lt))
                    eb = eidx[:].rearrange("p (o e) -> p o e", o=1).to_broadcast([P, T, E])
                    step(h, dve.scalar_tensor_tensor(lg, eq, float(E), eb, ALU.mult, ALU.add))
                    step(h, dve.tensor_reduce(sm(h, IDX, T), lg, AX.X, ALU.min))
                    dve.tensor_tensor(onehot[:, bass.ds(it * 4 + h * 2, T), :], eb,
                                      sm(h, IDX, T).rearrange("p (t o) -> p t o", o=1).to_broadcast([P, T, E]), ALU.is_equal)

            @block.scalar
            def _(act):
                tally = Tally(sems)

                def attention(a):
                    q = ATT[a]
                    nh, nk, hc, gpc, ng = q["nh"], q["nk"], q["hc"], q["gpc"], q["groups"]
                    units = 2 * ng
                    for u in range(units + 3):
                        for h in range(2):
                            if u < units:
                                g, t = divmod(u, 2)
                                tally.wait(act, "max_done", h)
                                if u >= 2:
                                    tally.wait(act, "t_done", h)
                                for j in range(nh):
                                    head = t * HEADS + g * nh + j
                                    ins_ = act.activation(PR[h][:, u % 2, j * nk:(j + 1) * nk],
                                                          bank(h, u % 2)[:, j * nk:(j + 1) * nk], ACT.Exp,
                                                          bias=sm(h, NMX + u * nh + j, 1), scale=1.0,
                                                          accum_out=sm(h, SUMS + head, 1))
                                ins_.then_inc(sem("exp_done", h), 1)
                            v = u - 2
                            if v >= 0 and v % (2 * gpc) == 2 * gpc - 1:
                                c = v // (2 * gpc)
                                tally.wait(act, "rt_done", h)
                                if c >= 1:
                                    tally.wait(act, "oT_ready", h)
                                act.activation(RTS[h], bank(h, 3)[:, ((c + 1) % 2) * S:((c + 1) % 2) * S + S], ACT.Copy
                                               ).then_inc(sem("rts_ready", h), 1)
                    for h in range(2):
                        tally.n["t_done", h] += 2
                        tally.n["oT_ready", h] += 1

                def transposed(h, dst, g, b):
                    for m in range(KC):
                        ins_ = act.activation(dst[h][:, m, :], bank(h, 3)[:, m * S:(m + 1) * S], ACT.Identity,
                                              bias=pv(b, m), scale=pv(g, m))
                    return ins_

                def mlp(a):
                    for h in range(2):
                        tally.wait(act, "xhatT_done", h)
                        transposed(h, FT, f"L1_xattn_{a}_ln3_g", f"L1_xattn_{a}_ln3_b").then_inc(sem("featT_ready", h), 1)
                    for h in range(2):
                        for k in range(HC // 2):
                            tally.wait(act, "h_done", h)
                            for m in (2 * k, 2 * k + 1):
                                ins_ = act.activation(HT[h][:, m, :], bank(h, k)[:, (m % 2) * S:(m % 2) * S + S], ACT.Gelu,
                                                      bias=pv(f"L1_xattn_{a}_li2_b", m), scale=1.0)
                            ins_.then_inc(sem("gelu_done", h), 1)

                for h in range(2):
                    tally.wait(act, "xhatT_done", h)
                    act.activation(CTT[h], bank(h, 3)[:, 0:KV], ACT.Copy)
                    act.activation(CYT[h], bank(h, 3)[:, P:P + KV], ACT.Identity, bias=pv("L1_xattn_a2_lny_b", 0),
                                   scale=pv("L1_xattn_a2_lny_g", 0)).then_inc(sem("featT_ready", h), 1)
                for h in range(2):
                    tally.wait(act, "ctx_proj_done", h)
                    for m in range(2):
                        act.activation(KT0[h][:, m, :], bank(h, 0)[:, m * KV:(m + 1) * KV], ACT.Identity,
                                       bias=pv("L0_xattn_bk", m), scale=1.0)
                    act.activation(KT2[h].rearrange("p a k -> p (a k)"), bank(h, 1)[:, 0:4 * KV], ACT.Copy
                                   ).then_inc(sem("kT_ready", h), 1)
                for h in range(2):
                    tally.wait(act, "xhatT_done", h)
                    act.activation(FT[h].rearrange("p a s -> p (a s)"), bank(h, 3), ACT.Copy).then_inc(sem("featT_ready", h), 1)
                attention("L0")
                for h in range(2):
                    tally.wait(act, "xhatT_done", h)
                    act.activation(N1T[h].rearrange("p a s -> p (a s)"), bank(h, 3).bitcast(BF16)[:, 0:512], ACT.Copy
                                   ).then_inc(sem("featT_ready", h), 1)
                for k in range(4):
                    for h in range(2):
                        tally.wait(act, "gu_done", h)
                        if k >= 2:
                            tally.wait(act, "hh_done", h)
                        act.activation(SG[h][:, k % 2, :], bank(h, 2 * (k % 2)), ACT.Silu,
                                       scale=sm(h, SGT + k // 2, 1)).then_inc(sem("silu_done", h), 1)
                for h in range(2):
                    tally.n["hh_done", h] += 2
                for h in range(2):
                    for t in range(T):
                        tally.wait(act, "n2T_done", h)
                        act.activation(N2T[h][:, :, t * P:(t + 1) * P],
                                       bank(h, t).bitcast(BF16).rearrange("p (c s) -> p c s", c=HC), ACT.Copy
                                       ).then_inc(sem("n2T_ready", h), 1)
                for h in range(2):
                    tally.wait(act, "xhatT_done", h)
                    transposed(h, FT, "L1_xattn_a1_lnx_g", "L1_xattn_a1_lnx_b")
                    transposed(h, FT2, "L1_xattn_a1_lny_g", "L1_xattn_a1_lny_b").then_inc(sem("featT_ready", h), 1)
                for h in range(2):
                    tally.wait(act, "kv_done", h)
                    act.activation(KT[h].rearrange("p a s -> p (a s)").rearrange("p (a s) -> p a s", a=2), bank(h, 2, 2),
                                   ACT.Copy).then_inc(sem("kT_ready", h), 1)
                for h in range(2):
                    tally.wait(act, "kv_done", h)
                    act.activation(V1[h], bank(h, 0, 2), ACT.Copy).then_inc(sem("v_ready", h), 1)
                attention("a1")
                mlp("a1")
                for h in range(2):
                    tally.wait(act, "xhatT_done", h)
                    transposed(h, FT, "L1_xattn_a2_lnx_g", "L1_xattn_a2_lnx_b").then_inc(sem("featT_ready", h), 1)
                attention("a2")
                mlp("a2")
                for h in range(2):
                    tally.wait(act, "xhatT_done", h)
                    act.activation(FT[h].rearrange("p a s -> p (a s)"), bank(h, 3), ACT.Copy).then_inc(sem("featT_ready", h), 1)

            @block.tensor
            def _(pe):
                tally = Tally(sems)

                def transpose_x(h):
                    tally.wait(pe, "xhat_ready", h)
                    for m in range(KC):
                        for t in range(T):
                            ins_ = pe.transpose(bank(h, 3)[:, m * S + t * P:m * S + (t + 1) * P],
                                                XH[h][:, t, m * P:(m + 1) * P], ident[:])
                    ins_.then_inc(sem("xhatT_done", h), 1)

                def feature_major(outs, w, x, kc=KC):
                    for m, o in enumerate(outs):
                        for c in range(kc):
                            ins_ = pe.matmul(o, w[:, c, m * P:(m + 1) * P], x[:, c, :], start=(c == 0), stop=(c == kc - 1))
                    return ins_

                def attention(a, queries_waited=False):
                    q = ATT[a]
                    nh, nk, d, hc, gpc, ng = q["nh"], q["nk"], q["d"], q["hc"], q["gpc"], q["groups"]
                    units = 2 * ng

                    def scores(h, u):
                        g, t = divmod(u, 2)
                        if u == 0 and not queries_waited:
                            tally.wait(pe, "qT_ready", h)
                        if t == 0:
                            tally.wait(pe, "km_ready", h)
                        pe.matmul(bank(h, u % 2)[:, 0:nh * nk], QT[h][:, g // gpc, t * P:(t + 1) * P],
                                  KM[h][:, g % 2, 0:nh * nk], start=True, stop=True).then_inc(sem("s_done", h), 1)

                    def transpose_p(h, u):
                        g, t = divmod(u, 2)
                        tally.wait(pe, "exp_done", h)
                        if u >= 1:
                            tally.wait(pe, "pt_ready", h)
                        p = PR[h][:, u % 2, :]
                        if a == "a1":
                            blocks = [(c, j) for c in range(t, 2) for j in range(nh)]
                        else:
                            blocks = [(0, j) for j in range(nh)]
                        for n, (c, j) in enumerate(blocks):
                            kk = min(nk, P)
                            ins_ = pe.transpose(bank(h, 2)[0:kk, n * P:(n + 1) * P],
                                                p[:, j * nk + c * P:j * nk + c * P + kk], ident[:])
                        ins_.then_inc(sem("t_done", h), 1)

                    def values(h, g):
                        dve_seen = tally.n["pt_ready", h]
                        need = base[h] + 2 * g + 2
                        if need > dve_seen:
                            tally.wait(pe, "pt_ready", h, need - dve_seen)
                        c = g // gpc
                        if g % gpc == 0 and c >= 1:
                            tally.wait(pe, "oT_ready", h)
                        o = bank(h, 3)[:, (c % 2) * S:(c % 2) * S + S]
                        if a == "a1":
                            pt = PT[h][:, g % 2, :].rearrange("p (c j s) -> p c j s", c=2, j=nh)
                            for c2, n in ((1, S), (0, P)):
                                for j in range(nh):
                                    strip = 32 * ((g % 2) * nh + j)
                                    hd = (g * nh + j) * D1
                                    ins_ = pe.matmul(o[strip:strip + 32, 0:n], V1[h][:, c2, hd:hd + D1], pt[:, c2, j, 0:n],
                                                     start=(c2 == 1), stop=(c2 == 0), tile_position=(0, strip))
                        else:
                            pt = PT[h][0:KV, g % 2, :].rearrange("p (j s) -> p j s", j=nh)
                            order = (0, 2, 1, 3) if a == "L0" else range(nh)
                            for j in order:
                                head = g * nh + j
                                if a == "L0":
                                    strip = 32 * ((head // 2) % 4)
                                    ins_ = pe.matmul(o[strip:strip + 32, :], VM[h][0:KV, head // 2, head % 2, :], pt[:, j, :],
                                                     start=(head % 2 == 0), stop=(head % 2 == 1), tile_position=(0, strip))
                                else:
                                    strip = 32 * j
                                    ins_ = pe.matmul(o[strip:strip + 32, :], V2[h][0:KV, head * D1:(head + 1) * D1], pt[:, j, :],
                                                     start=True, stop=True, tile_position=(0, strip))
                        ins_.then_inc(sem("pv_done", h), 1)
                        if g % gpc == gpc - 1:
                            tally.wait(pe, "rbc_ready", h)
                            for t in range(T):
                                at = ((c + 1) % 2) * S + t * P
                                ins_ = pe.transpose(bank(h, 3)[:, at:at + P], RBC[h][:, t, :], ident[:])
                            ins_.then_inc(sem("rt_done", h), 1)

                    base = [tally.n["pt_ready", h] for h in range(2)]
                    for u in range(units + 3):
                        for h in range(2):
                            if u < units:
                                scores(h, u)
                            if 1 <= u <= units:
                                transpose_p(h, u - 1)
                            v = u - 2
                            if 0 <= v < units and v % 2 == 1:
                                values(h, v // 2)
                def output(h, w, chunks):
                    tally.wait(pe, "oT_ready", h)
                    for t in range(T):
                        for c in range(chunks):
                            ins_ = pe.matmul(bank(h, 0)[:, t * D:(t + 1) * D], OT[h][:, c, t * P:(t + 1) * P], w[:, c, :],
                                             start=(c == 0), stop=(c == chunks - 1))
                    ins_.then_inc(sem("out_done", h), 1)

                def mlp(a):
                    w = w1[a]
                    for h in range(2):
                        transpose_x(h)
                    for h in range(2):
                        tally.wait(pe, "featT_ready", h)
                        for k in range(HC // 2):
                            for m in (2 * k, 2 * k + 1):
                                for c in range(KC):
                                    ins_ = pe.matmul(bank(h, k)[:, (m % 2) * S:(m % 2) * S + S], w["li2"][:, c, m * P:(m + 1) * P],
                                                     FT[h][:, c, :], start=(c == 0), stop=(c == KC - 1))
                            ins_.then_inc(sem("h_done", h), 1)
                    for h in range(2):
                        tally.wait(pe, "gelu_done", h, 2)
                        for c in range(HC):
                            if c in (4, 6):
                                tally.wait(pe, "gelu_done", h)
                            for t in range(T):
                                ins_ = pe.matmul(bank(h, t)[:, 0:D], HT[h][:, c, t * P:(t + 1) * P], w["li3"][:, c, :],
                                                 start=(c == 0), stop=(c == HC - 1))
                        ins_.then_inc(sem("out_done", h), 1)

                for h in range(2):
                    tally.wait(pe, "xhat_ready", h)
                    pe.transpose(bank(h, 3)[:, 0:KV], CT[h][0:KV, :], ident[0:KV, 0:KV])
                    pe.transpose(bank(h, 3)[:, P:P + KV], CH[h][0:KV, :], ident[0:KV, 0:KV]).then_inc(sem("xhatT_done", h), 1)
                for h in range(2):
                    tally.wait(pe, "featT_ready", h)
                    for m in range(2):
                        pe.matmul(bank(h, 0)[:, m * KV:(m + 1) * KV], wk0[:, m * P:(m + 1) * P], CTT[h], start=True, stop=True)
                    pe.matmul(bank(h, 3)[0:KV, 256:512], CTT[h], wv0[:], start=True, stop=True)
                    for m in range(4):
                        pe.matmul(bank(h, 1)[:, m * KV:(m + 1) * KV], w1["a2"]["wk"][:, 0, m * P:(m + 1) * P], CYT[h],
                                  start=True, stop=True)
                    pe.matmul(bank(h, 2)[0:KV, :], CYT[h], w1["a2"]["wv"][:, 0, :], start=True, stop=True
                              ).then_inc(sem("ctx_proj_done", h), 1)
                for h in range(2):
                    tally.wait(pe, "v_ready", h)
                    transpose_x(h)
                for h in range(2):
                    tally.wait(pe, "featT_ready", h)
                    tally.wait(pe, "kT_ready", h)
                    feature_major([bank(h, 2)[:, m * S:(m + 1) * S] for m in range(2)], wq0, FT[h]
                                  ).then_inc(sem("q_done", h), 1)
                attention("L0")
                for h in range(2):
                    output(h, wo0, KC)
                for h in range(2):
                    tally.wait(pe, "xhat_ready", h)
                    n1t = bank(h, 3).bitcast(BF16)
                    for m in range(KC):
                        for t in range(T):
                            ins_ = pe.transpose(n1t[:, m * S + t * P:m * S + (t + 1) * P], N1[h][:, t, m * P:(m + 1) * P], identb[:])
                    ins_.then_inc(sem("xhatT_done", h), 1)
                for k in range(4):
                    for h in range(2):
                        t, j = divmod(k, 2)
                        if k == 0:
                            tally.wait(pe, "featT_ready", h)
                        if k >= 2:
                            tally.wait(pe, "hh_done", h)
                        for n, w in enumerate((wgT, wuT)):
                            for c in range(KC):
                                ins_ = pe.matmul(bank(h, 2 * (k % 2) + n), N1T[h][:, c, t * P:(t + 1) * P],
                                                 w[:, c, j * 512:(j + 1) * 512], start=(c == 0), stop=(c == KC - 1))
                        ins_.then_inc(sem("gu_done", h), 1)
                for h in range(2):
                    tally.n["hh_done", h] += 2
                for h in range(2):
                    for t in range(T):
                        tally.wait(pe, "n2_ready", h)
                        n2t = bank(h, t).bitcast(BF16)
                        for c in range(HC):
                            ins_ = pe.transpose(n2t[:, c * P:(c + 1) * P], N2[h][:, t, c * P:(c + 1) * P], identb[:])
                        ins_.then_inc(sem("n2T_done", h), 1)
                for h in range(2):
                    for t in range(T):
                        tally.wait(pe, "n2T_ready", h)
                        for c in range(HC):
                            ins_ = pe.matmul(bank(h, 2)[:, t * D:(t + 1) * D], N2T[h][:, c, t * P:(t + 1) * P], wdT[:, c, :],
                                             start=(c == 0), stop=(c == HC - 1))
                    ins_.then_inc(sem("out_done", h), 1)
                w = w1["a1"]
                for h in range(2):
                    transpose_x(h)
                for h in range(2):
                    tally.wait(pe, "featT_ready", h)
                    halves = [bank(h, b)[:, k * S:(k + 1) * S] for b in range(4) for k in range(2)]
                    feature_major(halves[0:4], w["wq"], FT[h]).then_inc(sem("q_done", h), 1)
                    feature_major(halves[4:8], w["wk"], FT2[h]).then_inc(sem("kv_done", h), 1)
                for h in range(2):
                    tally.wait(pe, "qT_ready", h)
                    for t in range(T):
                        for c in range(KC):
                            ins_ = pe.matmul(bank(h, t), FT2[h][:, c, t * P:(t + 1) * P], w["wv"][:, c, :],
                                             start=(c == 0), stop=(c == KC - 1))
                    ins_.then_inc(sem("kv_done", h), 1)
                for h in range(2):
                    tally.wait(pe, "v_ready", h)
                attention("a1", queries_waited=True)
                for h in range(2):
                    output(h, w["li1"], HD // P)
                mlp("a1")
                w = w1["a2"]
                for h in range(2):
                    transpose_x(h)
                for h in range(2):
                    tally.wait(pe, "featT_ready", h)
                    halves = [bank(h, b)[:, k * S:(k + 1) * S] for b in range(4) for k in range(2)]
                    feature_major(halves[0:4], w["wq"], FT[h]).then_inc(sem("q_done", h), 1)
                attention("a2")
                for h in range(2):
                    output(h, w["li1"], HD // P)
                mlp("a2")
                for h in range(2):
                    transpose_x(h)
                for h in range(2):
                    tally.wait(pe, "featT_ready", h)
                    for t in range(T):
                        for c in range(KC):
                            ins_ = pe.matmul(bank(h, 1)[:, t * E:(t + 1) * E], FT[h][:, c, t * P:(t + 1) * P], wg_moe[:, c, :],
                                             start=(c == 0), stop=(c == KC - 1))
                    ins_.then_inc(sem("logits_done", h), 1)

        with nc.Fori(0, B // 2) as it:
            with nc.Block() as block:
                layers(block, it)
            nc.all_engine_barrier(sems_to_clear=sem_range)

        rows = arena[0][:, 0:TILES * ROW].rearrange("p (t n) -> p t n", t=TILES)
        rt = arena[1]
        n_at = [0]

        def alloc(words):
            n_at[0] += words
            return rt[:, n_at[0] - words:n_at[0]]

        tot = [alloc(TILES * E).rearrange("p (t e) -> p t e", e=E) for _ in range(6)]
        seven = [alloc(E) for _ in range(6)]
        pos = alloc(TILES)
        posi = alloc(TILES).bitcast(I32)
        unit_no = alloc(UNITS * E).rearrange("p (u e) -> p u e", e=E)
        below = alloc(UNITS * E).rearrange("p (u e) -> p u e", e=E)
        unit_e = alloc(UNITS)
        unit_ei = sb("unit_ei", [P, UNITS], I32)
        x5_loaded = ctx.enter_context(nc.semaphore("x5_loaded"))
        ids_ready = ctx.enter_context(nc.semaphore("ids_ready"))
        counts_done = ctx.enter_context(nc.semaphore("counts_done"))
        route_chain = ctx.enter_context(nc.semaphore("route_chain"))
        slots_ready = ctx.enter_context(nc.semaphore("slots_ready"))
        rows_sent = ctx.enter_context(nc.semaphore("rows_sent"))

        with nc.Block() as block:
            @block.sync
            def _(sp):
                sp.dma_start(rows[:, :, 0:D], x5_dram.rearrange("(t p) n -> p t n", p=P)).then_inc(x5_loaded, 16)

            @block.tensor
            def _(pe):
                oh = onehot[:].rearrange("p t e -> p (t e)")
                pe.matmul(ps[:, 0, 0:TILES * E], strict[:], oh, start=True, stop=True)
                pe.matmul(ps[:, 1, 0:TILES * E], onesb[:], oh, start=True, stop=True).then_inc(counts_done, 1)

            @block.vector
            def _(dve):
                n = [0]

                def step(ins_):
                    ins_.then_inc(route_chain, 1)
                    n[0] += 1
                    dve.wait_ge(route_chain, n[0])

                dve.wait_ge(counts_done, 1)
                flat = "p (t e) -> p t e"
                step(dve.tensor_copy(tot[0], ps[:, 1, 0:TILES * E].rearrange(flat, e=E)))
                cur = 0
                for k, sh in enumerate((1, 2, 4, 8)):
                    dve.tensor_copy(tot[k + 1][:, 0:sh, :], tot[cur][:, 0:sh, :])
                    step(dve.tensor_tensor(tot[k + 1][:, sh:, :], tot[cur][:, sh:, :], tot[cur][:, :TILES - sh, :], ALU.add))
                    cur = k + 1
                incl = tot[cur]
                step(dve.tensor_scalar(seven[0], incl[:, TILES - 1, :], 1.0 / UNIT, (UNIT - 1.0) / UNIT - 0.5 + 0.25 / UNIT,
                                       ALU.mult, ALU.add))
                step(dve.tensor_scalar(seven[0], seven[0], MAGIC, None, ALU.add))
                step(dve.tensor_scalar(seven[1], seven[0], -MAGIC, None, ALU.add))
                cur = 1
                for k, sh in enumerate((1, 2, 4)):
                    dve.tensor_copy(seven[k + 2][:, 0:sh], seven[cur][:, 0:sh])
                    step(dve.tensor_tensor(seven[k + 2][:, sh:], seven[cur][:, sh:], seven[cur][:, :E - sh], ALU.add))
                    cur = k + 2
                uend = seven[cur]
                step(dve.tensor_tensor(seven[0], uend, seven[1], ALU.subtract))
                step(dve.tensor_scalar(seven[1], seven[0], float(UNIT), None, ALU.mult))
                step(dve.tensor_tensor(tot[5], incl, tot[0], ALU.subtract))
                step(dve.tensor_tensor(tot[5], tot[5], ps[:, 0, 0:TILES * E].rearrange(flat, e=E), ALU.add))
                step(dve.tensor_tensor(tot[5], tot[5], seven[1].rearrange("p (o e) -> p o e", o=1).to_broadcast([P, TILES, E]),
                                       ALU.add))
                step(dve.tensor_tensor(tot[5], tot[5], onehot[:], ALU.mult))
                step(dve.tensor_reduce(pos, tot[5], AX.X, ALU.add))
                dve.tensor_copy(posi, pos).then_inc(slots_ready, 1)
                dve.wait_ge(ids_ready, 2)
                step(dve.tensor_tensor(below, uend.rearrange("p (o e) -> p o e", o=1).to_broadcast([P, UNITS, E]), unit_no,
                                       ALU.is_le))
                step(dve.tensor_reduce(unit_e, below, AX.X, ALU.add))
                dve.tensor_scalar(unit_ei[:], unit_e, float(E - 1), None, ALU.min)

            @block.gpsimd
            def _(pool):
                pool.iota(unit_no, pattern=[[1, UNITS], [0, E]], base=0, channel_multiplier=0,
                          allow_small_or_imprecise_dtypes=True).then_inc(ids_ready, 1)
                pool.iota(rows[:, :, D:ROW], pattern=[[P, TILES]], base=0, channel_multiplier=1,
                          allow_small_or_imprecise_dtypes=True).then_inc(ids_ready, 1)
                pool.wait_ge(ids_ready, 2)
                pool.wait_ge(x5_loaded, 16)
                pool.wait_ge(slots_ready, 1)
                for t in range(TILES):
                    pool.indirect_dma_start(slots_dram, bass.IndirectOffsetOnAxis(ap=posi[:, t:t + 1], axis=0),
                                            rows[:, t, :], None).then_inc(rows_sent, 16)
                pool.wait_ge(rows_sent, 16 * TILES)
        nc.all_engine_barrier(sem_only=True)

        W1B = [view(h, 0, [KC, INNER]) for h in range(2)]
        W2B = [view(h, 2048, [HC, D]) for h in range(2)]
        RB = [view(h, 4096, [T, ROW]) for h in range(2)]
        XHB = [view(h, 4624, [T, D]) for h in range(2)]
        FTB = [view(h, 5136, [KC, UNIT]) for h in range(2)]
        HTB = [view(h, 5648, [HC, UNIT]) for h in range(2)]
        ZB = [view(h, 7696, [T, D]) for h in range(2)]
        IDB = [view(h, 8208, [T]).bitcast(I32) for h in range(2)]
        out_rows = out.rearrange("b s n -> (b s) n")
        enames = ["w_loaded", "rows_loaded", "e_var_ready", "e_rstd_ready", "e_xhat_ready", "e_xhatT_done", "e_featT_ready",
                  "e_h_done", "e_gelu_done", "e_y_done", "z_ready", "e_chain", "e_pool_chain", "scattered"]
        es = {(n, k): ctx.enter_context(nc.semaphore(f"{n}{k}")) for n in enames for k in range(2)}
        CHAIN = 1

        with nc.Block() as block:
            def wait(eng, name, k, value):
                eng.wait_ge(es[name, k], value)

            @block.sync
            def _(sp):
                def load(j, k):
                    e = sp.value_load(unit_ei[0:1, bass.ds(j, 1)] if not isinstance(j, int) else unit_ei[0:1, j:j + 1],
                                      min_val=0, max_val=E - 1)
                    sp.dma_start(RB[k], slots_dram[bass.ds(j * UNIT, UNIT), :].rearrange("(t p) n -> p t n", p=P)
                                 ).then_inc(es["rows_loaded", k], 16)
                    sp.dma_start(W1B[k], ins["L1_ffn_W1"][bass.ds(e, 1)].rearrange("o (c p) n -> p (o c) n", p=P)
                                 ).then_inc(es["w_loaded", k], 16)
                    sp.dma_start(W2B[k], ins["L1_ffn_W2"][bass.ds(e, 1)].rearrange("o (c p) n -> p (o c) n", p=P)
                                 ).then_inc(es["w_loaded", k], 16)

                load(0, 0)
                load(1, 1)
                with sp.Fori(0, UNITS // 2 - 1) as it:
                    for k in range(2):
                        wait(sp, "z_ready", k, it + 1)
                        load(it * 2 + 2 + k, k)
                wait(sp, "z_ready", 0, UNITS // 2)
                load(UNITS - 1, 0)

            @block.gpsimd
            def _(pool):
                def rstd(n, k):
                    wait(pool, "e_var_ready", k, n + 1)
                    pool.tensor_tensor(sm(k, VE, 2), sm(k, MV, 4).rearrange("p (t q) -> p t q", q=2)[:, :, 1],
                                       epst[:], ALU.add).then_inc(es["e_pool_chain", k], 1)
                    wait(pool, "e_pool_chain", k, n + 1)
                    pool.tensor_tensor(sm(k, RSTD, 2), sm(k, VE, 2), neghalf[:], ALU.pow).then_inc(es["e_rstd_ready", k], 1)

                def scatter(n, k):
                    wait(pool, "z_ready", k, n + 1)
                    pool.tensor_tensor(sm(k, IDX, 2), epst[:], epst[:], ALU.add)
                    for t in range(T):
                        pool.indirect_dma_start(out_rows, bass.IndirectOffsetOnAxis(ap=IDB[k][:, t:t + 1], axis=0),
                                                ZB[k][:, t, :], None, bounds_check=TOKENS - 1, oob_is_err=False
                                                ).then_inc(es["scattered", k], 16)

                rstd(0, 0)
                with pool.Fori(0, UNITS // 2) as it:
                    rstd(it, 1)
                    scatter(it, 0)
                    rstd(it + 1, 0)
                    scatter(it, 1)
                    for k in range(2):
                        wait(pool, "scattered", k, (it + 1) * 16 * T)
                scatter(UNITS // 2, 0)
                for k in range(2):
                    pool.wait_ge(es["scattered", k], 16 * T * (UNITS // 2 + 1 - k))

            @block.vector
            def _(dve):
                def link(ins_, n, k, c):
                    ins_.then_inc(es["e_chain", k], 1)
                    wait(dve, "e_chain", k, n * CHAIN + c)

                def normalise(n, k):
                    wait(dve, "rows_loaded", k, n * 16 + 16)
                    for t in range(T):
                        ins_ = dve.bn_stats(sm(k, ST + 6 * t, 6), RB[k][:, t, 0:D])
                    link(ins_, n, k, 1)
                    dve.tensor_copy(sm(k, EQ, 1), sm(k, ST, 1))
                    for t in range(T):
                        ins_ = dve.bn_aggr(sm(k, MV + 2 * t, 2), sm(k, ST + 6 * t, 6))
                    ins_.then_inc(es["e_var_ready", k], 1)
                    wait(dve, "e_rstd_ready", k, n + 1)
                    for t in range(T):
                        ins_ = dve.tensor_scalar(XHB[k][:, t, :], RB[k][:, t, 0:D], sm(k, MV + 2 * t, 1), sm(k, RSTD + t, 1),
                                                 ALU.subtract, ALU.mult)
                    ins_.then_inc(es["e_xhat_ready", k], 1)

                def feature_major(n, k):
                    wait(dve, "e_xhatT_done", k, n + 1)
                    dve.tensor_copy(FTB[k].rearrange("p c s -> p (c s)"), bank(k, 3)).then_inc(es["e_featT_ready", k], 1)

                def result(n, k):
                    ins_ = dve.tensor_copy(IDB[k].rearrange("p (t o) -> p t o", o=1), RB[k][:, :, D:ROW])
                    wait(dve, "e_y_done", k, n + 1)
                    dve.tensor_tensor(ZB[k], bank(k, 0, 2)[:, :, 0:D], RB[k][:, :, 0:D], ALU.add).then_inc(es["z_ready", k], 1)

                normalise(0, 0)
                feature_major(0, 0)
                with dve.Fori(0, UNITS // 2) as it:
                    normalise(it, 1)
                    feature_major(it, 1)
                    result(it, 0)
                    normalise(it + 1, 0)
                    feature_major(it + 1, 0)
                    result(it, 1)
                wait(dve, "scattered", 0, UNITS // 2 * 16 * T)
                result(UNITS // 2, 0)

            @block.scalar
            def _(act):
                def gelu(n, k):
                    for b in range(4):
                        wait(act, "e_h_done", k, n * 4 + b + 1)
                        act.activation(HTB[k][:, 2 * b:2 * b + 2, :].rearrange("p c s -> p (c s)"), bank(k, b),
                                       ACT.Gelu_apprx_tanh).then_inc(es["e_gelu_done", k], 1)

                with act.Fori(0, UNITS // 2) as it:
                    gelu(it, 0)
                    gelu(it, 1)
                gelu(UNITS // 2, 0)

            @block.tensor
            def _(pe):
                def transposes(n, k):
                    wait(pe, "e_xhat_ready", k, n + 1)
                    for m in range(KC):
                        for t in range(T):
                            ins_ = pe.transpose(bank(k, 3)[:, m * UNIT + t * P:m * UNIT + (t + 1) * P],
                                                XHB[k][:, t, m * P:(m + 1) * P], ident[:])
                    ins_.then_inc(es["e_xhatT_done", k], 1)

                def up(n, k):
                    wait(pe, "w_loaded", k, n * 32 + 32)
                    wait(pe, "e_featT_ready", k, n + 1)
                    for b in range(4):
                        for m in (2 * b, 2 * b + 1):
                            for c in range(KC):
                                ins_ = pe.matmul(bank(k, b)[:, (m % 2) * UNIT:(m % 2 + 1) * UNIT], W1B[k][:, c, m * P:(m + 1) * P],
                                                 FTB[k][:, c, :], start=(c == 0), stop=(c == KC - 1))
                        ins_.then_inc(es["e_h_done", k], 1)

                def down(n, k):
                    for c in range(HC):
                        if c in (0, 4, 6):
                            wait(pe, "e_gelu_done", k, n * 4 + (2 if c == 0 else c // 2 + 1))
                        for t in range(T):
                            ins_ = pe.matmul(bank(k, t)[:, 0:D], HTB[k][:, c, t * P:(t + 1) * P], W2B[k][:, c, :],
                                             start=(c == 0), stop=(c == HC - 1))
                    ins_.then_inc(es["e_y_done", k], 1)

                transposes(0, 0)
                with pe.Fori(0, UNITS // 2) as it:
                    up(it, 0)
                    transposes(it, 1)
                    down(it, 0)
                    up(it, 1)
                    transposes(it + 1, 0)
                    down(it, 1)
                up(UNITS // 2, 0)
                down(UNITS // 2, 0)


def kernel(**inputs):
    import numpy as _np
    import concourse.bacc as _bacc
    from concourse import mybir as _mybir
    from concourse.bass_utils import run_bass_kernel_spmd as _run

    nc = _bacc.Bacc("TRN2", target_bir_lowering=False, num_devices=1)
    arrays, ins = {}, {}
    for name, a in inputs.items():
        a = _np.ascontiguousarray(a)
        arrays[f"in_{name}"] = a
        ins[name] = nc.dram_tensor(f"in_{name}", a.shape, _mybir.dt.from_np(a.dtype), kind="ExternalInput").ap()
    out = nc.dram_tensor("out_0", (B, S, D), F32, kind="ExternalOutput").ap()
    build(nc, ins, out)
    r = _run(nc, [arrays], core_ids=[0])
    return r.results[0]["out_0"]
```

```python
from collections import Counter
from contextlib import ExitStack

import concourse.bass as bass
from concourse import mybir

F32 = mybir.dt.float32
BF16 = mybir.dt.bfloat16
I32 = mybir.dt.int32
ALU = mybir.AluOpType
ACT = mybir.ActivationFunctionType
AX = mybir.AxisListType

P = 128
B, S, D = 8, 256, 256
C2, KV = 128, 120
HEADS = 16
D0, D1 = D // HEADS, 32
HD = HEADS * D1
INNER = 1024
E = 8
T = S // P
KC = D // P
HC = INNER // P
TILES = B * T
TOKENS = B * S
EPS = 1e-5
UNIT = 2 * P
UNITS = TOKENS // UNIT + E - 1
ROW = D + 1
MAGIC = 1.5 * 2.0 ** 23
PAD_ID = 1 << 20


class Tally:

    def __init__(self, sems):
        self.sems, self.n = sems, Counter()

    def wait(self, eng, name, h=0, more=1):
        self.n[name, h] += more
        eng.wait_ge(self.sems[name, h], self.n[name, h])


def build(nc, ins, out):
    ctx = ExitStack()
    with ctx:
        def sb(name, shape, dt=F32):
            return ctx.enter_context(nc.sbuf_tensor(name, shape, dt))

        x5_all = nc.dram_tensor("x5_rows", [2 * S + TOKENS, D], F32).ap()
        x5_dram = x5_all[2 * S:, :]
        slots_dram = nc.dram_tensor("slot_rows", [UNITS * UNIT, ROW], F32).ap()

        wq0 = sb("wq0", [P, KC, D]); wk0 = sb("wk0", [P, D]); wv0 = sb("wv0", [P, D]); wo0 = sb("wo0", [P, KC, D])
        wgT = sb("wgT", [P, KC, INNER], BF16); wuT = sb("wuT", [P, KC, INNER], BF16)
        wdT = sb("wdT", [P, HC, D], BF16)
        w1 = {}
        for a, kc in (("a1", KC), ("a2", 1)):
            w1[a] = dict(wq=sb(a + "_wq", [P, KC, HD]), wk=sb(a + "_wk", [P, kc, HD]), wv=sb(a + "_wv", [P, kc, HD]),
                         li1=sb(a + "_li1", [P, HD // P, D]), li2=sb(a + "_li2", [P, KC, INNER]),
                         li3=sb(a + "_li3", [P, HC, D]))
        wg_moe = sb("wg_moe", [P, KC, E])
        PP = ["L0_xattn_bq", "L0_xattn_bk"]
        for a in ("a1", "a2"):
            PP += [f"L1_xattn_{a}_{n}" for n in ("lnx_g", "lnx_b", "lny_g", "lny_b", "ln3_g", "ln3_b", "li2_b")]
        col, ncol = {}, 0
        for n in PP:
            col[n] = (ncol, ins[n].shape[0] // P)
            ncol += ins[n].shape[0] // P
        pvec = sb("pvec", [P, ncol])
        BC = ["L0_xattn_bv", "L0_xattn_bo", "L1_xattn_ln1_g", "L1_xattn_ln1_b", "L1_xattn_ln2_g", "L1_xattn_ln2_b",
              "L1_xattn_a1_li1_b", "L1_xattn_a1_li3_b", "L1_xattn_a2_li1_b", "L1_xattn_a2_li3_b"]
        bvec = sb("bvec", [P, len(BC), D])
        bgt = sb("bgt", [P, E])

        def pv(n, m):
            return pvec[:, col[n][0] + m:col[n][0] + m + 1]

        def bv(n, tiles=T):
            return bvec[:, BC.index(n):BC.index(n) + 1, :].to_broadcast([P, tiles, D])

        ident = sb("ident", [P, P]); identb = sb("identb", [P, P], BF16)
        later = sb("later", [P, P])
        strict = sb("strict", [P, P], BF16)
        onesb = sb("onesb", [P, P], BF16)
        onesf = sb("onesf", [P, P])
        own16 = sb("own16", [P, 8]); own32 = sb("own32", [P, 4])
        epst = sb("epst", [P, 2]); neghalf = sb("neghalf", [P, 2])
        onepe = sb("onepe", [P, 2]); eps2 = sb("eps2", [P, 2])
        eidx = sb("eidx", [P, E])
        mean_w = sb("mean_w", [P, 3]); scale_w = sb("scale_w", [P, 3]); asum = sb("asum", [P, 3]); wtot = sb("wtot", [P, 3])

        ARENA = 13824
        arena = [sb(f"arena{h}", [P, ARENA]) for h in range(2)]
        small = [sb(f"small{h}", [P, 256]) for h in range(2)]
        onehot_all = sb("onehot", [P, 2 * T + TILES, E], BF16)
        onehot = onehot_all[:, 2 * T:, :]

        def view(h, at, shape, dt=F32):
            n = 1
            for s in shape:
                n *= s
            words = n if dt != BF16 else n // 2
            v = arena[h][:, at:at + words]
            if dt != F32:
                v = v.bitcast(dt)
            if len(shape) == 2:
                v = v.rearrange("p (a b) -> p a b", a=shape[0])
            elif len(shape) == 3:
                v = v.rearrange("p (a b c) -> p a b c", a=shape[0], b=shape[1])
            return v

        X = [view(h, 0, [T, D]) for h in range(2)]
        XH = [view(h, 512, [T, D]) for h in range(2)]
        Y = [view(h, 1024, [T, D]) for h in range(2)]
        XB = [view(h, 1536, [T, D]) for h in range(2)]
        FT = [view(h, 2048, [KC, S]) for h in range(2)]
        QT = [view(h, 2560, [4, S]) for h in range(2)]
        KT = [view(h, 3584, [4, S]) for h in range(2)]
        V1 = [view(h, 4608, [T, HD]) for h in range(2)]
        OT = [view(h, 5632, [4, S]) for h in range(2)]
        PR = [view(h, 6656, [2, 512]) for h in range(2)]
        PT = [view(h, 7680, [2, 1024]) for h in range(2)]
        KM = [view(h, 9728, [2, 512]) for h in range(2)]
        RTS = [view(h, 10752, [S]) for h in range(2)]
        RBC = [view(h, 11008, [T, P]) for h in range(2)]
        KT0 = [view(h, 11264, [2, KV]) for h in range(2)]
        KT2 = [view(h, 11520, [4, KV]) for h in range(2)]
        VM = [view(h, 12032, [8, 2, 32]) for h in range(2)]
        V2 = [view(h, 12544, [HD]) for h in range(2)]
        FT2 = [view(h, 6656, [KC, S]) for h in range(2)]
        XN = [view(h, 13056, [T, D]) for h in range(2)]
        CT = [view(h, 13568, [P]) for h in range(2)]
        CH = [view(h, 13696, [P]) for h in range(2)]
        CTT = [view(h, 10752, [KV]) for h in range(2)]
        CYT = [view(h, 10880, [KV]) for h in range(2)]
        FT5 = [view(h, 3584, [KC, S]) for h in range(2)]
        HH = [view(h, 7680, [T, INNER]) for h in range(2)]
        HT = [view(h, 7680, [HC, S]) for h in range(2)]
        N2 = [view(h, 2560, [T, INNER], BF16) for h in range(2)]
        N2T = [view(h, 3584, [HC, S], BF16) for h in range(2)]
        N1 = [view(h, 1024, [T, D], BF16) for h in range(2)]
        N1T = [view(h, 2048, [KC, S], BF16) for h in range(2)]
        SG = [view(h, 4608, [2, 512]) for h in range(2)]

        def sm(h, at, n):
            return small[h][:, at:at + n]

        ps = ctx.enter_context(nc.psum_tensor("ps", [P, 8, 512], F32))

        def bank(h, b, n=1):
            return ps[:, 4 * h + b, :] if n == 1 else ps[:, 4 * h + b:4 * h + b + n, :]

        NAMES = ["x_loaded", "ctx_loaded", "x5_stored", "cxhat_ready", "var_ready", "rstd_ready", "xhat_ready", "xhatT_done",
                 "featT_ready", "ctx_proj_done", "kT_ready", "v_ready", "cT_done", "cT_ready", "x5hat_ready", "x5T_done", "x5T_ready", "q_done", "qT_ready", "kv_done",
                 "res_ready", "km_ready", "s_done", "max_done", "exp_done", "t_done", "pt_ready", "pv_done",
                 "rec_ready", "rbc_ready", "rt_done", "rts_ready", "oT_ready", "out_done", "gu_done",
                 "silu_done", "hh_done", "n2_ready", "n2T_done", "n2T_ready", "h_done", "gelu_done",
                 "logits_done", "lg_ready", "dve_chain", "pool_chain"]
        sems = {}
        for n in NAMES:
            for h in range(2):
                sems[n, h] = ctx.enter_context(nc.semaphore(f"{n}{h}"))
        numbers = [s.num for s in sems.values()]
        sem_range = range(min(numbers), max(numbers) + 1)
        assert len(sem_range) == len(numbers)

        def sem(name, h=0):
            return sems[name, h]

        raw = [arena[0][:, 2048:4096], arena[0][:, 4096:6144], arena[0][:, 6144:8192]]
        tern = [arena[1][:, 1024 * k:1024 * (k + 1)].bitcast(BF16) for k in range(2, 5)]
        w_load = ctx.enter_context(nc.semaphore("w_load"))
        w1_load = ctx.enter_context(nc.semaphore("w1_load"))
        W1_LOADS = 2 * 3 + 3 + 3 + 3
        first_load = ctx.enter_context(nc.semaphore("first_load"))
        q_load = ctx.enter_context(nc.semaphore("q_load"))
        const_ready = ctx.enter_context(nc.semaphore("const_ready"))
        wsum_ready = ctx.enter_context(nc.semaphore("wsum_ready"))
        wtot_done = ctx.enter_context(nc.semaphore("wtot_done"))
        tern_ready = ctx.enter_context(nc.semaphore("tern_ready"))
        ternT_done = ctx.enter_context(nc.semaphore("ternT_done"))
        pro_chain = ctx.enter_context(nc.semaphore("pro_chain"))
        pads_written = ctx.enter_context(nc.semaphore("pads_written"))

        with nc.Block() as block:
            @block.sync
            def _(sp):
                for k, n in enumerate(("L0_ffn_w_gate", "L0_ffn_w_up")):
                    sp.dma_start(raw[k].rearrange("p (c i) -> p c i", i=D),
                                 ins[n].rearrange("(c p) i -> p c i", p=P)).then_inc(q_load, 16)
                sp.dma_start(raw[2].rearrange("p (c i) -> p c i", i=INNER),
                             ins["L0_ffn_w_down"].rearrange("(c p) i -> p c i", p=P)).then_inc(q_load, 16)
                for h in range(2):
                    sp.dma_start(CT[h][0:KV, :], ins["ctx_512"][h]).then_inc(first_load, 16)
                    sp.dma_start(XN[h], ins["x"][h].rearrange("(t p) n -> p t n", p=P)).then_inc(first_load, 16)
                n_w = 0

                def load(dst, src):
                    sp.dma_start(dst, src).then_inc(w_load, 16)
                    return 16
                n_w += load(wq0[:], ins["L0_xattn_Wq"].rearrange("(c p) n -> p c n", p=P))
                n_w += load(wk0[:], ins["L0_xattn_Wk"])
                n_w += load(wv0[:], ins["L0_xattn_Wv"])
                n_w += load(wo0[:], ins["L0_xattn_Wo"].rearrange("(c p) n -> p c n", p=P))
                n_w += load(wg_moe[:], ins["L1_ffn_Wg"].rearrange("(c p) n -> p c n", p=P))
                n_w += load(bgt[:], ins["L1_ffn_bg"].rearrange("(a n) -> a n", a=1).to_broadcast([P, E]))
                for k, n in enumerate(BC):
                    n_w += load(bvec[:, k, :], ins[n].rearrange("(a n) -> a n", a=1).to_broadcast([P, D]))
                with nc.allow_non_contiguous_dma(reason="per-feature vectors onto partitions, small"):
                    for n in PP:
                        c0, m = col[n]
                        n_w += load(pvec[:, c0:c0 + m], ins[n].rearrange("(c p) -> p c", p=P))
                for a in ("a2", "a1"):
                    w = w1[a]
                    for n in ("wk", "wv", "wq"):
                        src = ins[f"L1_xattn_{a}_{n}"]
                        for c in range(src.shape[1] // P):
                            sp.dma_start(w[n][:, c, :].rearrange("p (h d) -> p h d", h=HEADS),
                                         src[:, c * P:(c + 1) * P, :].rearrange("h p d -> p h d")).then_inc(w1_load, 16)
                    for n in ("li1", "li2", "li3"):
                        sp.dma_start(w[n][:], ins[f"L1_xattn_{a}_{n}_w"].rearrange("(c p) n -> p c n", p=P)
                                     ).then_inc(w1_load, 16)
                sp.wait_ge(first_load, 16 * 4)
                sp.wait_ge(w_load, n_w)

            @block.gpsimd
            def _(pool):
                pool.memset(ident[:], 0.0)
                pool.memset(identb[:], 0.0)
                pool.memset(later[:], 1.0)
                pool.memset(strict[:], 1.0)
                pool.memset(onesb[:], 1.0)
                pool.memset(onesf[:], 1.0)
                pool.memset(own16[:], 1.0)
                pool.memset(own32[:], 1.0)
                pool.memset(epst[:], EPS)
                pool.memset(onepe[:], 1.0 + EPS)
                pool.memset(eps2[:], EPS * EPS)
                pool.memset(neghalf[:], -0.5)
                pool.iota(eidx[:], pattern=[[1, E]], base=0, channel_multiplier=0,
                          allow_small_or_imprecise_dtypes=True).then_inc(const_ready, 1)
                pool.wait_ge(const_ready, 1)
                for m in (ident, identb):
                    pool.affine_select(out=m[:], in_=m[:], compare_op=ALU.not_equal, fill=1.0, base=0,
                                       pattern=[[-1, P]], channel_multiplier=1)
                pool.affine_select(out=later[:], in_=later[:], compare_op=ALU.is_gt, fill=0.0, base=0,
                                   pattern=[[-1, P]], channel_multiplier=1)
                pool.affine_select(out=strict[:], in_=strict[:], compare_op=ALU.is_gt, fill=0.0, base=0,
                                   pattern=[[1, P]], channel_multiplier=-1).then_inc(const_ready, 1)
                for m, width, n in ((own16, 16, 8), (own32, 32, 4)):
                    pool.affine_select(out=m[:], in_=m[:], compare_op=ALU.is_ge, fill=0.0, base=0,
                                       pattern=[[-width, n]], channel_multiplier=1).then_inc(const_ready, 1)
                pool.wait_ge(const_ready, 4)
                for m, width, n in ((own16, 16, 8), (own32, 32, 4)):
                    pool.affine_select(out=m[:], in_=m[:], compare_op=ALU.is_gt, fill=0.0, base=width,
                                       pattern=[[width, n]], channel_multiplier=-1).then_inc(const_ready, 1)
                for h in range(2):
                    pool.memset(VM[h], 0.0).then_inc(const_ready, 1)
                    pool.memset(small[h][:], 0.0)
                    pool.memset(X[h], 0.0)
                pad = arena[0][:, 8192:8192 + ROW]
                pool.memset(pad, float(PAD_ID)).then_inc(const_ready, 1)
                pool.wait_ge(const_ready, 9)
                n_rows = UNITS * UNIT // P
                pool.dma_start(slots_dram.rearrange("(p c) n -> p c n", c=n_rows),
                               pad.rearrange("p (a n) -> p a n", a=1).to_broadcast([P, n_rows, ROW])
                               ).then_inc(pads_written, 16)
                pool.wait_ge(pads_written, 16)

            @block.vector
            def _(dve):
                for k in range(3):
                    dve.wait_ge(q_load, 16 * 3)
                    dve.tensor_reduce(asum[:, k:k + 1], raw[k], AX.X, ALU.add,
                                      apply_absolute_value=True).then_inc(wsum_ready, 1)
                dve.wait_ge(wtot_done, 1)
                dve.tensor_scalar(mean_w[:], ps[:, 0, 0:3], 1.0 / (INNER * D), EPS, ALU.mult, ALU.max).then_inc(pro_chain, 1)
                dve.wait_ge(pro_chain, 1)
                dve.reciprocal(scale_w[:], mean_w[:]).then_inc(pro_chain, 1)
                dve.wait_ge(pro_chain, 2)
                n = 2
                for k in range(3):
                    dve.tensor_scalar(raw[k], raw[k], scale_w[:, k:k + 1], MAGIC, ALU.mult, ALU.add).then_inc(pro_chain, 1)
                    dve.wait_ge(pro_chain, n + 1)
                    dve.tensor_scalar(raw[k], raw[k], -MAGIC, 1.0, ALU.add, ALU.min).then_inc(pro_chain, 1)
                    dve.wait_ge(pro_chain, n + 2)
                    dve.tensor_scalar(tern[k], raw[k], -1.0, None, ALU.max).then_inc(tern_ready, 1)
                    n += 2
                dve.wait_ge(ternT_done, 1)
                for k, dst in ((0, wgT), (1, wuT)):
                    for i in range(KC):
                        dve.tensor_copy(dst[:, i, :], ps[:, 2 * k + i, :].bitcast(BF16))
                for c in range(KC):
                    dve.tensor_copy(wdT[:, :, c * P:(c + 1) * P],
                                    ps[:, 4 + c, :].bitcast(BF16).rearrange("p (i o) -> p i o", i=HC))

            @block.tensor
            def _(pe):
                pe.wait_ge(const_ready, 1)
                pe.wait_ge(wsum_ready, 3)
                pe.matmul(ps[:, 0, 0:3], onesf[:], asum[:], start=True, stop=True).then_inc(wtot_done, 1)
                pe.wait_ge(const_ready, 2)
                pe.wait_ge(tern_ready, 3)
                for k in range(2):
                    t_k = tern[k].rearrange("p (c i) -> p c i", i=D)
                    for i in range(KC):
                        for c in range(HC):
                            pe.transpose(ps[:, 2 * k + i, c * 64:(c + 1) * 64].bitcast(BF16),
                                         t_k[:, c, i * P:(i + 1) * P], identb[:])
                t_d = tern[2].rearrange("p (c i) -> p c i", i=INNER)
                for c in range(KC):
                    for i in range(HC):
                        last = pe.transpose(ps[:, 4 + c, i * 64:(i + 1) * 64].bitcast(BF16),
                                            t_d[:, c, i * P:(i + 1) * P], identb[:])
                last.then_inc(ternT_done, 1)
        nc.all_engine_barrier(sem_only=True)

        ATT = {"L0": dict(nh=4, nk=KV, d=D0, hc=8, gpc=2, groups=4), "a1": dict(nh=2, nk=S, d=D1, hc=4, gpc=2, groups=8),
               "a2": dict(nh=4, nk=KV, d=D1, hc=4, gpc=1, groups=4)}
        NMX, SUMS, REC, ST, MV, VE, RSTD = 0, 32, 64, 96, 108, 112, 114
        AM, RS, SC, SU, SGT, SUT = 120, 124, 128, 132, 136, 140
        LG, EQ, MX, IDX = 148, 164, 180, 182
        SD = 144
        X5 = 96

        def layers(block, it, final=False):
            @block.sync
            def _(sp):
                if final:
                    done = 2 * T * (B // 2 - 1)
                    sp.dma_start(rows[:, 0:done, 0:D], x5_dram[0:done * P, :].rearrange("(t p) n -> p t n", p=P)
                                 ).then_inc(x5_loaded, 16)
                    for h in range(2):
                        at = B // 2 * 2 * S + h * S
                        sp.dma_start(x5_all[at:at + S, :].rearrange("(t p) n -> p t n", p=P), X[h]
                                     ).then_inc(sem("x5_stored", h), 16)
                        t0 = done + h * T
                        sp.dma_start(rows[:, t0:t0 + T, 0:D], X[h]).then_inc(x5_loaded, 16)
                    for h in range(2):
                        sp.wait_ge(sem("x5_stored", h), 16)
                    sp.wait_ge(x5_loaded, 16 * 3)
                    return
                for h in range(2):
                    sp.dma_start(x5_all[bass.ds(it * 2 * S + h * S, S), :].rearrange("(t p) n -> p t n", p=P), X[h]
                                 ).then_inc(sem("x5_stored", h), 16)
                for h in range(2):
                    sp.wait_ge(sem("cT_done", h), 1)
                    sp.wait_ge(sem("cxhat_ready", h), 1)
                    sp.wait_ge(sem("res_ready", h), 1)
                    sp.dma_start(CT[h][0:KV, :], ins["ctx_512"][bass.ds((it * 2 + 2 + h) % B, 1)].rearrange("o p n -> p (o n)")
                                 ).then_inc(sem("ctx_loaded", h), 16)
                    sp.dma_start(XN[h], ins["x"][bass.ds((it * 2 + 2 + h) % B, 1)].rearrange("o (t p) n -> p (o t) n", p=P)
                                 ).then_inc(sem("x_loaded", h), 16)
                for h in range(2):
                    sp.wait_ge(sem("x5_stored", h), 16)
                    sp.wait_ge(sem("ctx_loaded", h), 16)
                    sp.wait_ge(sem("x_loaded", h), 16)

            @block.gpsimd
            def _(pool):
                tally = Tally(sems)
                chain = [0, 0]

                def link(h, ins_):
                    ins_.then_inc(sem("pool_chain", h), 1)
                    chain[h] += 1
                    pool.wait_ge(sem("pool_chain", h), chain[h])

                def rstd(h, o=0, twice=False):
                    tally.wait(pool, "var_ready", h)
                    v = sm(h, o + MV, 4).rearrange("p (t k) -> p t k", k=2)[:, :, 1]
                    if twice:
                        link(h, pool.tensor_tensor(sm(h, o + VE, 2), v, onepe[:], ALU.mult))
                        link(h, pool.tensor_tensor(sm(h, o + VE, 2), sm(h, o + VE, 2), eps2[:], ALU.add))
                    else:
                        link(h, pool.tensor_tensor(sm(h, o + VE, 2), v, epst[:], ALU.add))
                    pool.tensor_tensor(sm(h, o + RSTD, 2), sm(h, o + VE, 2), neghalf[:], ALU.pow
                                       ).then_inc(sem("rstd_ready", h), 1)

                def attention(a):
                    q = ATT[a]
                    nh, nk, d, hc, gpc = q["nh"], q["nk"], q["d"], q["hc"], q["gpc"]
                    own = own16 if d == D0 else own32
                    for g in range(q["groups"]):
                        for h in range(2):
                            if g == 0 and a != "a2":
                                tally.wait(pool, "kT_ready", h, 1 if a == "L0" else 2)
                            if g >= 2:
                                tally.wait(pool, "s_done", h, 2)
                            kt = {"L0": KT0, "a1": KT, "a2": KT2}[a][h][:, g // gpc, :]
                            j0 = (g % gpc) * nh
                            pool.tensor_tensor(
                                KM[h][:, g % 2, 0:nh * nk].rearrange("p (j k) -> p j k", j=nh),
                                kt.rearrange("p (o k) -> p o k", o=1).to_broadcast([P, nh, nk]),
                                own[:, j0:j0 + nh].rearrange("p (j o) -> p j o", o=1).to_broadcast([P, nh, nk]),
                                ALU.mult).then_inc(sem("km_ready", h), 1)
                        if g >= 1 and (g - 1) % gpc == gpc - 1:
                            recs((g - 1) // gpc, a)
                    for h in range(2):
                        tally.n["s_done", h] += 4
                    recs((q["groups"] - 1) // gpc, a)

                def recs(c, a):
                    q = ATT[a]
                    hc, d = q["hc"], q["d"]
                    for h in range(2):
                        tally.wait(pool, "rec_ready", h)
                        if c >= 1:
                            tally.wait(pool, "rt_done", h)
                        for t in range(T):
                            last = pool.tensor_tensor(
                                RBC[h][:, t, :].rearrange("p (j k) -> p j k", k=d),
                                sm(h, REC + t * HEADS + c * hc, hc).rearrange("p (j o) -> p j o", o=1).to_broadcast([P, hc, d]),
                                onesf[:, 0:P].rearrange("p (j k) -> p j k", k=d), ALU.mult)
                        last.then_inc(sem("rbc_ready", h), 1)
                    if c == q["groups"] // q["gpc"] - 1:
                        for h in range(2):
                            tally.n["rt_done", h] += 1

                def add(h, o, x, y, name="res_ready"):
                    pool.tensor_tensor(o, x, y, ALU.add).then_inc(sem(name, h), 1)

                def mlp_residual(h, a):
                    pool.tensor_tensor(Y[h], Y[h], XB[h], ALU.add).then_inc(sem("pool_chain", h), 1)
                    chain[h] += 1
                    pool.wait_ge(sem("pool_chain", h), chain[h])
                    add(h, Y[h], Y[h], bv(f"L1_xattn_{a}_li3_b"))

                if final:
                    for h in range(2):
                        rstd(h, X5)
                    return
                for h in range(2):
                    rstd(h)
                for h in range(2):
                    rstd(h, X5)
                for h in range(2):
                    rstd(h)
                for h in range(2):
                    add(h, XB[h], XN[h], bv("L0_xattn_bo"))
                attention("L0")
                for h in range(2):
                    rstd(h)
                for h in range(2):
                    rstd(h, twice=True)
                    rstd(h)
                for h in range(2):
                    add(h, XB[h], Y[h], bv("L1_xattn_a1_li1_b"))
                attention("a1")
                for h in range(2):
                    rstd(h)
                    mlp_residual(h, "a1")
                for h in range(2):
                    rstd(h)
                    rstd(h)
                for h in range(2):
                    add(h, XB[h], Y[h], bv("L1_xattn_a2_li1_b"))
                attention("a2")
                for h in range(2):
                    rstd(h)
                    mlp_residual(h, "a2")

            @block.vector
            def _(dve):
                tally = Tally(sems)
                chain = [0, 0]

                def step(h, ins_):
                    ins_.then_inc(sem("dve_chain", h), 1)
                    chain[h] += 1
                    dve.wait_ge(sem("dve_chain", h), chain[h])

                def stats(h, src, rows=P, tiles=T, o=0):
                    for t in range(tiles):
                        ins_ = dve.bn_stats(small[h][0:rows, o + ST + 6 * t:o + ST + 6 * t + 6], src[0:rows, t, :])
                    step(h, ins_)
                    for t in range(tiles):
                        ins_ = dve.bn_aggr(small[h][0:rows, o + MV + 2 * t:o + MV + 2 * t + 2],
                                           small[h][0:rows, o + ST + 6 * t:o + ST + 6 * t + 6])
                    ins_.then_inc(sem("var_ready", h), 1)

                def apply(h, dst, src, rows=P, tiles=T, o=0):
                    tally.wait(dve, "rstd_ready", h)
                    for t in range(tiles):
                        ins_ = dve.tensor_scalar(dst[0:rows, t, :], src[0:rows, t, :],
                                                 small[h][0:rows, o + MV + 2 * t:o + MV + 2 * t + 1],
                                                 small[h][0:rows, o + RSTD + t:o + RSTD + t + 1], ALU.subtract, ALU.mult)
                    return ins_

                def logits(h):
                    tally.wait(dve, "logits_done", h)
                    lg = sm(h, LG, 2 * E).rearrange("p (t e) -> p t e", t=T)
                    dve.tensor_tensor(lg, bank(h, 2)[:, 0:2 * E].rearrange("p (t e) -> p t e", t=T),
                                      bgt[:].rearrange("p (o e) -> p o e", o=1).to_broadcast([P, T, E]), ALU.add
                                      ).then_inc(sem("lg_ready", h), 1)

                def choose(h, at):
                    dve.wait_ge(sem("lg_ready", h), 1)
                    lg = sm(h, LG, 2 * E).rearrange("p (t e) -> p t e", t=T)
                    eq = sm(h, EQ, 2 * E).rearrange("p (t e) -> p t e", t=T)
                    step(h, dve.tensor_reduce(sm(h, MX, T), lg, AX.X, ALU.max))
                    step(h, dve.tensor_tensor(eq, lg, sm(h, MX, T).rearrange("p (t o) -> p t o", o=1).to_broadcast([P, T, E]),
                                              ALU.is_lt))
                    eb = eidx[:].rearrange("p (o e) -> p o e", o=1).to_broadcast([P, T, E])
                    step(h, dve.scalar_tensor_tensor(lg, eq, float(E), eb, ALU.mult, ALU.add))
                    step(h, dve.tensor_reduce(sm(h, IDX, T), lg, AX.X, ALU.min))
                    dve.tensor_tensor(at, eb, sm(h, IDX, T).rearrange("p (t o) -> p t o", o=1).to_broadcast([P, T, E]),
                                      ALU.is_equal)

                def gain(h, g, b):
                    step(h, dve.tensor_tensor(Y[h], XH[h], bv(g), ALU.mult))
                    step(h, dve.tensor_tensor(Y[h], Y[h], bv(b), ALU.add))

                def quant_scales(h, src, t0, n):
                    step(h, dve.tensor_reduce(sm(h, AM + t0, n), src, AX.X, ALU.max, apply_absolute_value=True))
                    step(h, dve.tensor_scalar(sm(h, AM + t0, n), sm(h, AM + t0, n), EPS, None, ALU.max))
                    step(h, dve.reciprocal(sm(h, RS + t0, n), sm(h, AM + t0, n)))
                    dve.tensor_scalar(sm(h, SU + t0, n), sm(h, AM + t0, n), 1.0 / 127.0, None, ALU.mult)
                    step(h, dve.tensor_scalar(sm(h, SC + t0, n), sm(h, RS + t0, n), 127.0, None, ALU.mult))

                def attention(a):
                    q = ATT[a]
                    nh, nk, d, hc, gpc, ng = q["nh"], q["nk"], q["d"], q["hc"], q["gpc"], q["groups"]
                    units = 2 * ng

                    def row_max(h, u):
                        tally.wait(dve, "s_done", h)
                        dve.tensor_reduce(sm(h, NMX + u * nh, nh),
                                          bank(h, u % 2)[:, 0:nh * nk].rearrange("p (j k) -> p j k", j=nh),
                                          AX.X, ALU.max, negate=True).then_inc(sem("max_done", h), 1)

                    def evacuate(h, u):
                        g, t = divmod(u, 2)
                        tally.wait(dve, "t_done", h)
                        if t == 0 and g >= 2:
                            tally.wait(dve, "pv_done", h)
                        if a == "a1":
                            pt = PT[h][:, g % 2, :].rearrange("p (c j s) -> p c j s", c=2, j=nh)
                            msk = later[:].rearrange("p (o s) -> p o s", o=1).to_broadcast([P, nh, P])
                            if t == 0:
                                src = bank(h, 2).rearrange("p (c j s) -> p c j s", c=2, j=nh)
                                dve.tensor_tensor(pt[:, 0, :, 0:P], src[:, 0], msk, ALU.mult)
                                ins_ = dve.tensor_copy(pt[:, 1, :, 0:P], src[:, 1])
                            else:
                                src = bank(h, 2)[:, 0:nh * P].rearrange("p (j s) -> p j s", j=nh)
                                ins_ = dve.tensor_tensor(pt[:, 1, :, P:S], src, msk, ALU.mult)
                        else:
                            pt = PT[h][0:KV, g % 2, :].rearrange("p (j s) -> p j s", j=nh)
                            ins_ = dve.tensor_copy(pt[:, :, t * P:(t + 1) * P],
                                                   bank(h, 2)[0:KV].rearrange("p (j s) -> p j s", j=nh))
                        ins_.then_inc(sem("pt_ready", h), 1)

                    def recip(h, c):
                        tally.wait(dve, "exp_done", h, 2 * gpc)
                        sums = sm(h, SUMS, 2 * HEADS).rearrange("p (t j) -> p t j", t=T)[:, :, c * hc:(c + 1) * hc]
                        rec = sm(h, REC, 2 * HEADS).rearrange("p (t j) -> p t j", t=T)[:, :, c * hc:(c + 1) * hc]
                        dve.reciprocal(rec, sums).then_inc(sem("rec_ready", h), 1)

                    def normalise(h, c):
                        tally.wait(dve, "rts_ready", h)
                        dve.tensor_tensor(OT[h][:, c, :], bank(h, 3)[:, (c % 2) * S:(c % 2) * S + S], RTS[h], ALU.mult
                                          ).then_inc(sem("oT_ready", h), 1)

                    for u in range(units + 3):
                        for h in range(2):
                            v = u - 3
                            if v >= 0 and v % (2 * gpc) == 2 * gpc - 1:
                                normalise(h, v // (2 * gpc))
                            if u < units:
                                row_max(h, u)
                            if 1 <= u <= units:
                                evacuate(h, u - 1)
                            v = u - 1
                            if 0 <= v < units and v % (2 * gpc) == 2 * gpc - 1:
                                recip(h, v // (2 * gpc))
                    for h in range(2):
                        tally.n["pv_done", h] += 2

                def mlp(a, dst_residual):
                    for h in range(2):
                        tally.wait(dve, "out_done", h)
                        tally.wait(dve, "res_ready", h)
                        step(h, dve.tensor_tensor(XB[h], bank(h, 0).rearrange("p (t n) -> p t n", t=T), XB[h], ALU.add))
                        stats(h, XB[h])
                        apply(h, XH[h], XB[h]).then_inc(sem("xhat_ready", h), 1)
                    for h in range(2):
                        tally.wait(dve, "out_done", h)
                        tally.wait(dve, "res_ready", h)
                        step(h, dve.tensor_tensor(Y[h], bank(h, 0, 2)[:, :, 0:D], Y[h], ALU.add))
                        dst_residual(h)

                def x5_norm(h):
                    apply(h, Y[h], X[h], o=X5).then_inc(sem("x5hat_ready", h), 1)

                if final:
                    for h in range(2):
                        stats(h, X[h], o=X5)
                    for h in range(2):
                        x5_norm(h)
                    for h in range(2):
                        logits(h)
                        choose(h, onehot_all[:, TILES + h * T:TILES + (h + 1) * T, :])
                    return
                for h in range(2):
                    stats(h, XN[h])
                for h in range(2):
                    apply(h, XH[h], XN[h]).then_inc(sem("xhat_ready", h), 1)
                    stats(h, X[h], o=X5)
                for h in range(2):
                    x5_norm(h)
                one = "p (t n) -> p t n"
                for h in range(2):
                    stats(h, CT[h].rearrange(one, t=1), KV, 1)
                for h in range(2):
                    apply(h, CH[h].rearrange(one, t=1), CT[h].rearrange(one, t=1), KV, 1).then_inc(sem("cxhat_ready", h), 1)
                for h in range(2):
                    tally.wait(dve, "ctx_proj_done", h)
                    for par in range(2):
                        ins_ = dve.tensor_tensor(VM[h][0:KV, :, par, par * D0:(par + 1) * D0],
                                          bank(h, 1)[0:KV, 256:512].rearrange("p (a b d) -> p a b d", b=2, d=D0)[:, :, par, :],
                                          bvec[0:KV, BC.index("L0_xattn_bv"), :].rearrange("p (a b d) -> p a b d", b=2, d=D0)[:, :, par, :],
                                          ALU.add)
                    ins_.then_inc(sem("v_ready", h), 1)
                for h in range(2):
                    tally.wait(dve, "q_done", h)
                    for m in range(KC):
                        ins_ = dve.tensor_scalar(QT[h][:, m, :], bank(h, 3)[:, m * S:(m + 1) * S], pv("L0_xattn_bq", m),
                                                 D0 ** -0.5, ALU.add, ALU.mult)
                    ins_.then_inc(sem("qT_ready", h), 1)
                attention("L0")

                for h in range(2):
                    tally.wait(dve, "out_done", h)
                    tally.wait(dve, "res_ready", h)
                    dve.wait_ge(sem("x5_stored", h), 16)
                    step(h, dve.tensor_tensor(X[h], bank(h, 0).rearrange("p (t n) -> p t n", t=T), XB[h], ALU.add))
                    stats(h, X[h])
                    step(h, apply(h, XH[h], X[h]))
                    quant_scales(h, XH[h], 0, T)
                    dve.tensor_scalar(sm(h, SGT, T), sm(h, SU, T), mean_w[:, 0:1], None, ALU.mult)
                    dve.tensor_scalar(sm(h, SUT, T), sm(h, SU, T), mean_w[:, 1:2], None, ALU.mult)
                    for t in range(T):
                        ins_ = dve.tensor_scalar(XH[h][:, t, :], XH[h][:, t, :], sm(h, SC + t, 1), MAGIC, ALU.mult, ALU.add)
                    step(h, ins_)
                    dve.tensor_scalar(N1[h], XH[h], -MAGIC, 127.0, ALU.add, ALU.min).then_inc(sem("xhat_ready", h), 1)
                for h in range(2):
                    logits(h)
                def gated(k):
                    for h in range(2):
                        t, j = divmod(k, 2)
                        tally.wait(dve, "silu_done", h)
                        dve.scalar_tensor_tensor(HH[h][:, t, j * 512:(j + 1) * 512], bank(h, 2 * (k % 2) + 1),
                                                 sm(h, SUT + t, 1), SG[h][:, k % 2, :], ALU.mult, ALU.mult
                                                 ).then_inc(sem("hh_done", h), 1)

                def quantise(t):
                    for h in range(2):
                        tally.wait(dve, "hh_done", h, 2)
                        quant_scales(h, HH[h][:, t, :], t, 1)
                        dve.tensor_scalar(sm(h, SD + t, 1), sm(h, SU + t, 1), mean_w[:, 2:3], None, ALU.mult)
                        step(h, dve.tensor_scalar(HH[h][:, t, :], HH[h][:, t, :], sm(h, SC + t, 1), MAGIC, ALU.mult, ALU.add))
                        dve.tensor_scalar(N2[h][:, t, :], HH[h][:, t, :], -MAGIC, 127.0, ALU.add, ALU.min
                                          ).then_inc(sem("n2_ready", h), 1)

                for t in range(T):
                    gated(2 * t)
                    gated(2 * t + 1)
                    quantise(t)
                for h in range(2):
                    choose(h, onehot_all[:, bass.ds(it * 4 + h * 2, T), :])
                for h in range(2):
                    tally.wait(dve, "out_done", h)
                    for t in range(T):
                        ins_ = dve.scalar_tensor_tensor(X[h][:, t, :], bank(h, 2)[:, t * D:(t + 1) * D], sm(h, SD + t, 1),
                                                        X[h][:, t, :], ALU.mult, ALU.add)
                    step(h, ins_)
                    stats(h, X[h])
                    step(h, apply(h, XH[h], X[h]))
                    gain(h, "L1_xattn_ln1_g", "L1_xattn_ln1_b")
                    stats(h, Y[h])
                    apply(h, XH[h], Y[h]).then_inc(sem("xhat_ready", h), 1)
                for h in range(2):
                    tally.wait(dve, "q_done", h)
                    dve.tensor_scalar(QT[h].rearrange("p a s -> p (a s)").rearrange("p (a s) -> p a s", a=2), bank(h, 0, 2),
                                      D1 ** -0.5, None, ALU.mult).then_inc(sem("qT_ready", h), 1)
                attention("a1")

                def after_a1(h):
                    stats(h, Y[h])
                    step(h, apply(h, XH[h], Y[h]))
                    gain(h, "L1_xattn_ln2_g", "L1_xattn_ln2_b")
                    stats(h, Y[h])
                    apply(h, XH[h], Y[h]).then_inc(sem("xhat_ready", h), 1)
                mlp("a1", after_a1)
                for h in range(2):
                    tally.wait(dve, "q_done", h)
                    dve.tensor_scalar(QT[h].rearrange("p a s -> p (a s)").rearrange("p (a s) -> p a s", a=2), bank(h, 0, 2),
                                      D1 ** -0.5, None, ALU.mult).then_inc(sem("qT_ready", h), 1)
                attention("a2")

                def after_a2(h):
                    dve.tensor_tensor(X[h], X[h], Y[h], ALU.add)
                mlp("a2", after_a2)

            @block.scalar
            def _(act):
                tally = Tally(sems)

                def attention(a):
                    q = ATT[a]
                    nh, nk, hc, gpc, ng = q["nh"], q["nk"], q["hc"], q["gpc"], q["groups"]
                    units = 2 * ng
                    for u in range(units + 3):
                        for h in range(2):
                            if u < units:
                                g, t = divmod(u, 2)
                                tally.wait(act, "max_done", h)
                                if u >= 2:
                                    tally.wait(act, "t_done", h)
                                for j in range(nh):
                                    head = t * HEADS + g * nh + j
                                    ins_ = act.activation(PR[h][:, u % 2, j * nk:(j + 1) * nk],
                                                          bank(h, u % 2)[:, j * nk:(j + 1) * nk], ACT.Exp,
                                                          bias=sm(h, NMX + u * nh + j, 1), scale=1.0,
                                                          accum_out=sm(h, SUMS + head, 1))
                                ins_.then_inc(sem("exp_done", h), 1)
                            v = u - 2
                            if v >= 0 and v % (2 * gpc) == 2 * gpc - 1:
                                c = v // (2 * gpc)
                                tally.wait(act, "rt_done", h)
                                if c >= 1:
                                    tally.wait(act, "oT_ready", h)
                                act.activation(RTS[h], bank(h, 3)[:, ((c + 1) % 2) * S:((c + 1) % 2) * S + S], ACT.Copy
                                               ).then_inc(sem("rts_ready", h), 1)
                    for h in range(2):
                        tally.n["t_done", h] += 2
                        tally.n["oT_ready", h] += 1

                def transposed(h, dst, g, b):
                    for m in range(KC):
                        ins_ = act.activation(dst[h][:, m, :], bank(h, 3)[:, m * S:(m + 1) * S], ACT.Identity,
                                              bias=pv(b, m), scale=pv(g, m))
                    return ins_

                def mlp(a):
                    def inputs(h):
                        tally.wait(act, "xhatT_done", h)
                        transposed(h, FT, f"L1_xattn_{a}_ln3_g", f"L1_xattn_{a}_ln3_b").then_inc(sem("featT_ready", h), 1)

                    def gelu(h, banks):
                        for k in banks:
                            tally.wait(act, "h_done", h)
                            for m in (2 * k, 2 * k + 1):
                                ins_ = act.activation(HT[h][:, m, :], bank(h, k)[:, (m % 2) * S:(m % 2) * S + S], ACT.Gelu,
                                                      bias=pv(f"L1_xattn_{a}_li2_b", m), scale=1.0)
                            ins_.then_inc(sem("gelu_done", h), 1)

                    inputs(0)
                    gelu(0, (0, 1))
                    inputs(1)
                    gelu(0, (2, 3))
                    gelu(1, (0, 1, 2, 3))

                def x5T(h):
                    tally.wait(act, "x5T_done", h)
                    act.activation(FT5[h].rearrange("p a s -> p (a s)"), bank(h, 2), ACT.Copy).then_inc(sem("x5T_ready", h), 1)

                if final:
                    for h in range(2):
                        x5T(h)
                    return
                for h in range(2):
                    tally.wait(act, "cT_done", h)
                    act.activation(CTT[h], bank(h, 1)[:, 0:KV], ACT.Copy).then_inc(sem("cT_ready", h), 1)
                for h in range(2):
                    tally.wait(act, "ctx_proj_done", h)
                    for m in range(2):
                        ins_ = act.activation(KT0[h][:, m, :], bank(h, 0)[:, m * KV:(m + 1) * KV], ACT.Identity,
                                              bias=pv("L0_xattn_bk", m), scale=1.0)
                    ins_.then_inc(sem("kT_ready", h), 1)
                for h in range(2):
                    tally.wait(act, "xhatT_done", h)
                    act.activation(FT[h].rearrange("p a s -> p (a s)"), bank(h, 3), ACT.Copy).then_inc(sem("featT_ready", h), 1)
                for h in range(2):
                    x5T(h)
                attention("L0")
                for h in range(2):
                    tally.wait(act, "xhatT_done", h)
                    act.activation(N1T[h].rearrange("p a s -> p (a s)"), bank(h, 3).bitcast(BF16)[:, 0:512], ACT.Copy
                                   ).then_inc(sem("featT_ready", h), 1)
                for k in range(4):
                    for h in range(2):
                        tally.wait(act, "gu_done", h)
                        if k >= 2:
                            tally.wait(act, "hh_done", h)
                        act.activation(SG[h][:, k % 2, :], bank(h, 2 * (k % 2)), ACT.Silu,
                                       scale=sm(h, SGT + k // 2, 1)).then_inc(sem("silu_done", h), 1)
                for h in range(2):
                    tally.n["hh_done", h] += 2
                for h in range(2):
                    tally.wait(act, "cT_done", h)
                    act.activation(CYT[h], bank(h, 2)[:, 0:KV], ACT.Identity, bias=pv("L1_xattn_a2_lny_b", 0),
                                   scale=pv("L1_xattn_a2_lny_g", 0)).then_inc(sem("cT_ready", h), 1)

                def context1(h):
                    tally.wait(act, "ctx_proj_done", h)
                    act.activation(V2[h][0:KV, :], bank(h, 2)[0:KV], ACT.Copy)
                    act.activation(KT2[h].rearrange("p a k -> p (a k)"), bank(h, 3)[:, 0:4 * KV], ACT.Copy
                                   ).then_inc(sem("kT_ready", h), 1)

                context1(0)
                for t in range(T):
                    for h in range(2):
                        tally.wait(act, "n2T_done", h)
                        act.activation(N2T[h][:, :, t * P:(t + 1) * P],
                                       bank(h, t).bitcast(BF16).rearrange("p (c s) -> p c s", c=HC), ACT.Copy
                                       ).then_inc(sem("n2T_ready", h), 1)
                    if t == 0:
                        context1(1)
                for h in range(2):
                    tally.wait(act, "xhatT_done", h)
                    transposed(h, FT, "L1_xattn_a1_lnx_g", "L1_xattn_a1_lnx_b")
                    transposed(h, FT2, "L1_xattn_a1_lny_g", "L1_xattn_a1_lny_b").then_inc(sem("featT_ready", h), 1)
                for h in range(2):
                    tally.wait(act, "kv_done", h)
                    act.activation(KT[h].rearrange("p a s -> p (a s)").rearrange("p (a s) -> p a s", a=2), bank(h, 2, 2),
                                   ACT.Copy).then_inc(sem("kT_ready", h), 1)
                for h in range(2):
                    tally.wait(act, "kv_done", h)
                    act.activation(V1[h], bank(h, 0, 2), ACT.Copy).then_inc(sem("v_ready", h), 1)
                attention("a1")
                mlp("a1")
                for h in range(2):
                    tally.wait(act, "xhatT_done", h)
                    transposed(h, FT, "L1_xattn_a2_lnx_g", "L1_xattn_a2_lnx_b").then_inc(sem("featT_ready", h), 1)
                attention("a2")
                mlp("a2")

            @block.tensor
            def _(pe):
                tally = Tally(sems)

                def transpose_x(h):
                    tally.wait(pe, "xhat_ready", h)
                    for m in range(KC):
                        for t in range(T):
                            ins_ = pe.transpose(bank(h, 3)[:, m * S + t * P:m * S + (t + 1) * P],
                                                XH[h][:, t, m * P:(m + 1) * P], ident[:])
                    ins_.then_inc(sem("xhatT_done", h), 1)

                def feature_major(outs, w, x, kc=KC):
                    for m, o in enumerate(outs):
                        for c in range(kc):
                            ins_ = pe.matmul(o, w[:, c, m * P:(m + 1) * P], x[:, c, :], start=(c == 0), stop=(c == kc - 1))
                    return ins_

                def attention(a, queries_waited=False):
                    q = ATT[a]
                    nh, nk, d, hc, gpc, ng = q["nh"], q["nk"], q["d"], q["hc"], q["gpc"], q["groups"]
                    units = 2 * ng

                    def scores(h, u):
                        g, t = divmod(u, 2)
                        if u == 0 and not queries_waited:
                            tally.wait(pe, "qT_ready", h)
                        if t == 0:
                            tally.wait(pe, "km_ready", h)
                        pe.matmul(bank(h, u % 2)[:, 0:nh * nk], QT[h][:, g // gpc, t * P:(t + 1) * P],
                                  KM[h][:, g % 2, 0:nh * nk], start=True, stop=True).then_inc(sem("s_done", h), 1)

                    def transpose_p(h, u):
                        g, t = divmod(u, 2)
                        tally.wait(pe, "exp_done", h)
                        if u >= 1:
                            tally.wait(pe, "pt_ready", h)
                        p = PR[h][:, u % 2, :]
                        if a == "a1":
                            blocks = [(c, j) for c in range(t, 2) for j in range(nh)]
                        else:
                            blocks = [(0, j) for j in range(nh)]
                        for n, (c, j) in enumerate(blocks):
                            kk = min(nk, P)
                            ins_ = pe.transpose(bank(h, 2)[0:kk, n * P:(n + 1) * P],
                                                p[:, j * nk + c * P:j * nk + c * P + kk], ident[:])
                        ins_.then_inc(sem("t_done", h), 1)

                    def values(h, g):
                        dve_seen = tally.n["pt_ready", h]
                        need = base[h] + 2 * g + 2
                        if need > dve_seen:
                            tally.wait(pe, "pt_ready", h, need - dve_seen)
                        c = g // gpc
                        if g % gpc == 0 and c >= 1:
                            tally.wait(pe, "oT_ready", h)
                        o = bank(h, 3)[:, (c % 2) * S:(c % 2) * S + S]
                        if a == "a1":
                            pt = PT[h][:, g % 2, :].rearrange("p (c j s) -> p c j s", c=2, j=nh)
                            for c2, n in ((1, S), (0, P)):
                                for j in range(nh):
                                    strip = 32 * ((g % 2) * nh + j)
                                    hd = (g * nh + j) * D1
                                    ins_ = pe.matmul(o[strip:strip + 32, 0:n], V1[h][:, c2, hd:hd + D1], pt[:, c2, j, 0:n],
                                                     start=(c2 == 1), stop=(c2 == 0), tile_position=(0, strip))
                        else:
                            pt = PT[h][0:KV, g % 2, :].rearrange("p (j s) -> p j s", j=nh)
                            order = (0, 2, 1, 3) if a == "L0" else range(nh)
                            for j in order:
                                head = g * nh + j
                                if a == "L0":
                                    strip = 32 * ((head // 2) % 4)
                                    ins_ = pe.matmul(o[strip:strip + 32, :], VM[h][0:KV, head // 2, head % 2, :], pt[:, j, :],
                                                     start=(head % 2 == 0), stop=(head % 2 == 1), tile_position=(0, strip))
                                else:
                                    strip = 32 * j
                                    ins_ = pe.matmul(o[strip:strip + 32, :], V2[h][0:KV, head * D1:(head + 1) * D1], pt[:, j, :],
                                                     start=True, stop=True, tile_position=(0, strip))
                        ins_.then_inc(sem("pv_done", h), 1)
                        if g % gpc == gpc - 1:
                            tally.wait(pe, "rbc_ready", h)
                            for t in range(T):
                                at = ((c + 1) % 2) * S + t * P
                                ins_ = pe.transpose(bank(h, 3)[:, at:at + P], RBC[h][:, t, :], ident[:])
                            ins_.then_inc(sem("rt_done", h), 1)

                    base = [tally.n["pt_ready", h] for h in range(2)]
                    for u in range(units + 3):
                        for h in range(2):
                            if u < units:
                                scores(h, u)
                            if 1 <= u <= units:
                                transpose_p(h, u - 1)
                            v = u - 2
                            if 0 <= v < units and v % 2 == 1:
                                values(h, v // 2)
                def output(h, w, chunks):
                    tally.wait(pe, "oT_ready", h)
                    for t in range(T):
                        for c in range(chunks):
                            ins_ = pe.matmul(bank(h, 0)[:, t * D:(t + 1) * D], OT[h][:, c, t * P:(t + 1) * P], w[:, c, :],
                                             start=(c == 0), stop=(c == chunks - 1))
                    ins_.then_inc(sem("out_done", h), 1)

                def mlp(a):
                    w = w1[a]

                    def up(h, banks):
                        if 0 in banks:
                            tally.wait(pe, "featT_ready", h)
                        for k in banks:
                            for m in (2 * k, 2 * k + 1):
                                for c in range(KC):
                                    ins_ = pe.matmul(bank(h, k)[:, (m % 2) * S:(m % 2) * S + S], w["li2"][:, c, m * P:(m + 1) * P],
                                                     FT[h][:, c, :], start=(c == 0), stop=(c == KC - 1))
                            ins_.then_inc(sem("h_done", h), 1)

                    transpose_x(0)
                    up(0, (0, 1))
                    transpose_x(1)
                    up(0, (2, 3))
                    up(1, (0, 1, 2, 3))
                    for h in range(2):
                        tally.wait(pe, "gelu_done", h, 2)
                        for c in range(HC):
                            if c in (4, 6):
                                tally.wait(pe, "gelu_done", h)
                            for t in range(T):
                                ins_ = pe.matmul(bank(h, t)[:, 0:D], HT[h][:, c, t * P:(t + 1) * P], w["li3"][:, c, :],
                                                 start=(c == 0), stop=(c == HC - 1))
                        ins_.then_inc(sem("out_done", h), 1)

                def x5_transposes(h):
                    tally.wait(pe, "x5hat_ready", h)
                    for m in range(KC):
                        for t in range(T):
                            ins_ = pe.transpose(bank(h, 2)[:, m * S + t * P:m * S + (t + 1) * P],
                                                Y[h][:, t, m * P:(m + 1) * P], ident[:])
                    ins_.then_inc(sem("x5T_done", h), 1)

                def x5_logits(h):
                    for t in range(T):
                        for c in range(KC):
                            ins_ = pe.matmul(bank(h, 2)[:, t * E:(t + 1) * E], FT5[h][:, c, t * P:(t + 1) * P], wg_moe[:, c, :],
                                             start=(c == 0), stop=(c == KC - 1))
                    ins_.then_inc(sem("logits_done", h), 1)

                if final:
                    for h in range(2):
                        x5_transposes(h)
                    for h in range(2):
                        tally.wait(pe, "x5T_ready", h)
                        x5_logits(h)
                    return
                for h in range(2):
                    pe.transpose(bank(h, 1)[:, 0:KV], CT[h][0:KV, :], ident[0:KV, 0:KV]).then_inc(sem("cT_done", h), 1)
                for h in range(2):
                    tally.wait(pe, "cT_ready", h)
                    for m in range(2):
                        pe.matmul(bank(h, 0)[:, m * KV:(m + 1) * KV], wk0[:, m * P:(m + 1) * P], CTT[h], start=True, stop=True)
                    pe.matmul(bank(h, 1)[0:KV, 256:512], CTT[h], wv0[:], start=True, stop=True
                              ).then_inc(sem("ctx_proj_done", h), 1)
                for h in range(2):
                    transpose_x(h)
                for h in range(2):
                    tally.wait(pe, "featT_ready", h)
                    feature_major([bank(h, 3)[:, m * S:(m + 1) * S] for m in range(2)], wq0, FT[h]
                                  ).then_inc(sem("q_done", h), 1)
                for h in range(2):
                    x5_transposes(h)
                for h in range(2):
                    tally.wait(pe, "x5T_ready", h)
                    tally.wait(pe, "kT_ready", h)
                    tally.wait(pe, "v_ready", h)
                attention("L0")
                for h in range(2):
                    output(h, wo0, KC)
                for h in range(2):
                    x5_logits(h)
                for h in range(2):
                    tally.wait(pe, "xhat_ready", h)
                    n1t = bank(h, 3).bitcast(BF16)
                    for m in range(KC):
                        for t in range(T):
                            ins_ = pe.transpose(n1t[:, m * S + t * P:m * S + (t + 1) * P], N1[h][:, t, m * P:(m + 1) * P], identb[:])
                    ins_.then_inc(sem("xhatT_done", h), 1)
                for k in range(4):
                    for h in range(2):
                        t, j = divmod(k, 2)
                        if k == 0:
                            tally.wait(pe, "featT_ready", h)
                        if k == 1:
                            tally.wait(pe, "lg_ready", h)
                        if k >= 2:
                            tally.wait(pe, "hh_done", h)
                        for n, w in enumerate((wgT, wuT)):
                            for c in range(KC):
                                ins_ = pe.matmul(bank(h, 2 * (k % 2) + n), N1T[h][:, c, t * P:(t + 1) * P],
                                                 w[:, c, j * 512:(j + 1) * 512], start=(c == 0), stop=(c == KC - 1))
                        ins_.then_inc(sem("gu_done", h), 1)
                def context1(h):
                    tally.wait(pe, "cT_ready", h)
                    for m in range(4):
                        pe.matmul(bank(h, 3)[:, m * KV:(m + 1) * KV], w1["a2"]["wk"][:, 0, m * P:(m + 1) * P], CYT[h],
                                  start=True, stop=True)
                    pe.matmul(bank(h, 2)[0:KV, :], CYT[h], w1["a2"]["wv"][:, 0, :], start=True, stop=True
                              ).then_inc(sem("ctx_proj_done", h), 1)

                pe.wait_ge(w1_load, 16 * W1_LOADS)
                for h in range(2):
                    tally.wait(pe, "cxhat_ready", h)
                    tally.wait(pe, "hh_done", h, 2)
                    pe.transpose(bank(h, 2)[:, 0:KV], CH[h][0:KV, :], ident[0:KV, 0:KV]).then_inc(sem("cT_done", h), 1)
                context1(0)
                for t in range(T):
                    for h in range(2):
                        tally.wait(pe, "n2_ready", h)
                        n2t = bank(h, t).bitcast(BF16)
                        for c in range(HC):
                            ins_ = pe.transpose(n2t[:, c * P:(c + 1) * P], N2[h][:, t, c * P:(c + 1) * P], identb[:])
                        ins_.then_inc(sem("n2T_done", h), 1)
                    if t == 0:
                        context1(1)
                for h in range(2):
                    tally.wait(pe, "kT_ready", h)
                    for t in range(T):
                        tally.wait(pe, "n2T_ready", h)
                        for c in range(HC):
                            ins_ = pe.matmul(bank(h, 2)[:, t * D:(t + 1) * D], N2T[h][:, c, t * P:(t + 1) * P], wdT[:, c, :],
                                             start=(c == 0), stop=(c == HC - 1))
                    ins_.then_inc(sem("out_done", h), 1)
                w = w1["a1"]
                halves = [[bank(h, b)[:, k * S:(k + 1) * S] for b in range(4) for k in range(2)] for h in range(2)]

                def queries(h):
                    tally.wait(pe, "featT_ready", h)
                    feature_major(halves[h][0:4], w["wq"], FT[h]).then_inc(sem("q_done", h), 1)

                def keys(h):
                    feature_major(halves[h][4:8], w["wk"], FT2[h]).then_inc(sem("kv_done", h), 1)

                transpose_x(0)
                queries(0)
                transpose_x(1)
                keys(0)
                queries(1)
                keys(1)
                for h in range(2):
                    tally.wait(pe, "qT_ready", h)
                    for t in range(T):
                        for c in range(KC):
                            ins_ = pe.matmul(bank(h, t), FT2[h][:, c, t * P:(t + 1) * P], w["wv"][:, c, :],
                                             start=(c == 0), stop=(c == KC - 1))
                    ins_.then_inc(sem("kv_done", h), 1)
                for h in range(2):
                    tally.wait(pe, "v_ready", h)
                attention("a1", queries_waited=True)
                for h in range(2):
                    output(h, w["li1"], HD // P)
                mlp("a1")
                w = w1["a2"]

                def two(h, m0):
                    for m in (m0, m0 + 1):
                        for c in range(KC):
                            ins_ = pe.matmul(halves[h][m], w["wq"][:, c, m * P:(m + 1) * P], FT[h][:, c, :],
                                             start=(c == 0), stop=(c == KC - 1))
                    return ins_

                transpose_x(0)
                tally.wait(pe, "featT_ready", 0)
                two(0, 0)
                transpose_x(1)
                two(0, 2).then_inc(sem("q_done", 0), 1)
                tally.wait(pe, "featT_ready", 1)
                two(1, 0)
                two(1, 2).then_inc(sem("q_done", 1), 1)
                attention("a2")
                for h in range(2):
                    output(h, w["li1"], HD // P)
                mlp("a2")

        rows = arena[0][:, 8704:8704 + TILES * ROW].rearrange("p (t n) -> p t n", t=TILES)
        rt = arena[1]
        n_at = [0]

        def alloc(words):
            n_at[0] += words
            return rt[:, n_at[0] - words:n_at[0]]

        tot = [alloc(TILES * E).rearrange("p (t e) -> p t e", e=E) for _ in range(6)]
        seven = [alloc(E) for _ in range(6)]
        pos = alloc(TILES)
        posi = alloc(TILES).bitcast(I32)
        unit_no = alloc(UNITS * E).rearrange("p (u e) -> p u e", e=E)
        below = alloc(UNITS * E).rearrange("p (u e) -> p u e", e=E)
        unit_e = alloc(UNITS)
        unit_ei = sb("unit_ei", [P, UNITS], I32)
        x5_loaded = ctx.enter_context(nc.semaphore("x5_loaded"))
        ids_ready = ctx.enter_context(nc.semaphore("ids_ready"))
        counts_done = ctx.enter_context(nc.semaphore("counts_done"))
        route_chain = ctx.enter_context(nc.semaphore("route_chain"))
        slots_ready = ctx.enter_context(nc.semaphore("slots_ready"))
        rows_sent = ctx.enter_context(nc.semaphore("rows_sent"))

        with nc.Fori(0, B // 2) as it:
            with nc.Block() as block:
                layers(block, it)
            nc.all_engine_barrier(sems_to_clear=sem_range)

        with nc.Block() as block:
            layers(block, None, final=True)
        nc.all_engine_barrier(sem_only=True)

        with nc.Block() as block:
            @block.tensor
            def _(pe):
                oh = onehot[:].rearrange("p t e -> p (t e)")
                pe.matmul(ps[:, 0, 0:TILES * E], strict[:], oh, start=True, stop=True)
                pe.matmul(ps[:, 1, 0:TILES * E], onesb[:], oh, start=True, stop=True).then_inc(counts_done, 1)

            @block.vector
            def _(dve):
                n = [0]

                def step(ins_):
                    ins_.then_inc(route_chain, 1)
                    n[0] += 1
                    dve.wait_ge(route_chain, n[0])

                dve.wait_ge(counts_done, 1)
                flat = "p (t e) -> p t e"
                step(dve.tensor_copy(tot[0], ps[:, 1, 0:TILES * E].rearrange(flat, e=E)))
                cur = 0
                for k, sh in enumerate((1, 2, 4, 8)):
                    dve.tensor_copy(tot[k + 1][:, 0:sh, :], tot[cur][:, 0:sh, :])
                    step(dve.tensor_tensor(tot[k + 1][:, sh:, :], tot[cur][:, sh:, :], tot[cur][:, :TILES - sh, :], ALU.add))
                    cur = k + 1
                incl = tot[cur]
                step(dve.tensor_scalar(seven[0], incl[:, TILES - 1, :], 1.0 / UNIT, (UNIT - 1.0) / UNIT - 0.5 + 0.25 / UNIT,
                                       ALU.mult, ALU.add))
                step(dve.tensor_scalar(seven[0], seven[0], MAGIC, None, ALU.add))
                step(dve.tensor_scalar(seven[1], seven[0], -MAGIC, None, ALU.add))
                cur = 1
                for k, sh in enumerate((1, 2, 4)):
                    dve.tensor_copy(seven[k + 2][:, 0:sh], seven[cur][:, 0:sh])
                    step(dve.tensor_tensor(seven[k + 2][:, sh:], seven[cur][:, sh:], seven[cur][:, :E - sh], ALU.add))
                    cur = k + 2
                uend = seven[cur]
                step(dve.tensor_tensor(seven[0], uend, seven[1], ALU.subtract))
                step(dve.tensor_scalar(seven[1], seven[0], float(UNIT), None, ALU.mult))
                step(dve.tensor_tensor(tot[5], incl, tot[0], ALU.subtract))
                step(dve.tensor_tensor(tot[5], tot[5], ps[:, 0, 0:TILES * E].rearrange(flat, e=E), ALU.add))
                step(dve.tensor_tensor(tot[5], tot[5], seven[1].rearrange("p (o e) -> p o e", o=1).to_broadcast([P, TILES, E]),
                                       ALU.add))
                step(dve.tensor_tensor(tot[5], tot[5], onehot[:], ALU.mult))
                step(dve.tensor_reduce(pos, tot[5], AX.X, ALU.add))
                dve.tensor_copy(posi, pos).then_inc(slots_ready, 1)
                dve.wait_ge(ids_ready, 2)
                step(dve.tensor_tensor(below, uend.rearrange("p (o e) -> p o e", o=1).to_broadcast([P, UNITS, E]), unit_no,
                                       ALU.is_le))
                step(dve.tensor_reduce(unit_e, below, AX.X, ALU.add))
                dve.tensor_scalar(unit_ei[:], unit_e, float(E - 1), None, ALU.min)

            @block.gpsimd
            def _(pool):
                pool.iota(unit_no, pattern=[[1, UNITS], [0, E]], base=0, channel_multiplier=0,
                          allow_small_or_imprecise_dtypes=True).then_inc(ids_ready, 1)
                pool.iota(rows[:, :, D:ROW], pattern=[[P, TILES]], base=0, channel_multiplier=1,
                          allow_small_or_imprecise_dtypes=True).then_inc(ids_ready, 1)
                pool.wait_ge(ids_ready, 2)
                pool.wait_ge(slots_ready, 1)
                for t in range(TILES):
                    pool.indirect_dma_start(slots_dram, bass.IndirectOffsetOnAxis(ap=posi[:, t:t + 1], axis=0),
                                            rows[:, t, :], None).then_inc(rows_sent, 16)
                pool.wait_ge(rows_sent, 16 * TILES)
        nc.all_engine_barrier(sem_only=True)

        W1B = [view(h, 0, [KC, INNER]) for h in range(2)]
        W2B = [view(h, 2048, [HC, D]) for h in range(2)]
        RB = [view(h, 4096, [T, ROW]) for h in range(2)]
        XHB = [view(h, 4624, [T, D]) for h in range(2)]
        FTB = [view(h, 5136, [KC, UNIT]) for h in range(2)]
        HTB = [view(h, 5648, [HC, UNIT]) for h in range(2)]
        ZB = [view(h, 7696, [T, D]) for h in range(2)]
        IDB = [view(h, 8208, [T]).bitcast(I32) for h in range(2)]
        out_rows = out.rearrange("b s n -> (b s) n")
        enames = ["w_loaded", "rows_loaded", "e_var_ready", "e_rstd_ready", "e_xhat_ready", "e_xhatT_done", "e_featT_ready",
                  "e_h_done", "e_gelu_done", "e_y_done", "z_ready", "z_free", "e_chain", "e_pool_chain", "scattered"]
        es = {(n, k): ctx.enter_context(nc.semaphore(f"{n}{k}")) for n in enames for k in range(2)}
        empty_ready = ctx.enter_context(nc.semaphore("empty_ready"))
        CHAIN = 1

        with nc.Block() as block:
            def wait(eng, name, k, value):
                eng.wait_ge(es[name, k], value)

            @block.sync
            def _(sp):
                def load(j, k):
                    e = sp.value_load(unit_ei[0:1, bass.ds(j, 1)] if not isinstance(j, int) else unit_ei[0:1, j:j + 1],
                                      min_val=0, max_val=E - 1)
                    sp.dma_start(RB[k], slots_dram[bass.ds(j * UNIT, UNIT), :].rearrange("(t p) n -> p t n", p=P)
                                 ).then_inc(es["rows_loaded", k], 16)
                    sp.dma_start(W1B[k], ins["L1_ffn_W1"][bass.ds(e, 1)].rearrange("o (c p) n -> p (o c) n", p=P)
                                 ).then_inc(es["w_loaded", k], 16)
                    sp.dma_start(W2B[k], ins["L1_ffn_W2"][bass.ds(e, 1)].rearrange("o (c p) n -> p (o c) n", p=P)
                                 ).then_inc(es["w_loaded", k], 16)

                load(0, 0)
                load(1, 1)
                with sp.Fori(0, UNITS // 2 - 1) as it:
                    for k in range(2):
                        wait(sp, "z_ready", k, it + 1)
                        load(it * 2 + 2 + k, k)
                wait(sp, "z_ready", 0, UNITS // 2)
                load(UNITS - 1, 0)

            @block.gpsimd
            def _(pool):
                def rstd(n, k):
                    wait(pool, "e_var_ready", k, n + 1)
                    pool.tensor_tensor(sm(k, VE, 2), sm(k, MV, 4).rearrange("p (t q) -> p t q", q=2)[:, :, 1],
                                       epst[:], ALU.add).then_inc(es["e_pool_chain", k], 1)
                    wait(pool, "e_pool_chain", k, n + 1)
                    pool.tensor_tensor(sm(k, RSTD, 2), sm(k, VE, 2), neghalf[:], ALU.pow).then_inc(es["e_rstd_ready", k], 1)

                def scatter(n, k):
                    wait(pool, "z_ready", k, n + 1)
                    pool.tensor_tensor(sm(k, IDX, 2), epst[:], epst[:], ALU.add)
                    for t in range(T):
                        pool.indirect_dma_start(out_rows, bass.IndirectOffsetOnAxis(ap=IDB[k][:, t:t + 1], axis=0),
                                                ZB[k][:, t, :], None, bounds_check=TOKENS - 1, oob_is_err=False
                                                ).then_inc(es["scattered", k], 16)

                def relay(n, k):
                    wait(pool, "scattered", k, n * 16 * T)
                    pool.sem_inc(es["z_free", k], 1)

                for k in range(2):
                    pool.memset(ZB[k], 0.0).then_inc(empty_ready, 1)
                    pool.iota(IDB[k], pattern=[[0, T]], base=PAD_ID, channel_multiplier=0).then_inc(empty_ready, 1)
                pool.wait_ge(empty_ready, 4)
                for k in range(2):
                    for t in range(T):
                        pool.indirect_dma_start(out_rows, bass.IndirectOffsetOnAxis(ap=IDB[k][:, t:t + 1], axis=0),
                                                ZB[k][:, t, :], None, bounds_check=TOKENS - 1, oob_is_err=False
                                                ).then_inc(es["scattered", k], 16)
                rstd(0, 0)
                with pool.Fori(0, UNITS // 2) as it:
                    rstd(it, 1)
                    relay(it + 1, 0)
                    scatter(it, 0)
                    rstd(it + 1, 0)
                    relay(it + 1, 1)
                    scatter(it, 1)
                relay(UNITS // 2 + 1, 0)
                scatter(UNITS // 2, 0)
                for k in range(2):
                    pool.wait_ge(es["scattered", k], 16 * T * (UNITS // 2 + 2 - k))

            @block.vector
            def _(dve):
                def link(ins_, n, k, c):
                    ins_.then_inc(es["e_chain", k], 1)
                    wait(dve, "e_chain", k, n * CHAIN + c)

                def normalise(n, k):
                    wait(dve, "rows_loaded", k, n * 16 + 16)
                    for t in range(T):
                        ins_ = dve.bn_stats(sm(k, ST + 6 * t, 6), RB[k][:, t, 0:D])
                    link(ins_, n, k, 1)
                    dve.tensor_copy(sm(k, EQ, 1), sm(k, ST, 1))
                    for t in range(T):
                        ins_ = dve.bn_aggr(sm(k, MV + 2 * t, 2), sm(k, ST + 6 * t, 6))
                    ins_.then_inc(es["e_var_ready", k], 1)
                    wait(dve, "e_rstd_ready", k, n + 1)
                    for t in range(T):
                        ins_ = dve.tensor_scalar(XHB[k][:, t, :], RB[k][:, t, 0:D], sm(k, MV + 2 * t, 1), sm(k, RSTD + t, 1),
                                                 ALU.subtract, ALU.mult)
                    ins_.then_inc(es["e_xhat_ready", k], 1)

                def feature_major(n, k):
                    wait(dve, "e_xhatT_done", k, n + 1)
                    dve.tensor_copy(FTB[k].rearrange("p c s -> p (c s)"), bank(k, 3)).then_inc(es["e_featT_ready", k], 1)

                def result(n, k):
                    wait(dve, "z_free", k, n + 1)
                    ins_ = dve.tensor_copy(IDB[k].rearrange("p (t o) -> p t o", o=1), RB[k][:, :, D:ROW])
                    wait(dve, "e_y_done", k, n + 1)
                    dve.tensor_tensor(ZB[k], bank(k, 0, 2)[:, :, 0:D], RB[k][:, :, 0:D], ALU.add).then_inc(es["z_ready", k], 1)

                normalise(0, 0)
                feature_major(0, 0)
                with dve.Fori(0, UNITS // 2) as it:
                    normalise(it, 1)
                    feature_major(it, 1)
                    result(it, 0)
                    normalise(it + 1, 0)
                    feature_major(it + 1, 0)
                    result(it, 1)
                wait(dve, "scattered", 0, UNITS // 2 * 16 * T)
                result(UNITS // 2, 0)

            @block.scalar
            def _(act):
                def gelu(n, k):
                    for b in range(4):
                        wait(act, "e_h_done", k, n * 4 + b + 1)
                        act.activation(HTB[k][:, 2 * b:2 * b + 2, :].rearrange("p c s -> p (c s)"), bank(k, b),
                                       ACT.Gelu_apprx_tanh).then_inc(es["e_gelu_done", k], 1)

                with act.Fori(0, UNITS // 2) as it:
                    gelu(it, 0)
                    gelu(it, 1)
                gelu(UNITS // 2, 0)

            @block.tensor
            def _(pe):
                def transposes(n, k):
                    wait(pe, "e_xhat_ready", k, n + 1)
                    for m in range(KC):
                        for t in range(T):
                            ins_ = pe.transpose(bank(k, 3)[:, m * UNIT + t * P:m * UNIT + (t + 1) * P],
                                                XHB[k][:, t, m * P:(m + 1) * P], ident[:])
                    ins_.then_inc(es["e_xhatT_done", k], 1)

                def up(n, k):
                    wait(pe, "w_loaded", k, n * 32 + 32)
                    wait(pe, "e_featT_ready", k, n + 1)
                    for b in range(4):
                        for m in (2 * b, 2 * b + 1):
                            for c in range(KC):
                                ins_ = pe.matmul(bank(k, b)[:, (m % 2) * UNIT:(m % 2 + 1) * UNIT], W1B[k][:, c, m * P:(m + 1) * P],
                                                 FTB[k][:, c, :], start=(c == 0), stop=(c == KC - 1))
                        ins_.then_inc(es["e_h_done", k], 1)

                def down(n, k):
                    for c in range(HC):
                        if c in (0, 4, 6):
                            wait(pe, "e_gelu_done", k, n * 4 + (2 if c == 0 else c // 2 + 1))
                        for t in range(T):
                            ins_ = pe.matmul(bank(k, t)[:, 0:D], HTB[k][:, c, t * P:(t + 1) * P], W2B[k][:, c, :],
                                             start=(c == 0), stop=(c == HC - 1))
                    ins_.then_inc(es["e_y_done", k], 1)

                transposes(0, 0)
                with pe.Fori(0, UNITS // 2) as it:
                    up(it, 0)
                    transposes(it, 1)
                    down(it, 0)
                    up(it, 1)
                    transposes(it + 1, 0)
                    down(it, 1)
                up(UNITS // 2, 0)
                down(UNITS // 2, 0)


def kernel(**inputs):
    import numpy as _np
    import concourse.bacc as _bacc
    from concourse import mybir as _mybir
    from concourse.bass_utils import run_bass_kernel_spmd as _run

    nc = _bacc.Bacc("TRN2", target_bir_lowering=False, num_devices=1)
    arrays, ins = {}, {}
    for name, a in inputs.items():
        a = _np.ascontiguousarray(a)
        arrays[f"in_{name}"] = a
        ins[name] = nc.dram_tensor(f"in_{name}", a.shape, _mybir.dt.from_np(a.dtype), kind="ExternalInput").ap()
    out = nc.dram_tensor("out_0", (B, S, D), F32, kind="ExternalOutput").ap()
    build(nc, ins, out)
    r = _run(nc, [arrays], core_ids=[0])
    return r.results[0]["out_0"]
```

```python
from collections import Counter
from contextlib import ExitStack

import concourse.bass as bass
from concourse import mybir

F32 = mybir.dt.float32
BF16 = mybir.dt.bfloat16
F32R = mybir.dt.float32r
I32 = mybir.dt.int32
ALU = mybir.AluOpType
ACT = mybir.ActivationFunctionType
AX = mybir.AxisListType

P = 128
B, S, D = 8, 256, 256
C2, KV = 128, 120
HEADS = 16
D0, D1 = D // HEADS, 32
HD = HEADS * D1
INNER = 1024
E = 8
T = S // P
KC = D // P
HC = INNER // P
TILES = B * T
TOKENS = B * S
EPS = 1e-5
UNIT = 2 * P
UNITS = TOKENS // UNIT + E - 1
BLOCKS = UNITS * T
MAGIC = 1.5 * 2.0 ** 23
PAD_ID = TOKENS


class Tally:

    def __init__(self, sems):
        self.sems, self.n = sems, Counter()

    def wait(self, eng, name, h=0, more=1):
        self.n[name, h] += more
        eng.wait_ge(self.sems[name, h], self.n[name, h])


def build(nc, ins, out):
    ctx = ExitStack()
    with ctx:
        weights_mem, arenas_mem = ExitStack(), ExitStack()

        def sb(name, shape, dt=F32, mem=ctx, side="left"):
            return mem.enter_context(nc.sbuf_tensor(name, shape, dt, side=side))

        x5_all = nc.dram_tensor("x5_rows", [2 * S + TOKENS, D], F32).ap()

        def pv(n, m):
            return pvec[:, col[n][0] + m:col[n][0] + m + 1]

        def bv(n, tiles=T):
            return bvec[:, BC.index(n):BC.index(n) + 1, :].to_broadcast([P, tiles, D])

        ident = sb("ident", [P, P]); identb = sb("identb", [P, P], BF16)
        later = sb("later", [P, P])
        strict = sb("strict", [P, P], BF16)
        onesb = sb("onesb", [P, P], BF16)
        onesf = sb("onesf", [P, P])
        own16 = sb("own16", [P, 8]); own32 = sb("own32", [P, 4])
        epst = sb("epst", [P, 2]); neghalf = sb("neghalf", [P, 2])
        onepe = sb("onepe", [P, 2]); eps2 = sb("eps2", [P, 2])
        eidx = sb("eidx", [P, E])
        neg_magic = sb("neg_magic", [P, 1])
        mean_w = sb("mean_w", [P, 3]); scale_w = sb("scale_w", [P, 3]); asum = sb("asum", [P, 3]); wtot = sb("wtot", [P, 3])

        ARENA = 13824
        arena = [sb(f"arena{h}", [P, ARENA], mem=arenas_mem, side="right") for h in range(2)]
        small = [sb(f"small{h}", [P, 256]) for h in range(2)]
        onehot_all = sb("onehot", [P, 2 * T + TILES, E], BF16)
        unit_ei = sb("unit_ei", [P, UNITS], I32)
        slot_ids = sb("slot_ids", [P, BLOCKS], I32)
        slot_rows = sb("slot_rows", [P, BLOCKS + 2 * T], I32)
        onehot = onehot_all[:, 2 * T:, :]

        def weight(name, shape, dt=F32):
            return sb(name, shape, dt, weights_mem)

        wq0 = weight("wq0", [P, KC, D]); wk0 = weight("wk0", [P, D]); wv0 = weight("wv0", [P, D]); wo0 = weight("wo0", [P, KC, D])
        wgT = weight("wgT", [P, KC, INNER], BF16); wuT = weight("wuT", [P, KC, INNER], BF16)
        wdT = weight("wdT", [P, HC, D], BF16)
        w1 = {}
        for a, kc in (("a1", KC), ("a2", 1)):
            w1[a] = dict(wq=weight(a + "_wq", [P, KC, HD]), wk=weight(a + "_wk", [P, kc, HD]), wv=weight(a + "_wv", [P, kc, HD]),
                         li1=weight(a + "_li1", [P, HD // P, D]), li2=weight(a + "_li2", [P, KC, INNER]),
                         li3=weight(a + "_li3", [P, HC, D]))
        wg_moe = weight("wg_moe", [P, KC, E])
        PP = ["L0_xattn_bq", "L0_xattn_bk"]
        for a in ("a1", "a2"):
            PP += [f"L1_xattn_{a}_{n}" for n in ("lnx_g", "lnx_b", "lny_g", "lny_b", "ln3_g", "ln3_b", "li2_b")]
        col, ncol = {}, 0
        for n in PP:
            col[n] = (ncol, ins[n].shape[0] // P)
            ncol += ins[n].shape[0] // P
        pvec = weight("pvec", [P, ncol])
        BC = ["L0_xattn_bv", "L0_xattn_bo", "L1_xattn_ln1_g", "L1_xattn_ln1_b", "L1_xattn_ln2_g", "L1_xattn_ln2_b",
              "L1_xattn_a1_li1_b", "L1_xattn_a1_li3_b", "L1_xattn_a2_li1_b", "L1_xattn_a2_li3_b"]
        bvec = weight("bvec", [P, len(BC), D])
        bgt = weight("bgt", [P, E])

        def view(h, at, shape, dt=F32):
            n = 1
            for s in shape:
                n *= s
            words = n if dt != BF16 else n // 2
            v = arena[h][:, at:at + words]
            if dt != F32:
                v = v.bitcast(dt)
            if len(shape) == 2:
                v = v.rearrange("p (a b) -> p a b", a=shape[0])
            elif len(shape) == 3:
                v = v.rearrange("p (a b c) -> p a b c", a=shape[0], b=shape[1])
            return v

        X = [view(h, 0, [T, D]) for h in range(2)]
        XH = [view(h, 512, [T, D]) for h in range(2)]
        Y = [view(h, 1024, [T, D]) for h in range(2)]
        XB = [view(h, 1536, [T, D]) for h in range(2)]
        FT = [view(h, 2048, [KC, S]) for h in range(2)]
        QT = [view(h, 2560, [4, S]) for h in range(2)]
        KT = [view(h, 3584, [4, S]) for h in range(2)]
        V1 = [view(h, 4608, [T, HD]) for h in range(2)]
        OT = [view(h, 5632, [4, S]) for h in range(2)]
        PR = [view(h, 6656, [2, 512]) for h in range(2)]
        PT = [view(h, 7680, [2, 1024]) for h in range(2)]
        KM = [view(h, 9728, [2, 512]) for h in range(2)]
        RTS = [view(h, 10752, [S]) for h in range(2)]
        RBC = [view(h, 11008, [T, P]) for h in range(2)]
        KT0 = [view(h, 11264, [2, KV]) for h in range(2)]
        KT2 = [view(h, 11520, [4, KV]) for h in range(2)]
        VM = [view(h, 12032, [8, 2, 32]) for h in range(2)]
        V2 = [view(h, 12544, [HD]) for h in range(2)]
        FT2 = [view(h, 6656, [KC, S]) for h in range(2)]
        XN = [view(h, 13056, [T, D]) for h in range(2)]
        CT = [view(h, 13568, [P]) for h in range(2)]
        CH = [view(h, 13696, [P]) for h in range(2)]
        CTT = [view(h, 10752, [KV]) for h in range(2)]
        CYT = [view(h, 10880, [KV]) for h in range(2)]
        FT5 = [view(h, 3584, [KC, S]) for h in range(2)]
        HH = [view(h, 7680, [T, INNER]) for h in range(2)]
        HT = [view(h, 7680, [HC, S]) for h in range(2)]
        N2 = [view(h, 2560, [T, INNER], BF16) for h in range(2)]
        N2T = [view(h, 3584, [HC, S], BF16) for h in range(2)]
        N1 = [view(h, 1024, [T, D], BF16) for h in range(2)]
        N1T = [view(h, 2048, [KC, S], BF16) for h in range(2)]
        SG = [view(h, 4608, [2, 512]) for h in range(2)]

        def sm(h, at, n):
            return small[h][:, at:at + n]

        ps = ctx.enter_context(nc.psum_tensor("ps", [P, 8, 512], F32))

        def bank(h, b, n=1):
            return ps[:, 4 * h + b, :] if n == 1 else ps[:, 4 * h + b:4 * h + b + n, :]

        NAMES = ["x_loaded", "ctx_loaded", "x5_stored", "cxhat_ready", "var_ready", "rstd_ready", "xhat_ready", "xhatT_done",
                 "featT_ready", "ctx_proj_done", "kT_ready", "v_ready", "cT_done", "cT_ready", "x5hat_ready", "x5T_done", "x5T_ready", "q_done", "qT_ready", "kv_done",
                 "res_ready", "km_ready", "s_done", "max_done", "exp_done", "t_done", "pt_ready", "pv_done",
                 "rec_ready", "rbc_ready", "rt_done", "rts_ready", "oT_ready", "out_done", "gu_done",
                 "silu_done", "hh_done", "n2_ready", "n2T_done", "n2T_ready", "h_done", "gelu_done",
                 "logits_done", "lg_ready", "dve_chain", "pool_chain"]
        sems, layer_sems = {}, ExitStack()
        for n in NAMES:
            for h in range(2):
                sems[n, h] = layer_sems.enter_context(nc.semaphore(f"{n}{h}"))
        numbers = [s.num for s in sems.values()]
        sem_range = range(min(numbers), max(numbers) + 1)
        assert len(sem_range) == len(numbers)

        def sem(name, h=0):
            return sems[name, h]

        raw = [arena[0][:, 2048:4096], arena[0][:, 4096:6144], arena[0][:, 6144:8192]]
        tern = [arena[1][:, 1024 * k:1024 * (k + 1)].bitcast(BF16) for k in range(2, 5)]
        w_load = ctx.enter_context(nc.semaphore("w_load"))
        w1_load = ctx.enter_context(nc.semaphore("w1_load"))
        W1_LOADS = 2 * 3 + 3 + 3 + 3
        first_load = ctx.enter_context(nc.semaphore("first_load"))
        q_load = [ctx.enter_context(nc.semaphore(f"q_load{k}")) for k in range(3)]
        rounded = ctx.enter_context(nc.semaphore("rounded"))
        const_ready = ctx.enter_context(nc.semaphore("const_ready"))
        wsum_ready = [ctx.enter_context(nc.semaphore(f"wsum_ready{k}")) for k in range(3)]
        wtot_done = ctx.enter_context(nc.semaphore("wtot_done"))
        tern_ready = ctx.enter_context(nc.semaphore("tern_ready"))
        ternT_done = ctx.enter_context(nc.semaphore("ternT_done"))
        pro_chain = ctx.enter_context(nc.semaphore("pro_chain"))

        with nc.Block() as block:
            @block.sync
            def _(sp):
                for k, n in enumerate(("L0_ffn_w_gate", "L0_ffn_w_up")):
                    sp.dma_start(raw[k].rearrange("p (c i) -> p c i", i=D),
                                 ins[n].rearrange("(c p) i -> p c i", p=P)).then_inc(q_load[k], 16)
                sp.dma_start(raw[2].rearrange("p (c i) -> p c i", i=INNER),
                             ins["L0_ffn_w_down"].rearrange("(c p) i -> p c i", p=P)).then_inc(q_load[2], 16)
                for h in range(2):
                    sp.dma_start(CT[h][0:KV, :], ins["ctx_512"][h]).then_inc(first_load, 16)
                    sp.dma_start(XN[h], ins["x"][h].rearrange("(t p) n -> p t n", p=P)).then_inc(first_load, 16)
                n_w = 0

                def load(dst, src):
                    sp.dma_start(dst, src).then_inc(w_load, 16)
                    return 16
                n_w += load(wq0[:], ins["L0_xattn_Wq"].rearrange("(c p) n -> p c n", p=P))
                n_w += load(wk0[:], ins["L0_xattn_Wk"])
                n_w += load(wv0[:], ins["L0_xattn_Wv"])
                n_w += load(wo0[:], ins["L0_xattn_Wo"].rearrange("(c p) n -> p c n", p=P))
                n_w += load(wg_moe[:], ins["L1_ffn_Wg"].rearrange("(c p) n -> p c n", p=P))
                n_w += load(bgt[:], ins["L1_ffn_bg"].rearrange("(a n) -> a n", a=1).to_broadcast([P, E]))
                for k, n in enumerate(BC):
                    n_w += load(bvec[:, k, :], ins[n].rearrange("(a n) -> a n", a=1).to_broadcast([P, D]))
                with nc.allow_non_contiguous_dma(reason="per-feature vectors onto partitions, small"):
                    for n in PP:
                        c0, m = col[n]
                        n_w += load(pvec[:, c0:c0 + m], ins[n].rearrange("(c p) -> p c", p=P))
                for a in ("a2", "a1"):
                    w = w1[a]
                    for n in ("wk", "wv", "wq"):
                        src = ins[f"L1_xattn_{a}_{n}"]
                        for c in range(src.shape[1] // P):
                            sp.dma_start(w[n][:, c, :].rearrange("p (h d) -> p h d", h=HEADS),
                                         src[:, c * P:(c + 1) * P, :].rearrange("h p d -> p h d")).then_inc(w1_load, 16)
                    for n in ("li1", "li2", "li3"):
                        sp.dma_start(w[n][:], ins[f"L1_xattn_{a}_{n}_w"].rearrange("(c p) n -> p c n", p=P)
                                     ).then_inc(w1_load, 16)
                sp.wait_ge(first_load, 16 * 4)
                sp.wait_ge(w_load, n_w)

            @block.gpsimd
            def _(pool):
                pool.memset(ident[:], 0.0)
                pool.memset(identb[:], 0.0)
                pool.memset(later[:], 1.0)
                pool.memset(strict[:], 1.0)
                pool.memset(onesb[:], 1.0)
                pool.memset(onesf[:], 1.0)
                pool.memset(own16[:], 1.0)
                pool.memset(own32[:], 1.0)
                pool.memset(epst[:], EPS)
                pool.memset(onepe[:], 1.0 + EPS)
                pool.memset(eps2[:], EPS * EPS)
                pool.memset(neg_magic[:], -MAGIC)
                pool.memset(neghalf[:], -0.5)
                pool.iota(eidx[:], pattern=[[1, E]], base=0, channel_multiplier=0,
                          allow_small_or_imprecise_dtypes=True).then_inc(const_ready, 1)
                pool.wait_ge(const_ready, 1)
                for m in (ident, identb):
                    pool.affine_select(out=m[:], in_=m[:], compare_op=ALU.not_equal, fill=1.0, base=0,
                                       pattern=[[-1, P]], channel_multiplier=1)
                pool.affine_select(out=later[:], in_=later[:], compare_op=ALU.is_gt, fill=0.0, base=0,
                                   pattern=[[-1, P]], channel_multiplier=1)
                pool.affine_select(out=strict[:], in_=strict[:], compare_op=ALU.is_gt, fill=0.0, base=0,
                                   pattern=[[1, P]], channel_multiplier=-1).then_inc(const_ready, 1)
                for m, width, n in ((own16, 16, 8), (own32, 32, 4)):
                    pool.affine_select(out=m[:], in_=m[:], compare_op=ALU.is_ge, fill=0.0, base=0,
                                       pattern=[[-width, n]], channel_multiplier=1).then_inc(const_ready, 1)
                pool.wait_ge(const_ready, 4)
                for m, width, n in ((own16, 16, 8), (own32, 32, 4)):
                    pool.affine_select(out=m[:], in_=m[:], compare_op=ALU.is_gt, fill=0.0, base=width,
                                       pattern=[[width, n]], channel_multiplier=-1).then_inc(const_ready, 1)
                for h in range(2):
                    pool.memset(VM[h], 0.0).then_inc(const_ready, 1)
                    pool.memset(small[h][:], 0.0)
                    pool.memset(X[h], 0.0)

            @block.vector
            def _(dve):
                n = 0

                def step(ins_):
                    nonlocal n
                    ins_.then_inc(pro_chain, 1)
                    n += 1
                    dve.wait_ge(pro_chain, n)

                for k in range(3):
                    if k != 1:
                        dve.wait_ge(q_load[k], 16)
                        dve.tensor_reduce(asum[:, k:k + 1], raw[k], AX.X, ALU.add,
                                          apply_absolute_value=True).then_inc(wsum_ready[k], 1)
                    dve.wait_ge(wtot_done, k + 1)
                    step(dve.tensor_scalar(mean_w[:, k:k + 1], ps[:, 6 + k % 2, 0:1], 1.0 / (INNER * D), EPS, ALU.mult, ALU.max))
                    step(dve.reciprocal(scale_w[:, k:k + 1], mean_w[:, k:k + 1]))
                    step(dve.tensor_scalar(raw[k], raw[k], scale_w[:, k:k + 1], MAGIC, ALU.mult, ALU.add))
                    dve.tensor_scalar(raw[k], raw[k], MAGIC + 1.0, MAGIC - 1.0, ALU.min, ALU.max).then_inc(rounded, 1)
                dve.wait_ge(ternT_done, 3)
                for c in range(KC):
                    dve.tensor_copy(wdT[:, :, c * P:(c + 1) * P],
                                    ps[:, 4 + c, :].bitcast(BF16).rearrange("p (i o) -> p i o", i=HC))

            @block.scalar
            def _(act):
                act.wait_ge(q_load[1], 16)
                act.activation(arena[1][:, 5120:5120 + KC * INNER], raw[1], ACT.Abs, accum_out=asum[:, 1:2]
                               ).then_inc(wsum_ready[1], 1)
                act.wait_ge(const_ready, 1)
                for k in range(3):
                    act.wait_ge(rounded, k + 1)
                    act.activation(tern[k], raw[k], ACT.Identity, bias=neg_magic[:], scale=1.0).then_inc(tern_ready, 1)
                for k, dst in ((0, wgT), (1, wuT)):
                    act.wait_ge(ternT_done, k + 1)
                    for i in range(KC):
                        act.activation(dst[:, i, :], ps[:, 2 * k + i, :].bitcast(BF16), ACT.Copy)

            @block.tensor
            def _(pe):
                def total(k):
                    pe.wait_ge(wsum_ready[k], 1)
                    if k == 2:
                        pe.wait_ge(pro_chain, 1)
                    pe.matmul(ps[:, 6 + k % 2, 0:1], onesf[:], asum[:, k:k + 1], start=True, stop=True).then_inc(wtot_done, 1)

                pe.wait_ge(const_ready, 1)
                total(0)
                total(1)
                total(2)
                pe.wait_ge(const_ready, 2)
                for k in range(2):
                    pe.wait_ge(tern_ready, k + 1)
                    t_k = tern[k].rearrange("p (c i) -> p c i", i=D)
                    for i in range(KC):
                        for c in range(HC):
                            last = pe.transpose(ps[:, 2 * k + i, c * 64:(c + 1) * 64].bitcast(BF16),
                                                t_k[:, c, i * P:(i + 1) * P], identb[:])
                    last.then_inc(ternT_done, 1)
                pe.wait_ge(tern_ready, 3)
                t_d = tern[2].rearrange("p (c i) -> p c i", i=INNER)
                for c in range(KC):
                    for i in range(HC):
                        last = pe.transpose(ps[:, 4 + c, i * 64:(i + 1) * 64].bitcast(BF16),
                                            t_d[:, c, i * P:(i + 1) * P], identb[:])
                last.then_inc(ternT_done, 1)
        nc.all_engine_barrier(sem_only=True)

        ATT = {"L0": dict(nh=4, nk=KV, d=D0, hc=8, gpc=2, groups=4), "a1": dict(nh=2, nk=S, d=D1, hc=4, gpc=2, groups=8),
               "a2": dict(nh=4, nk=KV, d=D1, hc=4, gpc=1, groups=4)}
        NMX, SUMS, REC, ST, MV, VE, RSTD = 0, 32, 64, 96, 108, 112, 114
        AM, SC, SU, SGT, SUT = 120, 128, 132, 136, 140
        LG, EQ, MX, IDX = 148, 164, 180, 182
        SD = 144
        X5 = 96

        def layers(block, it, final=False):
            @block.sync
            def _(sp):
                if final:
                    for h in range(2):
                        at = B // 2 * 2 * S + h * S
                        sp.dma_start(x5_all[at:at + S, :].rearrange("(t p) n -> p t n", p=P), X[h]
                                     ).then_inc(sem("x5_stored", h), 16)
                    for h in range(2):
                        sp.wait_ge(sem("x5_stored", h), 16)
                    return
                for h in range(2):
                    sp.dma_start(x5_all[bass.ds(it * 2 * S + h * S, S), :].rearrange("(t p) n -> p t n", p=P), X[h]
                                 ).then_inc(sem("x5_stored", h), 16)
                for h in range(2):
                    sp.wait_ge(sem("cT_done", h), 1)
                    sp.wait_ge(sem("cxhat_ready", h), 1)
                    sp.wait_ge(sem("res_ready", h), 1)
                    sp.dma_start(CT[h][0:KV, :], ins["ctx_512"][bass.ds((it * 2 + 2 + h) % B, 1)].rearrange("o p n -> p (o n)")
                                 ).then_inc(sem("ctx_loaded", h), 16)
                    sp.dma_start(XN[h], ins["x"][bass.ds((it * 2 + 2 + h) % B, 1)].rearrange("o (t p) n -> p (o t) n", p=P)
                                 ).then_inc(sem("x_loaded", h), 16)
                for h in range(2):
                    sp.wait_ge(sem("x5_stored", h), 16)
                    sp.wait_ge(sem("ctx_loaded", h), 16)
                    sp.wait_ge(sem("x_loaded", h), 16)

            @block.gpsimd
            def _(pool):
                tally = Tally(sems)
                chain = [0, 0]

                def link(h, ins_):
                    ins_.then_inc(sem("pool_chain", h), 1)
                    chain[h] += 1
                    pool.wait_ge(sem("pool_chain", h), chain[h])

                def rstd(h, o=0, twice=False):
                    tally.wait(pool, "var_ready", h)
                    v = sm(h, o + MV, 4).rearrange("p (t k) -> p t k", k=2)[:, :, 1]
                    if twice:
                        link(h, pool.tensor_tensor(sm(h, o + VE, 2), v, onepe[:], ALU.mult))
                        link(h, pool.tensor_tensor(sm(h, o + VE, 2), sm(h, o + VE, 2), eps2[:], ALU.add))
                    else:
                        link(h, pool.tensor_tensor(sm(h, o + VE, 2), v, epst[:], ALU.add))
                    pool.tensor_tensor(sm(h, o + RSTD, 2), sm(h, o + VE, 2), neghalf[:], ALU.pow
                                       ).then_inc(sem("rstd_ready", h), 1)

                def attention(a):
                    q = ATT[a]
                    nh, nk, d, hc, gpc = q["nh"], q["nk"], q["d"], q["hc"], q["gpc"]
                    own = own16 if d == D0 else own32
                    for g in range(q["groups"]):
                        for h in range(2):
                            if g == 0 and a != "a2":
                                tally.wait(pool, "kT_ready", h, 1 if a == "L0" else 2)
                            if g >= 2:
                                tally.wait(pool, "s_done", h, 2)
                            kt = {"L0": KT0, "a1": KT, "a2": KT2}[a][h][:, g // gpc, :]
                            j0 = (g % gpc) * nh
                            pool.tensor_tensor(
                                KM[h][:, g % 2, 0:nh * nk].rearrange("p (j k) -> p j k", j=nh),
                                kt.rearrange("p (o k) -> p o k", o=1).to_broadcast([P, nh, nk]),
                                own[:, j0:j0 + nh].rearrange("p (j o) -> p j o", o=1).to_broadcast([P, nh, nk]),
                                ALU.mult).then_inc(sem("km_ready", h), 1)
                        if g >= 1 and (g - 1) % gpc == gpc - 1:
                            recs((g - 1) // gpc, a)
                    for h in range(2):
                        tally.n["s_done", h] += 4
                    recs((q["groups"] - 1) // gpc, a)

                def recs(c, a):
                    q = ATT[a]
                    hc, d = q["hc"], q["d"]
                    for h in range(2):
                        tally.wait(pool, "rec_ready", h)
                        if c >= 1:
                            tally.wait(pool, "rt_done", h)
                        for t in range(T):
                            last = pool.tensor_tensor(
                                RBC[h][:, t, :].rearrange("p (j k) -> p j k", k=d),
                                sm(h, REC + t * HEADS + c * hc, hc).rearrange("p (j o) -> p j o", o=1).to_broadcast([P, hc, d]),
                                onesf[:, 0:P].rearrange("p (j k) -> p j k", k=d), ALU.mult)
                        last.then_inc(sem("rbc_ready", h), 1)
                    if c == q["groups"] // q["gpc"] - 1:
                        for h in range(2):
                            tally.n["rt_done", h] += 1

                def add(h, o, x, y, name="res_ready"):
                    pool.tensor_tensor(o, x, y, ALU.add).then_inc(sem(name, h), 1)

                def mlp_residual(h, a):
                    pool.tensor_tensor(Y[h], Y[h], XB[h], ALU.add).then_inc(sem("pool_chain", h), 1)
                    chain[h] += 1
                    pool.wait_ge(sem("pool_chain", h), chain[h])
                    add(h, Y[h], Y[h], bv(f"L1_xattn_{a}_li3_b"))

                if final:
                    for h in range(2):
                        rstd(h, X5)
                    return
                for h in range(2):
                    rstd(h)
                for h in range(2):
                    rstd(h, X5)
                for h in range(2):
                    rstd(h)
                attention("L0")
                for h in range(2):
                    add(h, XB[h], XN[h], bv("L0_xattn_bo"))
                for h in range(2):
                    rstd(h)
                for h in range(2):
                    rstd(h, twice=True)
                    rstd(h)
                for h in range(2):
                    add(h, XB[h], Y[h], bv("L1_xattn_a1_li1_b"))
                attention("a1")
                for h in range(2):
                    rstd(h)
                    mlp_residual(h, "a1")
                for h in range(2):
                    rstd(h)
                    rstd(h)
                for h in range(2):
                    add(h, XB[h], Y[h], bv("L1_xattn_a2_li1_b"))
                attention("a2")
                for h in range(2):
                    rstd(h)
                    mlp_residual(h, "a2")

            @block.vector
            def _(dve):
                tally = Tally(sems)
                chain = [0, 0]
                norms = [0, 0]

                def step(h, ins_):
                    ins_.then_inc(sem("dve_chain", h), 1)
                    chain[h] += 1
                    dve.wait_ge(sem("dve_chain", h), chain[h])

                def stats(h, src, rows=P, tiles=T, o=0):
                    for t in range(tiles):
                        ins_ = dve.bn_stats(small[h][0:rows, o + ST + 6 * t:o + ST + 6 * t + 6], src[0:rows, t, :])
                    step(h, ins_)
                    for t in range(tiles):
                        ins_ = dve.bn_aggr(small[h][0:rows, o + MV + 2 * t:o + MV + 2 * t + 2],
                                           small[h][0:rows, o + ST + 6 * t:o + ST + 6 * t + 6])
                    ins_.then_inc(sem("var_ready", h), 1)
                    norms[h] += 1

                def apply(h, dst, src, rows=P, tiles=T, o=0):
                    tally.wait(dve, "rstd_ready", h)
                    for t in range(tiles):
                        ins_ = dve.tensor_scalar(dst[0:rows, t, :], src[0:rows, t, :],
                                                 small[h][0:rows, o + MV + 2 * t:o + MV + 2 * t + 1],
                                                 small[h][0:rows, o + RSTD + t:o + RSTD + t + 1], ALU.subtract, ALU.mult)
                    return ins_

                def logits(h):
                    tally.wait(dve, "logits_done", h)
                    lg = sm(h, LG, 2 * E).rearrange("p (t e) -> p t e", t=T)
                    dve.tensor_tensor(lg, bank(h, 2)[:, 0:2 * E].rearrange("p (t e) -> p t e", t=T),
                                      bgt[:].rearrange("p (o e) -> p o e", o=1).to_broadcast([P, T, E]), ALU.add
                                      ).then_inc(sem("lg_ready", h), 1)

                def choose(h, at):
                    dve.wait_ge(sem("lg_ready", h), 1)
                    lg = sm(h, LG, 2 * E).rearrange("p (t e) -> p t e", t=T)
                    eq = sm(h, EQ, 2 * E).rearrange("p (t e) -> p t e", t=T)
                    step(h, dve.tensor_reduce(sm(h, MX, T), lg, AX.X, ALU.max))
                    step(h, dve.tensor_tensor(eq, lg, sm(h, MX, T).rearrange("p (t o) -> p t o", o=1).to_broadcast([P, T, E]),
                                              ALU.is_lt))
                    eb = eidx[:].rearrange("p (o e) -> p o e", o=1).to_broadcast([P, T, E])
                    step(h, dve.scalar_tensor_tensor(lg, eq, float(E), eb, ALU.mult, ALU.add))
                    step(h, dve.tensor_reduce(sm(h, IDX, T), lg, AX.X, ALU.min))
                    dve.tensor_tensor(at, eb, sm(h, IDX, T).rearrange("p (t o) -> p t o", o=1).to_broadcast([P, T, E]),
                                      ALU.is_equal)

                def norm_gain(h, src, g, b):
                    g, b = (bvec[:, BC.index(n), :] for n in (g, b))
                    dve.wait_ge(sem("var_ready", h), norms[h])
                    for t in range(T):
                        ins_ = dve.scalar_tensor_tensor(XH[h][:, t, :], src[:, t, :], sm(h, MV + 2 * t, 1), g,
                                                        ALU.subtract, ALU.mult)
                    step(h, ins_)
                    tally.wait(dve, "rstd_ready", h)
                    for t in range(T):
                        ins_ = dve.scalar_tensor_tensor(Y[h][:, t, :], XH[h][:, t, :], sm(h, RSTD + t, 1), b,
                                                        ALU.mult, ALU.add)
                    step(h, ins_)

                def quant_scales(h, src, t0, n):
                    step(h, dve.tensor_reduce(sm(h, AM + t0, n), src, AX.X, ALU.max, apply_absolute_value=True))
                    step(h, dve.tensor_scalar(sm(h, SU + t0, n), sm(h, AM + t0, n), EPS, 1.0 / 127.0, ALU.max, ALU.mult))
                    step(h, dve.reciprocal(sm(h, SC + t0, n), sm(h, SU + t0, n)))

                def attention(a):
                    q = ATT[a]
                    nh, nk, d, hc, gpc, ng = q["nh"], q["nk"], q["d"], q["hc"], q["gpc"], q["groups"]
                    units = 2 * ng

                    def row_max(h, u):
                        tally.wait(dve, "s_done", h)
                        dve.tensor_reduce(sm(h, NMX + u * nh, nh),
                                          bank(h, u % 2)[:, 0:nh * nk].rearrange("p (j k) -> p j k", j=nh),
                                          AX.X, ALU.max, negate=True).then_inc(sem("max_done", h), 1)

                    def evacuate(h, u):
                        g, t = divmod(u, 2)
                        tally.wait(dve, "t_done", h)
                        if t == 0 and g >= 2:
                            tally.wait(dve, "pv_done", h)
                        if a == "a1":
                            pt = PT[h][:, g % 2, :].rearrange("p (c j s) -> p c j s", c=2, j=nh)
                            msk = later[:].rearrange("p (o s) -> p o s", o=1).to_broadcast([P, nh, P])
                            if t == 0:
                                src = bank(h, 2).rearrange("p (c j s) -> p c j s", c=2, j=nh)
                                dve.tensor_tensor(pt[:, 0, :, 0:P], src[:, 0], msk, ALU.mult)
                                ins_ = dve.tensor_copy(pt[:, 1, :, 0:P], src[:, 1])
                            else:
                                src = bank(h, 2)[:, 0:nh * P].rearrange("p (j s) -> p j s", j=nh)
                                ins_ = dve.tensor_tensor(pt[:, 1, :, P:S], src, msk, ALU.mult)
                        else:
                            pt = PT[h][0:KV, g % 2, :].rearrange("p (j s) -> p j s", j=nh)
                            ins_ = dve.tensor_copy(pt[:, :, t * P:(t + 1) * P],
                                                   bank(h, 2)[0:KV].rearrange("p (j s) -> p j s", j=nh))
                        ins_.then_inc(sem("pt_ready", h), 1)

                    def recip(h, c):
                        tally.wait(dve, "exp_done", h, 2 * gpc)
                        sums = sm(h, SUMS, 2 * HEADS).rearrange("p (t j) -> p t j", t=T)[:, :, c * hc:(c + 1) * hc]
                        rec = sm(h, REC, 2 * HEADS).rearrange("p (t j) -> p t j", t=T)[:, :, c * hc:(c + 1) * hc]
                        dve.reciprocal(rec, sums).then_inc(sem("rec_ready", h), 1)

                    def normalise(h, c):
                        tally.wait(dve, "rts_ready", h)
                        dve.tensor_tensor(OT[h][:, c, :], bank(h, 3)[:, (c % 2) * S:(c % 2) * S + S], RTS[h], ALU.mult
                                          ).then_inc(sem("oT_ready", h), 1)

                    for u in range(units + 3):
                        for h in range(2):
                            v = u - 3
                            if v >= 0 and v % (2 * gpc) == 2 * gpc - 1:
                                normalise(h, v // (2 * gpc))
                            if u < units:
                                row_max(h, u)
                            if 1 <= u <= units:
                                evacuate(h, u - 1)
                            v = u - 1
                            if 0 <= v < units and v % (2 * gpc) == 2 * gpc - 1:
                                recip(h, v // (2 * gpc))
                    for h in range(2):
                        tally.n["pv_done", h] += 2

                def mlp(a, dst_residual):
                    for h in range(2):
                        tally.wait(dve, "out_done", h)
                        tally.wait(dve, "res_ready", h)
                        step(h, dve.tensor_tensor(XB[h], bank(h, 0).rearrange("p (t n) -> p t n", t=T), XB[h], ALU.add))
                        stats(h, XB[h])
                        apply(h, XH[h], XB[h]).then_inc(sem("xhat_ready", h), 1)
                    for h in range(2):
                        tally.wait(dve, "out_done", h)
                        tally.wait(dve, "res_ready", h)
                        step(h, dve.tensor_tensor(Y[h], bank(h, 0, 2)[:, :, 0:D], Y[h], ALU.add))
                        dst_residual(h)

                def x5_norm(h):
                    apply(h, Y[h], X[h], o=X5).then_inc(sem("x5hat_ready", h), 1)

                if final:
                    for h in range(2):
                        stats(h, X[h], o=X5)
                    for h in range(2):
                        x5_norm(h)
                    for h in range(2):
                        logits(h)
                        choose(h, onehot_all[:, TILES + h * T:TILES + (h + 1) * T, :])
                    return
                for h in range(2):
                    stats(h, XN[h])
                for h in range(2):
                    apply(h, XH[h], XN[h]).then_inc(sem("xhat_ready", h), 1)
                    stats(h, X[h], o=X5)
                for h in range(2):
                    x5_norm(h)
                one = "p (t n) -> p t n"
                for h in range(2):
                    stats(h, CT[h].rearrange(one, t=1), KV, 1)
                for h in range(2):
                    tally.wait(dve, "ctx_proj_done", h)
                    for par in range(2):
                        ins_ = dve.tensor_tensor(VM[h][0:KV, :, par, par * D0:(par + 1) * D0],
                                          bank(h, 1)[0:KV, 256:512].rearrange("p (a b d) -> p a b d", b=2, d=D0)[:, :, par, :],
                                          bvec[0:KV, BC.index("L0_xattn_bv"), :].rearrange("p (a b d) -> p a b d", b=2, d=D0)[:, :, par, :],
                                          ALU.add)
                    ins_.then_inc(sem("v_ready", h), 1)
                for h in range(2):
                    tally.wait(dve, "q_done", h)
                    for m in range(KC):
                        ins_ = dve.tensor_scalar(QT[h][:, m, :], bank(h, 3)[:, m * S:(m + 1) * S], pv("L0_xattn_bq", m),
                                                 D0 ** -0.5, ALU.add, ALU.mult)
                    ins_.then_inc(sem("qT_ready", h), 1)
                for h in range(2):
                    apply(h, CH[h].rearrange(one, t=1), CT[h].rearrange(one, t=1), KV, 1).then_inc(sem("cxhat_ready", h), 1)
                attention("L0")

                def quantised_input(h):
                    tally.wait(dve, "out_done", h)
                    tally.wait(dve, "res_ready", h)
                    dve.wait_ge(sem("x5_stored", h), 16)
                    step(h, dve.tensor_tensor(X[h], bank(h, 0).rearrange("p (t n) -> p t n", t=T), XB[h], ALU.add))
                    stats(h, X[h])
                    step(h, apply(h, XH[h], X[h]))
                    quant_scales(h, XH[h], 0, T)
                    dve.tensor_scalar(sm(h, SGT, T), sm(h, SU, T), mean_w[:, 0:1], None, ALU.mult)
                    dve.tensor_scalar(sm(h, SUT, T), sm(h, SU, T), mean_w[:, 1:2], None, ALU.mult)
                    for t in range(T):
                        ins_ = dve.tensor_scalar(XH[h][:, t, :], XH[h][:, t, :], sm(h, SC + t, 1), MAGIC, ALU.mult, ALU.add)
                    step(h, ins_)
                    dve.tensor_scalar(N1[h], XH[h], -MAGIC, 127.0, ALU.add, ALU.min).then_inc(sem("xhat_ready", h), 1)

                quantised_input(0)
                for h in range(2):
                    logits(h)
                quantised_input(1)

                def gated(t, h):
                    for j in range(2):
                        tally.wait(dve, "silu_done", h)
                        dve.scalar_tensor_tensor(HH[h][:, t, j * 512:(j + 1) * 512], bank(h, 2 * j + 1),
                                                 sm(h, SUT + t, 1), SG[h][:, j, :], ALU.mult, ALU.mult
                                                 ).then_inc(sem("hh_done", h), 1)

                def quantise(t, h):
                    tally.wait(dve, "hh_done", h, 2)
                    quant_scales(h, HH[h][:, t, :], t, 1)
                    step(h, dve.tensor_scalar(HH[h][:, t, :], HH[h][:, t, :], sm(h, SC + t, 1), MAGIC, ALU.mult, ALU.add))
                    dve.tensor_scalar(N2[h][:, t, :], HH[h][:, t, :], -MAGIC, 127.0, ALU.add, ALU.min
                                      ).then_inc(sem("n2_ready", h), 1)
                    dve.tensor_scalar(sm(h, SD + t, 1), sm(h, SU + t, 1), mean_w[:, 2:3], None, ALU.mult)

                for t in range(T):
                    for h in range(2):
                        gated(t, h)
                        quantise(t, h)
                for h in range(2):
                    tally.wait(dve, "out_done", h)
                    for t in range(T):
                        ins_ = dve.scalar_tensor_tensor(X[h][:, t, :], bank(h, 2)[:, t * D:(t + 1) * D], sm(h, SD + t, 1),
                                                        X[h][:, t, :], ALU.mult, ALU.add)
                    step(h, ins_)
                    stats(h, X[h])
                    norm_gain(h, X[h], "L1_xattn_ln1_g", "L1_xattn_ln1_b")
                    stats(h, Y[h])
                    apply(h, XH[h], Y[h]).then_inc(sem("xhat_ready", h), 1)
                for h in range(2):
                    tally.wait(dve, "q_done", h)
                    dve.tensor_scalar(QT[h].rearrange("p a s -> p (a s)").rearrange("p (a s) -> p a s", a=2), bank(h, 0, 2),
                                      D1 ** -0.5, None, ALU.mult).then_inc(sem("qT_ready", h), 1)
                for h in range(2):
                    choose(h, onehot_all[:, bass.ds(it * 4 + h * 2, T), :])
                attention("a1")

                def after_a1(h):
                    stats(h, Y[h])
                    norm_gain(h, Y[h], "L1_xattn_ln2_g", "L1_xattn_ln2_b")
                    stats(h, Y[h])
                    apply(h, XH[h], Y[h]).then_inc(sem("xhat_ready", h), 1)
                mlp("a1", after_a1)
                for h in range(2):
                    tally.wait(dve, "q_done", h)
                    dve.tensor_scalar(QT[h].rearrange("p a s -> p (a s)").rearrange("p (a s) -> p a s", a=2), bank(h, 0, 2),
                                      D1 ** -0.5, None, ALU.mult).then_inc(sem("qT_ready", h), 1)
                attention("a2")

                def after_a2(h):
                    dve.tensor_tensor(X[h], X[h], Y[h], ALU.add)
                mlp("a2", after_a2)

            @block.scalar
            def _(act):
                tally = Tally(sems)

                def attention(a):
                    q = ATT[a]
                    nh, nk, hc, gpc, ng = q["nh"], q["nk"], q["hc"], q["gpc"], q["groups"]
                    units = 2 * ng
                    for u in range(units + 3):
                        for h in range(2):
                            if u < units:
                                g, t = divmod(u, 2)
                                tally.wait(act, "max_done", h)
                                if u >= 2:
                                    tally.wait(act, "t_done", h)
                                for j in range(nh):
                                    head = t * HEADS + g * nh + j
                                    ins_ = act.activation(PR[h][:, u % 2, j * nk:(j + 1) * nk],
                                                          bank(h, u % 2)[:, j * nk:(j + 1) * nk], ACT.Exp,
                                                          bias=sm(h, NMX + u * nh + j, 1), scale=1.0,
                                                          accum_out=sm(h, SUMS + head, 1))
                                ins_.then_inc(sem("exp_done", h), 1)
                            v = u - 2
                            if v >= 0 and v % (2 * gpc) == 2 * gpc - 1:
                                c = v // (2 * gpc)
                                tally.wait(act, "rt_done", h)
                                if c >= 1:
                                    tally.wait(act, "oT_ready", h)
                                act.activation(RTS[h], bank(h, 3)[:, ((c + 1) % 2) * S:((c + 1) % 2) * S + S], ACT.Copy
                                               ).then_inc(sem("rts_ready", h), 1)
                    for h in range(2):
                        tally.n["t_done", h] += 2
                        tally.n["oT_ready", h] += 1

                def transposed(h, dst, g, b):
                    for m in range(KC):
                        ins_ = act.activation(dst[h][:, m, :], bank(h, 3)[:, m * S:(m + 1) * S], ACT.Identity,
                                              bias=pv(b, m), scale=pv(g, m))
                    return ins_

                def mlp(a):
                    def inputs(h):
                        tally.wait(act, "xhatT_done", h)
                        transposed(h, FT, f"L1_xattn_{a}_ln3_g", f"L1_xattn_{a}_ln3_b").then_inc(sem("featT_ready", h), 1)

                    def gelu(h, banks):
                        for k in banks:
                            tally.wait(act, "h_done", h)
                            for m in (2 * k, 2 * k + 1):
                                ins_ = act.activation(HT[h][:, m, :], bank(h, k)[:, (m % 2) * S:(m % 2) * S + S], ACT.Gelu,
                                                      bias=pv(f"L1_xattn_{a}_li2_b", m), scale=1.0)
                            ins_.then_inc(sem("gelu_done", h), 1)

                    inputs(0)
                    gelu(0, (0, 1))
                    inputs(1)
                    gelu(0, (2, 3))
                    gelu(1, (0, 1, 2, 3))

                def x5T(h):
                    tally.wait(act, "x5T_done", h)
                    act.activation(FT5[h].rearrange("p a s -> p (a s)"), bank(h, 2), ACT.Copy).then_inc(sem("x5T_ready", h), 1)

                if final:
                    for h in range(2):
                        x5T(h)
                    return
                for h in range(2):
                    tally.wait(act, "cT_done", h)
                    act.activation(CTT[h], bank(h, 1)[:, 0:KV], ACT.Copy).then_inc(sem("cT_ready", h), 1)
                for h in range(2):
                    tally.wait(act, "ctx_proj_done", h)
                    for m in range(2):
                        ins_ = act.activation(KT0[h][:, m, :], bank(h, 0)[:, m * KV:(m + 1) * KV], ACT.Identity,
                                              bias=pv("L0_xattn_bk", m), scale=1.0)
                    ins_.then_inc(sem("kT_ready", h), 1)
                for h in range(2):
                    tally.wait(act, "xhatT_done", h)
                    act.activation(FT[h].rearrange("p a s -> p (a s)"), bank(h, 3), ACT.Copy).then_inc(sem("featT_ready", h), 1)
                for h in range(2):
                    x5T(h)
                attention("L0")
                for t in range(T):
                    for h in range(2):
                        if t == 0:
                            tally.wait(act, "xhatT_done", h)
                            act.activation(N1T[h].rearrange("p a s -> p (a s)"), bank(h, 3).bitcast(BF16)[:, 0:512], ACT.Copy
                                           ).then_inc(sem("featT_ready", h), 1)
                        for j in range(2):
                            tally.wait(act, "gu_done", h)
                            if t == 1:
                                tally.wait(act, "hh_done", h)
                            act.activation(SG[h][:, j, :], bank(h, 2 * j), ACT.Silu,
                                           scale=sm(h, SGT + t, 1)).then_inc(sem("silu_done", h), 1)
                for h in range(2):
                    tally.n["hh_done", h] += 2

                def quantisedT(t, h):
                    tally.wait(act, "n2T_done", h)
                    act.activation(N2T[h][:, :, t * P:(t + 1) * P],
                                   bank(h, t).bitcast(BF16).rearrange("p (c s) -> p c s", c=HC), ACT.Copy
                                   ).then_inc(sem("n2T_ready", h), 1)

                for h in range(2):
                    quantisedT(0, h)
                    tally.wait(act, "cT_done", h)
                    act.activation(CYT[h], bank(h, 2)[:, 0:KV], ACT.Identity, bias=pv("L1_xattn_a2_lny_b", 0),
                                   scale=pv("L1_xattn_a2_lny_g", 0)).then_inc(sem("cT_ready", h), 1)
                    tally.wait(act, "ctx_proj_done", h)
                    act.activation(V2[h][0:KV, :], bank(h, 2)[0:KV], ACT.Copy)
                    act.activation(KT2[h].rearrange("p a k -> p (a k)"), bank(h, 3)[:, 0:4 * KV], ACT.Copy
                                   ).then_inc(sem("kT_ready", h), 1)
                    quantisedT(1, h)
                for h in range(2):
                    tally.wait(act, "xhatT_done", h)
                    transposed(h, FT, "L1_xattn_a1_lnx_g", "L1_xattn_a1_lnx_b").then_inc(sem("featT_ready", h), 1)
                    transposed(h, FT2, "L1_xattn_a1_lny_g", "L1_xattn_a1_lny_b").then_inc(sem("featT_ready", h), 1)
                for h in range(2):
                    tally.wait(act, "kv_done", h)
                    act.activation(KT[h].rearrange("p a s -> p (a s)").rearrange("p (a s) -> p a s", a=2), bank(h, 2, 2),
                                   ACT.Copy).then_inc(sem("kT_ready", h), 1)
                for h in range(2):
                    tally.wait(act, "kv_done", h)
                    act.activation(V1[h], bank(h, 0, 2), ACT.Copy).then_inc(sem("v_ready", h), 1)
                attention("a1")
                mlp("a1")
                for h in range(2):
                    tally.wait(act, "xhatT_done", h)
                    transposed(h, FT, "L1_xattn_a2_lnx_g", "L1_xattn_a2_lnx_b").then_inc(sem("featT_ready", h), 1)
                attention("a2")
                mlp("a2")

            @block.tensor
            def _(pe):
                tally = Tally(sems)

                def transpose_x(h):
                    tally.wait(pe, "xhat_ready", h)
                    for m in range(KC):
                        for t in range(T):
                            ins_ = pe.transpose(bank(h, 3)[:, m * S + t * P:m * S + (t + 1) * P],
                                                XH[h][:, t, m * P:(m + 1) * P], ident[:])
                    ins_.then_inc(sem("xhatT_done", h), 1)

                def feature_major(outs, w, x, kc=KC):
                    for m, o in enumerate(outs):
                        for c in range(kc):
                            ins_ = pe.matmul(o, w[:, c, m * P:(m + 1) * P], x[:, c, :], start=(c == 0), stop=(c == kc - 1))
                    return ins_

                def attention(a, queries_waited=False):
                    q = ATT[a]
                    nh, nk, d, hc, gpc, ng = q["nh"], q["nk"], q["d"], q["hc"], q["gpc"], q["groups"]
                    units = 2 * ng

                    def scores(h, u):
                        g, t = divmod(u, 2)
                        if u == 0 and not queries_waited:
                            tally.wait(pe, "qT_ready", h)
                        if t == 0:
                            tally.wait(pe, "km_ready", h)
                        pe.matmul(bank(h, u % 2)[:, 0:nh * nk], QT[h][:, g // gpc, t * P:(t + 1) * P],
                                  KM[h][:, g % 2, 0:nh * nk], start=True, stop=True).then_inc(sem("s_done", h), 1)

                    def transpose_p(h, u):
                        g, t = divmod(u, 2)
                        tally.wait(pe, "exp_done", h)
                        if u >= 1:
                            tally.wait(pe, "pt_ready", h)
                        p = PR[h][:, u % 2, :]
                        if a == "a1":
                            blocks = [(c, j) for c in range(t, 2) for j in range(nh)]
                        else:
                            blocks = [(0, j) for j in range(nh)]
                        for n, (c, j) in enumerate(blocks):
                            kk = min(nk, P)
                            ins_ = pe.transpose(bank(h, 2)[0:kk, n * P:(n + 1) * P],
                                                p[:, j * nk + c * P:j * nk + c * P + kk], ident[:])
                        ins_.then_inc(sem("t_done", h), 1)

                    def values(h, g):
                        dve_seen = tally.n["pt_ready", h]
                        need = base[h] + 2 * g + 2
                        if need > dve_seen:
                            tally.wait(pe, "pt_ready", h, need - dve_seen)
                        c = g // gpc
                        if g % gpc == 0 and c >= 1:
                            tally.wait(pe, "oT_ready", h)
                        o = bank(h, 3)[:, (c % 2) * S:(c % 2) * S + S]
                        if a == "a1":
                            pt = PT[h][:, g % 2, :].rearrange("p (c j s) -> p c j s", c=2, j=nh)
                            for c2, n in ((1, S), (0, P)):
                                for j in range(nh):
                                    strip = 32 * ((g % 2) * nh + j)
                                    hd = (g * nh + j) * D1
                                    ins_ = pe.matmul(o[strip:strip + 32, 0:n], V1[h][:, c2, hd:hd + D1], pt[:, c2, j, 0:n],
                                                     start=(c2 == 1), stop=(c2 == 0), tile_position=(0, strip))
                        else:
                            pt = PT[h][0:KV, g % 2, :].rearrange("p (j s) -> p j s", j=nh)
                            order = (0, 2, 1, 3) if a == "L0" else range(nh)
                            for j in order:
                                head = g * nh + j
                                if a == "L0":
                                    strip = 32 * ((head // 2) % 4)
                                    ins_ = pe.matmul(o[strip:strip + 32, :], VM[h][0:KV, head // 2, head % 2, :], pt[:, j, :],
                                                     start=(head % 2 == 0), stop=(head % 2 == 1), tile_position=(0, strip))
                                else:
                                    strip = 32 * j
                                    ins_ = pe.matmul(o[strip:strip + 32, :], V2[h][0:KV, head * D1:(head + 1) * D1], pt[:, j, :],
                                                     start=True, stop=True, tile_position=(0, strip))
                        ins_.then_inc(sem("pv_done", h), 1)
                        if g % gpc == gpc - 1:
                            tally.wait(pe, "rbc_ready", h)
                            for t in range(T):
                                at = ((c + 1) % 2) * S + t * P
                                ins_ = pe.transpose(bank(h, 3)[:, at:at + P], RBC[h][:, t, :], ident[:])
                            ins_.then_inc(sem("rt_done", h), 1)

                    base = [tally.n["pt_ready", h] for h in range(2)]
                    for u in range(units + 3):
                        for h in range(2):
                            if u < units:
                                scores(h, u)
                            if 1 <= u <= units:
                                transpose_p(h, u - 1)
                            v = u - 2
                            if 0 <= v < units and v % 2 == 1:
                                values(h, v // 2)
                def output(h, w, chunks):
                    tally.wait(pe, "oT_ready", h)
                    for t in range(T):
                        for c in range(chunks):
                            ins_ = pe.matmul(bank(h, 0)[:, t * D:(t + 1) * D], OT[h][:, c, t * P:(t + 1) * P], w[:, c, :],
                                             start=(c == 0), stop=(c == chunks - 1))
                    ins_.then_inc(sem("out_done", h), 1)

                def mlp(a):
                    w = w1[a]

                    def up(h, banks):
                        if 0 in banks:
                            tally.wait(pe, "featT_ready", h)
                        for k in banks:
                            for m in (2 * k, 2 * k + 1):
                                for c in range(KC):
                                    ins_ = pe.matmul(bank(h, k)[:, (m % 2) * S:(m % 2) * S + S], w["li2"][:, c, m * P:(m + 1) * P],
                                                     FT[h][:, c, :], start=(c == 0), stop=(c == KC - 1))
                            ins_.then_inc(sem("h_done", h), 1)

                    def down(h):
                        tally.wait(pe, "gelu_done", h, 2)
                        for c in range(HC):
                            if c in (4, 6):
                                tally.wait(pe, "gelu_done", h)
                            for t in range(T):
                                ins_ = pe.matmul(bank(h, t)[:, 0:D], HT[h][:, c, t * P:(t + 1) * P], w["li3"][:, c, :],
                                                 start=(c == 0), stop=(c == HC - 1))
                        ins_.then_inc(sem("out_done", h), 1)

                    transpose_x(0)
                    up(0, (0, 1))
                    transpose_x(1)
                    up(0, (2, 3))
                    up(1, (0, 1))
                    down(0)
                    up(1, (2, 3))
                    down(1)

                def x5_transposes(h):
                    tally.wait(pe, "x5hat_ready", h)
                    for m in range(KC):
                        for t in range(T):
                            ins_ = pe.transpose(bank(h, 2)[:, m * S + t * P:m * S + (t + 1) * P],
                                                Y[h][:, t, m * P:(m + 1) * P], ident[:])
                    ins_.then_inc(sem("x5T_done", h), 1)

                def x5_logits(h):
                    for t in range(T):
                        for c in range(KC):
                            ins_ = pe.matmul(bank(h, 2)[:, t * E:(t + 1) * E], FT5[h][:, c, t * P:(t + 1) * P], wg_moe[:, c, :],
                                             start=(c == 0), stop=(c == KC - 1))
                    ins_.then_inc(sem("logits_done", h), 1)

                if final:
                    for h in range(2):
                        x5_transposes(h)
                    for h in range(2):
                        tally.wait(pe, "x5T_ready", h)
                        x5_logits(h)
                    return
                for h in range(2):
                    pe.transpose(bank(h, 1)[:, 0:KV], CT[h][0:KV, :], ident[0:KV, 0:KV]).then_inc(sem("cT_done", h), 1)
                for h in range(2):
                    tally.wait(pe, "cT_ready", h)
                    for m in range(2):
                        pe.matmul(bank(h, 0)[:, m * KV:(m + 1) * KV], wk0[:, m * P:(m + 1) * P], CTT[h], start=True, stop=True)
                    pe.matmul(bank(h, 1)[0:KV, 256:512], CTT[h], wv0[:], start=True, stop=True
                              ).then_inc(sem("ctx_proj_done", h), 1)
                for h in range(2):
                    transpose_x(h)
                for h in range(2):
                    tally.wait(pe, "featT_ready", h)
                    feature_major([bank(h, 3)[:, m * S:(m + 1) * S] for m in range(2)], wq0, FT[h]
                                  ).then_inc(sem("q_done", h), 1)
                for h in range(2):
                    x5_transposes(h)
                for h in range(2):
                    tally.wait(pe, "x5T_ready", h)
                    tally.wait(pe, "kT_ready", h)
                    tally.wait(pe, "v_ready", h)
                attention("L0")
                for h in range(2):
                    output(h, wo0, KC)
                for h in range(2):
                    x5_logits(h)
                def quantisedT(h):
                    tally.wait(pe, "xhat_ready", h)
                    n1t = bank(h, 3).bitcast(BF16)
                    for m in range(KC):
                        for t in range(T):
                            ins_ = pe.transpose(n1t[:, m * S + t * P:m * S + (t + 1) * P], N1[h][:, t, m * P:(m + 1) * P], identb[:])
                    ins_.then_inc(sem("xhatT_done", h), 1)

                def gate_up(t, h):
                    if t == 0:
                        tally.wait(pe, "featT_ready", h)
                    for j in range(2):
                        if t == 0 and j == 1:
                            tally.wait(pe, "lg_ready", h)
                        if t == 1:
                            tally.wait(pe, "hh_done", h)
                        for n, w in enumerate((wgT, wuT)):
                            for c in range(KC):
                                ins_ = pe.matmul(bank(h, 2 * j + n), N1T[h][:, c, t * P:(t + 1) * P],
                                                 w[:, c, j * 512:(j + 1) * 512], start=(c == 0), stop=(c == KC - 1))
                        ins_.then_inc(sem("gu_done", h), 1)

                def hiddenT(t, h):
                    tally.wait(pe, "n2_ready", h)
                    n2t = bank(h, t).bitcast(BF16)
                    for c in range(HC):
                        ins_ = pe.transpose(n2t[:, c * P:(c + 1) * P], N2[h][:, t, c * P:(c + 1) * P], identb[:])
                    ins_.then_inc(sem("n2T_done", h), 1)

                quantisedT(0)
                gate_up(0, 0)
                quantisedT(1)
                gate_up(0, 1)
                gate_up(1, 0)
                gate_up(1, 1)
                pe.wait_ge(w1_load, 16 * W1_LOADS)
                for h in range(2):
                    tally.wait(pe, "hh_done", h)
                    hiddenT(0, h)
                    tally.wait(pe, "cxhat_ready", h)
                    tally.wait(pe, "hh_done", h)
                    pe.transpose(bank(h, 2)[:, 0:KV], CH[h][0:KV, :], ident[0:KV, 0:KV]).then_inc(sem("cT_done", h), 1)
                    tally.wait(pe, "cT_ready", h)
                    for m in range(4):
                        pe.matmul(bank(h, 3)[:, m * KV:(m + 1) * KV], w1["a2"]["wk"][:, 0, m * P:(m + 1) * P], CYT[h],
                                  start=True, stop=True)
                    pe.matmul(bank(h, 2)[0:KV, :], CYT[h], w1["a2"]["wv"][:, 0, :], start=True, stop=True
                              ).then_inc(sem("ctx_proj_done", h), 1)
                    hiddenT(1, h)
                    tally.wait(pe, "kT_ready", h)
                    for t in range(T):
                        tally.wait(pe, "n2T_ready", h)
                        for c in range(HC):
                            ins_ = pe.matmul(bank(h, 2)[:, t * D:(t + 1) * D], N2T[h][:, c, t * P:(t + 1) * P], wdT[:, c, :],
                                             start=(c == 0), stop=(c == HC - 1))
                    ins_.then_inc(sem("out_done", h), 1)
                w = w1["a1"]
                halves = [[bank(h, b)[:, k * S:(k + 1) * S] for b in range(4) for k in range(2)] for h in range(2)]

                def queries(h):
                    tally.wait(pe, "featT_ready", h)
                    feature_major(halves[h][0:4], w["wq"], FT[h]).then_inc(sem("q_done", h), 1)

                def keys(h):
                    tally.wait(pe, "featT_ready", h)
                    feature_major(halves[h][4:8], w["wk"], FT2[h]).then_inc(sem("kv_done", h), 1)

                transpose_x(0)
                queries(0)
                transpose_x(1)
                keys(0)
                queries(1)
                keys(1)
                for h in range(2):
                    tally.wait(pe, "qT_ready", h)
                    for t in range(T):
                        for c in range(KC):
                            ins_ = pe.matmul(bank(h, t), FT2[h][:, c, t * P:(t + 1) * P], w["wv"][:, c, :],
                                             start=(c == 0), stop=(c == KC - 1))
                    ins_.then_inc(sem("kv_done", h), 1)
                for h in range(2):
                    tally.wait(pe, "v_ready", h)
                attention("a1", queries_waited=True)
                for h in range(2):
                    output(h, w["li1"], HD // P)
                mlp("a1")
                w = w1["a2"]

                def two(h, m0):
                    for m in (m0, m0 + 1):
                        for c in range(KC):
                            ins_ = pe.matmul(halves[h][m], w["wq"][:, c, m * P:(m + 1) * P], FT[h][:, c, :],
                                             start=(c == 0), stop=(c == KC - 1))
                    return ins_

                transpose_x(0)
                tally.wait(pe, "featT_ready", 0)
                two(0, 0)
                transpose_x(1)
                two(0, 2).then_inc(sem("q_done", 0), 1)
                tally.wait(pe, "featT_ready", 1)
                two(1, 0)
                two(1, 2).then_inc(sem("q_done", 1), 1)
                attention("a2")
                for h in range(2):
                    output(h, w["li1"], HD // P)
                mlp("a2")

        rt = arena[1]
        n_at = [0]

        def alloc(words):
            n_at[0] += words
            return rt[:, n_at[0] - words:n_at[0]]

        tot = [alloc(TILES * E).rearrange("p (t e) -> p t e", e=E) for _ in range(6)]
        seven = [alloc(E) for _ in range(6)]
        pos = alloc(TILES)
        block_of, lane_of = alloc(TILES), alloc(TILES)
        block_no, lane_no = alloc(BLOCKS), alloc(P)
        own_no = alloc(1)
        tile_no = alloc(TILES * BLOCKS).rearrange("p (t b) -> p t b", t=TILES)
        lanes = alloc(TILES * P // 2).bitcast(BF16).rearrange("p (t l) -> p t l", t=TILES)
        hit = alloc(TILES * BLOCKS).rearrange("p (t b) -> p t b", t=TILES)
        blocks = alloc(TILES * BLOCKS).bitcast(BF16).rearrange("p (t k b) -> p t k b", t=TILES, k=2)
        slot_id = alloc(BLOCKS)
        unit_no = alloc(UNITS * E).rearrange("p (u e) -> p u e", e=E)
        below = alloc(UNITS * E).rearrange("p (u e) -> p u e", e=E)
        unit_e = alloc(UNITS)

        out_rows = out.rearrange("b s n -> (b s) n")
        CHAIN = 2

        def load_weights(sp, j, k):
            e = sp.value_load(unit_ei[0:1, bass.ds(j, 1)] if not isinstance(j, int) else unit_ei[0:1, j:j + 1],
                              min_val=0, max_val=E - 1)
            sp.dma_start(W1B[k][:], ins["L1_ffn_W1"][bass.ds(e, 1)].rearrange("o (c p) n -> p (o c) n", p=P)
                         ).then_inc(es["w1_loaded", k], 16)
            sp.dma_start(W2B[k][:], ins["L1_ffn_W2"][bass.ds(e, 1)].rearrange("o (c p) n -> p (o c) n", p=P)
                         ).then_inc(es["w2_loaded", k], 16)

        def gather(pool, k):
            for t in range(T):
                pool.indirect_dma_start(RB[k][:, t, :], None, x5_all,
                                        bass.IndirectOffsetOnAxis(ap=GIDB[k][:, t:t + 1], axis=0),
                                        bounds_check=2 * S + TOKENS - 1, oob_is_err=False
                                        ).then_inc(es["rows_loaded", k], 16)

        ids_ready = ctx.enter_context(nc.semaphore("ids_ready"))
        counts_done = ctx.enter_context(nc.semaphore("counts_done"))
        route_chain = ctx.enter_context(nc.semaphore("route_chain"))
        slots_ready = ctx.enter_context(nc.semaphore("slots_ready"))
        onehots_ready = ctx.enter_context(nc.semaphore("onehots_ready"))
        ids_done = ctx.enter_context(nc.semaphore("ids_done"))

        with nc.Fori(0, B // 2) as it:
            with nc.Block() as block:
                layers(block, it)
            nc.all_engine_barrier(sems_to_clear=sem_range)

        with nc.Block() as block:
            layers(block, None, final=True)
        nc.all_engine_barrier(sems_to_clear=sem_range)
        layer_sems.close()

        weights_mem.close()
        W1B = [sb(f"w1_unit{k}", [P, KC, INNER]) for k in range(2)]
        W2B = [sb(f"w2_unit{k}", [P, HC, D]) for k in range(2)]
        RB = [sb(f"rows_unit{k}", [P, T, D]) for k in range(2)]
        XR = [sb(f"rows_kept_unit{k}", [P, T, D]) for k in range(2)]
        XHB = [sb(f"xhat_unit{k}", [P, T, D]) for k in range(2)]
        ZB = [sb(f"z_unit{k}", [P, T, D]) for k in range(2)]
        HTB = [sb(f"hidden_unit{k}", [P, HC, UNIT]) for k in range(2)]
        GIDB = [sb(f"gather_ids{k}", [P, T], I32) for k in range(2)]
        IDB = [sb(f"scatter_ids{k}", [P, T], I32) for k in range(2)]

        enames = ["w1_loaded", "w2_loaded", "rows_loaded", "rows_kept", "hi_ready", "lo1_ready", "lo2_ready", "e_var_ready",
                  "e_rstd_ready", "e_xhat_ready", "e_xhatT_done", "e_featT_ready", "e_h_done", "e_gelu_done", "h_split",
                  "e_y_done", "z_ready", "z_free", "e_chain", "e_pool_chain", "scattered"]
        es = {(n, k): ctx.enter_context(nc.semaphore(f"{n}{k}")) for n in enames for k in range(2)}
        empty_ready = ctx.enter_context(nc.semaphore("empty_ready"))
        experts_known = ctx.enter_context(nc.semaphore("experts_known"))

        with nc.Block() as block:
            @block.sync
            def _(sp):
                sp.wait_ge(experts_known, 1)
                load_weights(sp, 0, 0)

            @block.tensor
            def _(pe):
                oh = onehot[:].rearrange("p t e -> p (t e)")
                pe.matmul(ps[:, 0, 0:TILES * E], strict[:], oh, start=True, stop=True)
                pe.matmul(ps[:, 1, 0:TILES * E], onesb[:], oh, start=True, stop=True).then_inc(counts_done, 1)
                pe.wait_ge(onehots_ready, 1)
                for t in range(TILES):
                    ins_ = pe.matmul(ps[:, 2, 0:2 * BLOCKS], lanes[:, t, :], blocks[:, t].rearrange("p k b -> p (k b)"),
                                     start=(t == 0), stop=(t == TILES - 1))
                ins_.then_inc(ids_done, 1)

            @block.vector
            def _(dve):
                n = [0]

                def step(ins_):
                    ins_.then_inc(route_chain, 1)
                    n[0] += 1
                    dve.wait_ge(route_chain, n[0])

                dve.wait_ge(counts_done, 1)
                flat = "p (t e) -> p t e"
                step(dve.tensor_copy(tot[0], ps[:, 1, 0:TILES * E].rearrange(flat, e=E)))
                cur = 0
                for k, sh in enumerate((1, 2, 4, 8)):
                    dve.tensor_copy(tot[k + 1][:, 0:sh, :], tot[cur][:, 0:sh, :])
                    step(dve.tensor_tensor(tot[k + 1][:, sh:, :], tot[cur][:, sh:, :], tot[cur][:, :TILES - sh, :], ALU.add))
                    cur = k + 1
                incl = tot[cur]
                step(dve.tensor_scalar(seven[0], incl[:, TILES - 1, :], 1.0 / UNIT, (UNIT - 1.0) / UNIT - 0.5 + 0.25 / UNIT,
                                       ALU.mult, ALU.add))
                step(dve.tensor_scalar(seven[0], seven[0], MAGIC, None, ALU.add))
                step(dve.tensor_scalar(seven[1], seven[0], -MAGIC, None, ALU.add))
                cur = 1
                for k, sh in enumerate((1, 2, 4)):
                    dve.tensor_copy(seven[k + 2][:, 0:sh], seven[cur][:, 0:sh])
                    step(dve.tensor_tensor(seven[k + 2][:, sh:], seven[cur][:, sh:], seven[cur][:, :E - sh], ALU.add))
                    cur = k + 2
                uend = seven[cur]
                dve.wait_ge(ids_ready, 5)
                step(dve.tensor_tensor(below, uend.rearrange("p (o e) -> p o e", o=1).to_broadcast([P, UNITS, E]), unit_no,
                                       ALU.is_le))
                step(dve.tensor_reduce(unit_e, below, AX.X, ALU.add))
                dve.tensor_scalar(unit_ei[:], unit_e, float(E - 1), None, ALU.min).then_inc(experts_known, 1)
                step(dve.tensor_tensor(seven[0], uend, seven[1], ALU.subtract))
                step(dve.tensor_scalar(seven[1], seven[0], float(UNIT), None, ALU.mult))
                step(dve.tensor_tensor(tot[5], incl, tot[0], ALU.subtract))
                step(dve.tensor_tensor(tot[5], tot[5], ps[:, 0, 0:TILES * E].rearrange(flat, e=E), ALU.add))
                step(dve.tensor_tensor(tot[5], tot[5], seven[1].rearrange("p (o e) -> p o e", o=1).to_broadcast([P, TILES, E]),
                                       ALU.add))
                step(dve.tensor_tensor(tot[5], tot[5], onehot[:], ALU.mult))
                step(dve.tensor_reduce(pos, tot[5], AX.X, ALU.add))
                step(dve.tensor_scalar(block_of, pos, 1.0 / P, 0.5 / P - 0.5, ALU.mult, ALU.add))
                step(dve.tensor_scalar(block_of, block_of, MAGIC, None, ALU.add))
                step(dve.tensor_scalar(block_of, block_of, -MAGIC, None, ALU.add))
                step(dve.scalar_tensor_tensor(lane_of, block_of, -float(P), pos, ALU.mult, ALU.add))

                def spread(v, n):
                    return v.rearrange("p (t o) -> p t o", o=1).to_broadcast([P, TILES, n])

                def each(v, n):
                    return v.rearrange("p (o n) -> p o n", o=1).to_broadcast([P, TILES, n])

                step(dve.tensor_tensor(hit, each(block_no, BLOCKS), spread(block_of, BLOCKS), ALU.is_equal))
                dve.tensor_scalar(blocks[:, :, 0, :], hit, own_no, None, ALU.mult)
                dve.tensor_tensor(blocks[:, :, 1, :], hit, tile_no, ALU.mult)
                dve.tensor_tensor(lanes, each(lane_no, P), spread(lane_of, P), ALU.is_equal).then_inc(onehots_ready, 1)
                dve.wait_ge(ids_done, 1)
                step(dve.tensor_scalar(slot_id, ps[:, 2, BLOCKS:2 * BLOCKS], float(P), float(PAD_ID), ALU.mult, ALU.add))
                step(dve.tensor_tensor(slot_id, slot_id, ps[:, 2, 0:BLOCKS], ALU.add))
                dve.tensor_copy(slot_ids[:], slot_id)
                step(dve.tensor_scalar(slot_id, slot_id, float(2 * S), None, ALU.add))
                for k in range(2):
                    dve.tensor_copy(GIDB[k][:], slot_id[:, k * T:(k + 1) * T]).then_inc(slots_ready, 1)
                dve.tensor_copy(slot_rows[:, 0:BLOCKS], slot_id)

            @block.gpsimd
            def _(pool):
                pool.iota(unit_no, pattern=[[1, UNITS], [0, E]], base=0, channel_multiplier=0,
                          allow_small_or_imprecise_dtypes=True).then_inc(ids_ready, 1)
                pool.iota(block_no, pattern=[[1, BLOCKS]], base=0, channel_multiplier=0,
                          allow_small_or_imprecise_dtypes=True).then_inc(ids_ready, 1)
                pool.iota(lane_no, pattern=[[1, P]], base=0, channel_multiplier=0,
                          allow_small_or_imprecise_dtypes=True).then_inc(ids_ready, 1)
                pool.iota(own_no, pattern=[[0, 1]], base=0, channel_multiplier=1,
                          allow_small_or_imprecise_dtypes=True).then_inc(ids_ready, 1)
                pool.iota(tile_no, pattern=[[1, TILES], [0, BLOCKS]], base=-TILES, channel_multiplier=0,
                          allow_small_or_imprecise_dtypes=True).then_inc(ids_ready, 1)
                for k in range(2):
                    pool.memset(ZB[k][:], 0.0).then_inc(empty_ready, 1)
                    pool.memset(RB[k][:], 0.0).then_inc(empty_ready, 1)
                    pool.iota(IDB[k][:], pattern=[[0, T]], base=PAD_ID, channel_multiplier=0).then_inc(empty_ready, 1)
                pool.iota(slot_rows[:, BLOCKS:], pattern=[[0, 2 * T]], base=PAD_ID, channel_multiplier=0).then_inc(empty_ready, 1)
                pool.wait_ge(empty_ready, 7)
                for k in range(2):
                    for t in range(T):
                        pool.indirect_dma_start(out_rows, bass.IndirectOffsetOnAxis(ap=IDB[k][:, t:t + 1], axis=0),
                                                ZB[k][:, t, :], None, bounds_check=TOKENS - 1, oob_is_err=False
                                                ).then_inc(es["scattered", k], 16)
                pool.wait_ge(slots_ready, 2)
                for k in range(2):
                    gather(pool, k)
        nc.all_engine_barrier(sem_only=True)

        arenas_mem.close()

        def parts(name, shape):
            return [[sb(f"{name}_{part}{k}", shape, F32R, side="right") for k in range(2)] for part in ("high", "low")]

        W1H, W1L = parts("w1", [P, KC, INNER])
        W2H, W2L = parts("w2", [P, HC, D])
        FTH, FTL = parts("feat", [P, KC, UNIT])
        HTH, HTL = parts("hidden", [P, HC, UNIT])

        with nc.Block() as block:
            def wait(eng, name, k, value):
                eng.wait_ge(es[name, k], value)

            def windows(window, eng):
                half = UNITS // 2
                window((0, 0), (0, 1), None)
                with eng.Fori(0, half - 1) as it:
                    window((it, 1), (it + 1, 0), (it, 0))
                    window((it + 1, 0), (it + 1, 1), (it, 1))
                window((half - 1, 1), (half, 0), (half - 1, 0))
                window((half, 0), None, (half - 1, 1))

            @block.sync
            def _(sp):
                def next_weights(n, k):
                    wait(sp, "lo1_ready", k, n)
                    wait(sp, "lo2_ready", k, n)
                    load_weights(sp, n * 2 + k, k)

                load_weights(sp, 1, 1)
                with sp.Fori(0, UNITS // 2 - 1) as it:
                    for k in range(2):
                        next_weights(it + 1, k)
                next_weights(UNITS // 2, 0)

            @block.gpsimd
            def _(pool):
                def rstd(n, k):
                    wait(pool, "e_var_ready", k, n + 1)
                    pool.tensor_tensor(sm(k, VE, 2), sm(k, MV, 4).rearrange("p (t q) -> p t q", q=2)[:, :, 1],
                                       epst[:], ALU.add).then_inc(es["e_pool_chain", k], 1)
                    wait(pool, "e_pool_chain", k, n + 1)
                    pool.tensor_tensor(sm(k, RSTD, 2), sm(k, VE, 2), neghalf[:], ALU.pow).then_inc(es["e_rstd_ready", k], 1)

                def low_part1(n, k):
                    for c in range(KC):
                        wait(pool, "hi_ready", k, n * 4 + c + 1)
                        ins_ = pool.tensor_tensor(W1L[k][:, c, :], W1B[k][:, c, :], W1H[k][:, c, :].bitcast(F32), ALU.subtract)
                    ins_.then_inc(es["lo1_ready", k], 1)

                def relay(n, k):
                    wait(pool, "scattered", k, (n + 1) * 16 * T)
                    pool.sem_inc(es["z_free", k], 1)

                def scatter(n, k):
                    wait(pool, "z_ready", k, n + 1)
                    pool.tensor_tensor(sm(k, IDX, 2), epst[:], epst[:], ALU.add)
                    for t in range(T):
                        pool.indirect_dma_start(out_rows, bass.IndirectOffsetOnAxis(ap=IDB[k][:, t:t + 1], axis=0),
                                                ZB[k][:, t, :], None, bounds_check=TOKENS - 1, oob_is_err=False
                                                ).then_inc(es["scattered", k], 16)

                def next_rows(n, k):
                    wait(pool, "e_xhat_ready", k, n)
                    wait(pool, "rows_kept", k, n)
                    pool.tensor_tensor(sm(k, AM, 2), epst[:], epst[:], ALU.add)
                    gather(pool, k)

                def window(unit, after, before):
                    if not isinstance(unit[0], int) or 2 * (unit[0] + 1) + unit[1] < UNITS:
                        next_rows(unit[0] + 1, unit[1])
                    if after:
                        rstd(*after)
                    if before:
                        scatter(*before)
                    if after:
                        low_part1(*after)
                    relay(*unit)

                rstd(0, 0)
                low_part1(0, 0)
                windows(window, pool)
                scatter(UNITS // 2, 0)
                for k in range(2):
                    pool.wait_ge(es["scattered", k], 16 * T * (UNITS // 2 + 2 - k))

            @block.vector
            def _(dve):
                def link(ins_, n, k, c):
                    ins_.then_inc(es["e_chain", k], 1)
                    wait(dve, "e_chain", k, n * CHAIN + c)

                def normalise(n, k):
                    wait(dve, "rows_loaded", k, (n + 1) * 16 * T)
                    for t in range(T):
                        ins_ = dve.bn_stats(sm(k, ST + 6 * t, 6), RB[k][:, t, 0:D])
                    link(ins_, n, k, 1)
                    dve.tensor_copy(sm(k, EQ, 1), sm(k, ST, 1))
                    for t in range(T):
                        ins_ = dve.bn_aggr(sm(k, MV + 2 * t, 2), sm(k, ST + 6 * t, 6))
                    ins_.then_inc(es["e_var_ready", k], 1)
                    dve.tensor_copy(GIDB[k][:], slot_rows[:, bass.ds((n * 2 + 2 + k) * T, T)])
                    wait(dve, "e_rstd_ready", k, n + 1)
                    for t in range(T):
                        ins_ = dve.tensor_scalar(XHB[k][:, t, :], RB[k][:, t, 0:D], sm(k, MV + 2 * t, 1), sm(k, RSTD + t, 1),
                                                 ALU.subtract, ALU.mult)
                    ins_.then_inc(es["e_xhat_ready", k], 1)

                def feature_major(n, k):
                    wait(dve, "e_xhatT_done", k, n + 1)
                    flat = "p c s -> p (c s)"
                    link(dve.tensor_copy(FTH[k][:].rearrange(flat), bank(k, 3)), n, k, 2)
                    dve.tensor_tensor(FTL[k][:].rearrange(flat), bank(k, 3), FTH[k][:].bitcast(F32).rearrange(flat), ALU.subtract
                                      ).then_inc(es["e_featT_ready", k], 1)

                def hidden_parts(n, k, b):
                    wait(dve, "e_gelu_done", k, n * 4 + b + 1)
                    h = slice(2 * b, 2 * b + 2)
                    dve.tensor_tensor(HTL[k][:, h, :], HTB[k][:, h, :], HTH[k][:, h, :].bitcast(F32), ALU.subtract
                                      ).then_inc(es["h_split", k], 1)

                def low_part2(n, k):
                    for i, c in enumerate((slice(0, HC // 2), slice(HC // 2, HC))):
                        wait(dve, "hi_ready", k, n * 4 + 3 + i)
                        ins_ = dve.tensor_tensor(W2L[k][:, c, :], W2B[k][:, c, :], W2H[k][:, c, :].bitcast(F32), ALU.subtract)
                    ins_.then_inc(es["lo2_ready", k], 1)

                def result(n, k):
                    wait(dve, "z_free", k, n + 1)
                    wait(dve, "rows_kept", k, n + 1)
                    dve.tensor_copy(IDB[k][:], slot_ids[:, bass.ds((n * 2 + k) * T, T)])
                    wait(dve, "e_y_done", k, n + 1)
                    dve.tensor_tensor(ZB[k][:], bank(k, 0, 2)[:, :, 0:D], XR[k][:, :, 0:D], ALU.add).then_inc(es["z_ready", k], 1)

                def window(unit, after, before):
                    if before:
                        result(*before)
                    if after:
                        normalise(*after)
                    hidden_parts(*unit, 0)
                    hidden_parts(*unit, 1)
                    hidden_parts(*unit, 2)
                    hidden_parts(*unit, 3)
                    if after:
                        feature_major(*after)
                        low_part2(*after)

                normalise(0, 0)
                feature_major(0, 0)
                low_part2(0, 0)
                windows(window, dve)
                result(UNITS // 2, 0)

            @block.scalar
            def _(act):
                def gelu(n, k, b):
                    wait(act, "e_h_done", k, n * 4 + b + 1)
                    for o in (HTB[k], HTH[k]):
                        ins_ = act.activation(o[:, 2 * b:2 * b + 2, :].rearrange("p c s -> p (c s)"), bank(k, b),
                                              ACT.Gelu_apprx_tanh)
                    ins_.then_inc(es["e_gelu_done", k], 1)

                def high1(n, k, c, first=False):
                    wait(act, "w1_loaded", k, n * 16 + 16)
                    if not first:
                        wait(act, "e_h_done", k, n * 4)
                    act.activation(W1H[k][:, c, :], W1B[k][:, c, :], ACT.Copy).then_inc(es["hi_ready", k], 1)

                def high2(n, k, first=False):
                    wait(act, "w2_loaded", k, n * 16 + 16)
                    if not first:
                        wait(act, "e_y_done", k, n)
                    for c in (slice(0, HC // 2), slice(HC // 2, HC)):
                        act.activation(W2H[k][:, c, :], W2B[k][:, c, :], ACT.Copy).then_inc(es["hi_ready", k], 1)

                def keep_rows(n, k, first=False):
                    wait(act, "rows_loaded", k, (n + 1) * 16 * T)
                    if not first:
                        wait(act, "z_ready", k, n)
                    act.activation(XR[k][:], RB[k][:], ACT.Copy).then_inc(es["rows_kept", k], 1)

                def window(unit, after, before):
                    first = before is None
                    if after:
                        keep_rows(*after, first)
                    gelu(*unit, 0)
                    if after:
                        high1(*after, 0, first)
                    gelu(*unit, 1)
                    if after:
                        high1(*after, 1, first)
                    gelu(*unit, 2)
                    gelu(*unit, 3)
                    if after:
                        high2(*after, first)

                keep_rows(0, 0, True)
                high1(0, 0, 0, True)
                high1(0, 0, 1, True)
                high2(0, 0, True)
                windows(window, act)

            @block.tensor
            def _(pe):
                def product(o, a, b, start, stop):
                    (ah, al), (bh, bl) = a, b
                    pe.matmul(o, ah, bh, start=start, stop=False)
                    pe.matmul(o, ah, bl, start=False, stop=False)
                    return pe.matmul(o, al, bh, start=False, stop=stop)

                def transposes(n, k):
                    wait(pe, "e_xhat_ready", k, n + 1)
                    for m in range(KC):
                        for t in range(T):
                            ins_ = pe.transpose(bank(k, 3)[:, m * UNIT + t * P:m * UNIT + (t + 1) * P],
                                                XHB[k][:, t, m * P:(m + 1) * P], ident[:])
                    ins_.then_inc(es["e_xhatT_done", k], 1)

                def up(n, k):
                    wait(pe, "lo1_ready", k, n + 1)
                    wait(pe, "e_featT_ready", k, n + 1)
                    for b in range(4):
                        for m in (2 * b, 2 * b + 1):
                            for c in range(KC):
                                ins_ = product(bank(k, b)[:, (m % 2) * UNIT:(m % 2 + 1) * UNIT],
                                               [w[k][:, c, m * P:(m + 1) * P] for w in (W1H, W1L)],
                                               [x[k][:, c, :] for x in (FTH, FTL)], c == 0, c == KC - 1)
                        ins_.then_inc(es["e_h_done", k], 1)

                def down(n, k):
                    wait(pe, "lo2_ready", k, n + 1)
                    for c in range(HC):
                        if c in (0, 4, 6):
                            wait(pe, "h_split", k, n * 4 + (2 if c == 0 else c // 2 + 1))
                        for t in range(T):
                            ins_ = product(bank(k, t)[:, 0:D], [x[:, c, t * P:(t + 1) * P] for x in (HTH[k], HTL[k])],
                                           [w[k][:, c, :] for w in (W2H, W2L)], c == 0, c == HC - 1)
                    ins_.then_inc(es["e_y_done", k], 1)

                def window(unit, after, before):
                    up(*unit)
                    if after:
                        transposes(*after)
                    down(*unit)

                transposes(0, 0)
                windows(window, pe)


def kernel(**inputs):
    import numpy as _np
    import concourse.bacc as _bacc
    from concourse import mybir as _mybir
    from concourse.bass_utils import run_bass_kernel_spmd as _run

    nc = _bacc.Bacc("TRN2", target_bir_lowering=False, num_devices=1)
    arrays, ins = {}, {}
    for name, a in inputs.items():
        a = _np.ascontiguousarray(a)
        arrays[f"in_{name}"] = a
        ins[name] = nc.dram_tensor(f"in_{name}", a.shape, _mybir.dt.from_np(a.dtype), kind="ExternalInput").ap()
    out = nc.dram_tensor("out_0", (B, S, D), F32, kind="ExternalOutput").ap()
    build(nc, ins, out)
    r = _run(nc, [arrays], core_ids=[0])
    return r.results[0]["out_0"]
```
